# Optimizing a Trainium2 kernel written in Bass

```python
import numpy as np
import jax
import jax.numpy as jnp

def _softmax(x, axis=-1):
    return jax.nn.softmax(x, axis=axis)

def _gelu(x):
    return jax.nn.gelu(x, approximate=True)

def _silu(x):
    return jax.nn.silu(x)

def _sigmoid(x):
    return jax.nn.sigmoid(x)

def _layernorm(x, axis=-1, eps=1e-05):
    m = jnp.mean(x, axis=axis, keepdims=True)
    v = jnp.var(x, axis=axis, keepdims=True)
    return (x - m) / jnp.sqrt(v + eps)

def _scatter_add(tgt, idx, src, axis=0):
    return tgt.at[idx].add(src)

def _segment_sum(src, seg, n):
    return jax.ops.segment_sum(src, seg, n)
kernel_name = 'mk_xattn_seq_d2_seqx_r4_218674'

def setup_inputs(seed: int=0):
    np.random.seed(seed)
    _w = jnp.asarray

    def _rec_inputs():
        import jax
        import jax.numpy as jnp
        _rk = jax.random.key(seed)
        x = -0.0002928 + 1 * jax.random.normal(jax.random.fold_in(_rk, 1), (8, 256, 512), jnp.float32)
        _lenS = 256 - jax.random.randint(jax.random.fold_in(_rk, 7), (8,), 0, max(1, 256 // 4) + 1, jnp.int32)
        _lenS2 = 256 - jax.random.randint(jax.random.fold_in(_rk, 8), (8,), 0, max(1, 256 // 4) + 1, jnp.int32)
        _ctx_2048P = jax.random.normal(jax.random.fold_in(_rk, 11), (8, 16, 512), jnp.float32)
        _ctx_2048c = jax.random.dirichlet(jax.random.fold_in(_rk, 511), 0.3 * jnp.ones((16,), jnp.float32), (8, 256))
        _ctx_2048t = jnp.einsum('bsk,bkd->bsd', _ctx_2048c, _ctx_2048P)
        _ctx_2048t = _ctx_2048t * jax.lax.rsqrt(jnp.mean(jnp.square(_ctx_2048t)) + 1e-12) * 0.953939
        ctx_2048 = -1.39393e-06 + 0.999914 * (_ctx_2048t + 0.3 * jax.random.normal(jax.random.fold_in(_rk, 611), (8, 256, 512), jnp.float32))
        _validS = jnp.arange(256)[None, :] < _lenS[:, None]
        _validS2 = jnp.arange(256)[None, :] < _lenS2[:, None]
        _causal = jnp.tril(jnp.ones((256, 256), dtype=bool))
        mask_1x1xSxS2_fc1 = jnp.where(jnp.broadcast_to(_validS2[0:1, None, None, :], (1, 1, 256, 256)), 1.0, 0.0).astype(jnp.float32)
        mask_Bx1xSxS2_ff1 = jnp.where(jnp.ones((8, 1, 256, 256), dtype=bool), 1.0, 0.0).astype(jnp.float32)
        return (x, ctx_2048, mask_1x1xSxS2_fc1, mask_Bx1xSxS2_ff1)
    x, ctx_2048, mask_1x1xSxS2_fc1, mask_Bx1xSxS2_ff1 = _rec_inputs()

    def _L0_xattn_setup():
        import math
        import jax, jax.numpy as jnp
        import numpy as np
        C = 256
        H = 16
        DH = C // H
        EPS = 1e-05

        def pos_enc(c, T, dtype):
            pos = jnp.arange(T, dtype=jnp.float32)[:, None]
            div = jnp.exp(jnp.arange(0, c, 2, dtype=jnp.float32) * (-math.log(10000.0) / c))
            ang = pos * div
            pe = jnp.zeros((T, c), dtype=jnp.float32)
            pe = pe.at[:, 0::2].set(jnp.sin(ang)).at[:, 1::2].set(jnp.cos(ang))
            return pe.T.astype(dtype)

        def layer_norm(x, g, b):
            mu = jnp.mean(x, axis=-1, keepdims=True)
            var = jnp.mean(jnp.square(x - mu), axis=-1, keepdims=True)
            return (x - mu) * jax.lax.rsqrt(var + EPS) * g + b
        key = jax.random.key(seed)
        ks = jax.random.split(key, 16)
        s = 1.0 / math.sqrt(C)
        inp = {'zt_prev': jax.random.normal(ks[0], (2, C, 512), jnp.float32), 'za': jax.random.normal(ks[1], (2, C, 512), jnp.float32), 'Wq': jax.random.normal(ks[2], (C, C), jnp.float32) * s, 'Wk': jax.random.normal(ks[3], (C, C), jnp.float32) * s, 'Wv': jax.random.normal(ks[4], (C, C), jnp.float32) * s, 'Wo': jax.random.normal(ks[5], (C, C), jnp.float32) * s, 'ln_q_g': jnp.ones((C,), jnp.float32), 'ln_q_b': jnp.zeros((C,), jnp.float32), 'ln_kv_g': jnp.ones((C,), jnp.float32), 'ln_kv_b': jnp.zeros((C,), jnp.float32), 'ffn_ln_g': jnp.ones((C,), jnp.float32), 'ffn_ln_b': jnp.zeros((C,), jnp.float32), 'W1': jax.random.normal(ks[6], (C, 2 * C), jnp.float32) * s, 'b1': jnp.zeros((2 * C,), jnp.float32), 'W2': jax.random.normal(ks[7], (2 * C, C), jnp.float32) * (1.0 / math.sqrt(2 * C)), 'b2': jnp.zeros((C,), jnp.float32)}
        return inp
    _L0_xattn_all = _L0_xattn_setup()
    _L0_xattn_in = {k: v for k, v in _L0_xattn_all.items() if k in ('Wq', 'Wk', 'Wv', 'Wo', 'ln_q_g', 'ln_q_b', 'ln_kv_g', 'ln_kv_b', 'ffn_ln_g', 'ffn_ln_b', 'W1', 'b1', 'W2', 'b2')}
    del _L0_xattn_all

    def _L1_xattn_setup():
        import jax, jax.numpy as jnp
        import numpy as np
        H = 512
        NH = 16
        HD = H // NH
        EPS = 1e-05

        def gelu(x):
            return 0.5 * x * (1.0 + jnp.tanh(0.7978845608028654 * x * (1.0 + 0.044715 * x * x)))

        def layernorm(x, scale, bias):
            m = jnp.mean(x, axis=-1, keepdims=True)
            v = jnp.mean(jnp.square(x - m), axis=-1, keepdims=True)
            return (x - m) * jax.lax.rsqrt(v + EPS) * scale + bias

        def split_heads(x):
            b, s, _ = x.shape
            return x.reshape(b, s, NH, HD).transpose(0, 2, 1, 3)

        def merge_heads(x):
            b, nh, s, hd = x.shape
            return x.transpose(0, 2, 1, 3).reshape(b, s, nh * hd)

        def attention(q, k, v, mask):
            scores = jnp.einsum('bhqd,bhkd->bhqk', q, k) / jnp.sqrt(jnp.float32(HD))
            scores = scores * mask - 10000.0 * (1.0 - mask)
            probs = jax.nn.softmax(scores, axis=-1)
            return jnp.einsum('bhqk,bhkd->bhqd', probs, v)
        key = jax.random.key(seed)
        ks = jax.random.split(key, 16)
        b, s, t = (2, 256, 256)
        w = lambda k, i, o: jax.random.normal(k, (i, o), jnp.float32) * 0.02
        inp = {'hidden_states': jax.random.normal(ks[0], (b, s, H), jnp.float32), 'encoder_states': jax.random.normal(ks[1], (b, t, H), jnp.float32), 'ltor_mask': jnp.tril(jnp.ones((1, 1, s, s), jnp.float32)), 'cross_mask': jnp.ones((b, 1, s, t), jnp.float32), 'ln1_s': jnp.ones((H,), jnp.float32), 'ln1_b': jnp.zeros((H,), jnp.float32), 'w_qkv': w(ks[2], H, 3 * H), 'b_qkv': jnp.zeros((3 * H,), jnp.float32), 'w_ao': w(ks[3], H, H), 'b_ao': jnp.zeros((H,), jnp.float32), 'ln2_s': jnp.ones((H,), jnp.float32), 'ln2_b': jnp.zeros((H,), jnp.float32), 'w_q': w(ks[4], H, H), 'b_q': jnp.zeros((H,), jnp.float32), 'w_kv': w(ks[5], H, 2 * H), 'b_kv': jnp.zeros((2 * H,), jnp.float32), 'w_co': w(ks[6], H, H), 'b_co': jnp.zeros((H,), jnp.float32), 'ln3_s': jnp.ones((H,), jnp.float32), 'ln3_b': jnp.zeros((H,), jnp.float32), 'w1': w(ks[7], H, 4 * H), 'b1': jnp.zeros((4 * H,), jnp.float32), 'w2': w(ks[8], 4 * H, H), 'b2': jnp.zeros((H,), jnp.float32)}
        return inp
    _L1_xattn_all = _L1_xattn_setup()
    _L1_xattn_in = {k: v for k, v in _L1_xattn_all.items() if k in ('ln1_s', 'ln1_b', 'w_qkv', 'b_qkv', 'w_ao', 'b_ao', 'ln2_s', 'ln2_b', 'w_q', 'b_q', 'w_kv', 'b_kv', 'w_co', 'b_co', 'ln3_s', 'ln3_b', 'w1', 'b1', 'w2', 'b2')}
    del _L1_xattn_all
    return {'x': x, 'ctx_2048': ctx_2048, 'mask_1x1xSxS2_fc1': mask_1x1xSxS2_fc1, 'mask_Bx1xSxS2_ff1': mask_Bx1xSxS2_ff1, 'L0_xattn_Wq': _L0_xattn_in['Wq'], 'L0_xattn_Wk': _L0_xattn_in['Wk'], 'L0_xattn_Wv': _L0_xattn_in['Wv'], 'L0_xattn_Wo': _L0_xattn_in['Wo'], 'L0_xattn_ln_q_g': _L0_xattn_in['ln_q_g'], 'L0_xattn_ln_q_b': _L0_xattn_in['ln_q_b'], 'L0_xattn_ln_kv_g': _L0_xattn_in['ln_kv_g'], 'L0_xattn_ln_kv_b': _L0_xattn_in['ln_kv_b'], 'L0_xattn_ffn_ln_g': _L0_xattn_in['ffn_ln_g'], 'L0_xattn_ffn_ln_b': _L0_xattn_in['ffn_ln_b'], 'L0_xattn_W1': _L0_xattn_in['W1'], 'L0_xattn_b1': _L0_xattn_in['b1'], 'L0_xattn_W2': _L0_xattn_in['W2'], 'L0_xattn_b2': _L0_xattn_in['b2'], 'L1_xattn_ln1_s': _L1_xattn_in['ln1_s'], 'L1_xattn_ln1_b': _L1_xattn_in['ln1_b'], 'L1_xattn_w_qkv': _L1_xattn_in['w_qkv'], 'L1_xattn_b_qkv': _L1_xattn_in['b_qkv'], 'L1_xattn_w_ao': _L1_xattn_in['w_ao'], 'L1_xattn_b_ao': _L1_xattn_in['b_ao'], 'L1_xattn_ln2_s': _L1_xattn_in['ln2_s'], 'L1_xattn_ln2_b': _L1_xattn_in['ln2_b'], 'L1_xattn_w_q': _L1_xattn_in['w_q'], 'L1_xattn_b_q': _L1_xattn_in['b_q'], 'L1_xattn_w_kv': _L1_xattn_in['w_kv'], 'L1_xattn_b_kv': _L1_xattn_in['b_kv'], 'L1_xattn_w_co': _L1_xattn_in['w_co'], 'L1_xattn_b_co': _L1_xattn_in['b_co'], 'L1_xattn_ln3_s': _L1_xattn_in['ln3_s'], 'L1_xattn_ln3_b': _L1_xattn_in['ln3_b'], 'L1_xattn_w1': _L1_xattn_in['w1'], 'L1_xattn_b1': _L1_xattn_in['b1'], 'L1_xattn_w2': _L1_xattn_in['w2'], 'L1_xattn_b2': _L1_xattn_in['b2']}

def reference(x, ctx_2048, mask_1x1xSxS2_fc1, mask_Bx1xSxS2_ff1, L0_xattn_Wq, L0_xattn_Wk, L0_xattn_Wv, L0_xattn_Wo, L0_xattn_ln_q_g, L0_xattn_ln_q_b, L0_xattn_ln_kv_g, L0_xattn_ln_kv_b, L0_xattn_ffn_ln_g, L0_xattn_ffn_ln_b, L0_xattn_W1, L0_xattn_b1, L0_xattn_W2, L0_xattn_b2, L1_xattn_ln1_s, L1_xattn_ln1_b, L1_xattn_w_qkv, L1_xattn_b_qkv, L1_xattn_w_ao, L1_xattn_b_ao, L1_xattn_ln2_s, L1_xattn_ln2_b, L1_xattn_w_q, L1_xattn_b_q, L1_xattn_w_kv, L1_xattn_b_kv, L1_xattn_w_co, L1_xattn_b_co, L1_xattn_ln3_s, L1_xattn_ln3_b, L1_xattn_w1, L1_xattn_b1, L1_xattn_w2, L1_xattn_b2):
    import jax
    import jax.numpy as jnp

    def _L0_xattn_ref(zt_prev, za, Wq, Wk, Wv, Wo, ln_q_g, ln_q_b, ln_kv_g, ln_kv_b, ffn_ln_g, ffn_ln_b, W1, b1, W2, b2):
        import math
        import jax, jax.numpy as jnp
        import numpy as np
        C = 256
        H = 16
        DH = C // H
        EPS = 1e-05

        def pos_enc(c, T, dtype):
            pos = jnp.arange(T, dtype=jnp.float32)[:, None]
            div = jnp.exp(jnp.arange(0, c, 2, dtype=jnp.float32) * (-math.log(10000.0) / c))
            ang = pos * div
            pe = jnp.zeros((T, c), dtype=jnp.float32)
            pe = pe.at[:, 0::2].set(jnp.sin(ang)).at[:, 1::2].set(jnp.cos(ang))
            return pe.T.astype(dtype)

        def layer_norm(x, g, b):
            mu = jnp.mean(x, axis=-1, keepdims=True)
            var = jnp.mean(jnp.square(x - mu), axis=-1, keepdims=True)
            return (x - mu) * jax.lax.rsqrt(var + EPS) * g + b
        B, _, Tq = zt_prev.shape
        Tk = za.shape[-1]
        q = jnp.transpose(zt_prev + pos_enc(C, Tq, zt_prev.dtype)[None], (0, 2, 1))
        kv = jnp.transpose(za + pos_enc(C, Tk, za.dtype)[None], (0, 2, 1))
        q = layer_norm(q, ln_q_g, ln_q_b)
        kv = layer_norm(kv, ln_kv_g, ln_kv_b)

        def split(x):
            Bt, T, _ = x.shape
            return jnp.transpose(x.reshape(Bt, T, H, DH), (0, 2, 1, 3))
        Q = split(q @ Wq)
        K = split(kv @ Wk)
        V = split(kv @ Wv)
        attn = jnp.einsum('bhqd,bhkd->bhqk', Q, K) / math.sqrt(DH)
        ctx = jnp.einsum('bhqk,bhkd->bhqd', jax.nn.softmax(attn, axis=-1), V)
        ctx = jnp.transpose(ctx, (0, 2, 1, 3)).reshape(B, Tq, C)
        y = ctx @ Wo
        r = y + q
        h = layer_norm(r, ffn_ln_g, ffn_ln_b)
        h = jax.nn.gelu(h @ W1 + b1, approximate=False) @ W2 + b2
        out = h + r
        return jnp.transpose(out, (0, 2, 1))

    def _L1_xattn_ref(hidden_states, encoder_states, ltor_mask, cross_mask, ln1_s, ln1_b, w_qkv, b_qkv, w_ao, b_ao, ln2_s, ln2_b, w_q, b_q, w_kv, b_kv, w_co, b_co, ln3_s, ln3_b, w1, b1, w2, b2):
        import jax, jax.numpy as jnp
        import numpy as np
        H = 512
        NH = 16
        HD = H // NH
        EPS = 1e-05

        def gelu(x):
            return 0.5 * x * (1.0 + jnp.tanh(0.7978845608028654 * x * (1.0 + 0.044715 * x * x)))

        def layernorm(x, scale, bias):
            m = jnp.mean(x, axis=-1, keepdims=True)
            v = jnp.mean(jnp.square(x - m), axis=-1, keepdims=True)
            return (x - m) * jax.lax.rsqrt(v + EPS) * scale + bias

        def split_heads(x):
            b, s, _ = x.shape
            return x.reshape(b, s, NH, HD).transpose(0, 2, 1, 3)

        def merge_heads(x):
            b, nh, s, hd = x.shape
            return x.transpose(0, 2, 1, 3).reshape(b, s, nh * hd)

        def attention(q, k, v, mask):
            scores = jnp.einsum('bhqd,bhkd->bhqk', q, k) / jnp.sqrt(jnp.float32(HD))
            scores = scores * mask - 10000.0 * (1.0 - mask)
            probs = jax.nn.softmax(scores, axis=-1)
            return jnp.einsum('bhqk,bhkd->bhqd', probs, v)
        ln_out = layernorm(hidden_states, ln1_s, ln1_b)
        qkv = ln_out @ w_qkv + b_qkv
        q, k, v = jnp.split(qkv, 3, axis=-1)
        ctx = merge_heads(attention(split_heads(q), split_heads(k), split_heads(v), ltor_mask))
        attn_out = ctx @ w_ao + b_ao
        x = hidden_states + attn_out
        ln_out = layernorm(x, ln2_s, ln2_b)
        q = ln_out @ w_q + b_q
        kv = encoder_states @ w_kv + b_kv
        k, v = jnp.split(kv, 2, axis=-1)
        ctx = merge_heads(attention(split_heads(q), split_heads(k), split_heads(v), cross_mask))
        cross_out = ctx @ w_co + b_co
        x = x + cross_out
        ln_out = layernorm(x, ln3_s, ln3_b)
        mlp_out = gelu(ln_out @ w1 + b1) @ w2 + b2
        return x + mlp_out
    x = _L0_xattn_ref(x, ctx_2048, L0_xattn_Wq, L0_xattn_Wk, L0_xattn_Wv, L0_xattn_Wo, L0_xattn_ln_q_g, L0_xattn_ln_q_b, L0_xattn_ln_kv_g, L0_xattn_ln_kv_b, L0_xattn_ffn_ln_g, L0_xattn_ffn_ln_b, L0_xattn_W1, L0_xattn_b1, L0_xattn_W2, L0_xattn_b2)
    x = _L1_xattn_ref(x, ctx_2048, mask_1x1xSxS2_fc1, mask_Bx1xSxS2_ff1, L1_xattn_ln1_s, L1_xattn_ln1_b, L1_xattn_w_qkv, L1_xattn_b_qkv, L1_xattn_w_ao, L1_xattn_b_ao, L1_xattn_ln2_s, L1_xattn_ln2_b, L1_xattn_w_q, L1_xattn_b_q, L1_xattn_w_kv, L1_xattn_b_kv, L1_xattn_w_co, L1_xattn_b_co, L1_xattn_ln3_s, L1_xattn_ln3_b, L1_xattn_w1, L1_xattn_b1, L1_xattn_w2, L1_xattn_b2)
    return x

_drawn_inputs = setup_inputs


def setup_inputs(seed=0):
    import zlib

    import numpy as np

    out = dict(_drawn_inputs(seed))
    spreads = {'L0_xattn_ln_q_g': (1.0, 0.2),
     'L0_xattn_ln_q_b': (0.0, 0.1),
     'L0_xattn_ln_kv_g': (1.0, 0.2),
     'L0_xattn_ln_kv_b': (0.0, 0.1),
     'L0_xattn_ffn_ln_g': (1.0, 0.2),
     'L0_xattn_ffn_ln_b': (0.0, 0.1),
     'L0_xattn_b1': (0.0, 0.1),
     'L0_xattn_b2': (0.0, 0.1),
     'L1_xattn_ln1_s': (1.0, 0.6),
     'L1_xattn_ln1_b': (0.0, 0.498),
     'L1_xattn_b_qkv': (0.0, 0.1),
     'L1_xattn_b_ao': (0.0, 0.1),
     'L1_xattn_ln2_s': (1.0, 0.6),
     'L1_xattn_ln2_b': (0.0, 0.8),
     'L1_xattn_b_q': (0.0, 2.0),
     'L1_xattn_b_kv': (0.0, 0.28),
     'L1_xattn_b_co': (0.0, 0.1),
     'L1_xattn_ln3_s': (1.0, 0.2),
     'L1_xattn_ln3_b': (0.0, 0.441),
     'L1_xattn_b1': (0.0, 0.1),
     'L1_xattn_b2': (0.0, 0.1)}
    factors = {'L1_xattn_w_qkv': 3.086, 'L1_xattn_w_q': 8.0}
    for name, (base, spread) in spreads.items():
        noise = np.random.default_rng([zlib.crc32(name.encode()), seed]).standard_normal(out[name].shape)
        drawn = base * np.exp(spread * noise) if base else spread * noise
        out[name] = jnp.asarray(drawn.astype(out[name].dtype))
    for name, factor in factors.items():
        out[name] = (out[name] * factor).astype(out[name].dtype)
    return out
```

```python
from contextlib import ExitStack

import concourse.bass as bass
from concourse import mybir

F32 = mybir.dt.float32
F32R = mybir.dt.float32r
BF16 = mybir.dt.bfloat16
ALU = mybir.AluOpType
ACT = mybir.ActivationFunctionType
AX_X = mybir.AxisListType.X

P = 128
BANK = 512
EPS = 1e-5
HEADS = 16


class Signal:

    def __init__(self, ctx, nc, name, per, unit=1):
        self.sem = ctx.enter_context(nc.semaphore(name))
        self.per = per
        self.unit = unit

    def at(self, b, n):
        return b * (self.per * self.unit) + n * self.unit


class Banks:

    def __init__(self, ctx, nc, name, n, read, **order):
        self.n = n
        self.tile = ctx.enter_context(nc.psum_tensor(name, [P, n, BANK], F32))
        self.read = read
        self.order = order

    def bank(self, section, use):
        return self.tile[:, self.order[section].index(use) % self.n, :]

    def claim(self, eng, section, use, b, late=False):
        at = self.order[section].index(use)
        if late and section == "steady":
            b = b + 1
        if at >= self.n:
            signal, n, is_late = self.read[self.order[section][at - self.n]]
            batch = b - 1 if is_late and section == "steady" else b
            eng.wait_ge(signal.sem, signal.at(batch, n))
        elif section != "first":
            k = at % self.n
            batch = b - 1 if section == "steady" else b
            if section == "steady":
                for i, u in list(enumerate(self.order["first"]))[::-1]:
                    if i % self.n == k:
                        signal, n, _ = self.read[u]
                        eng.wait_ge(signal.sem, signal.at(0, n))
                        break
            signal, n, is_late = [self.read[u] for i, u in enumerate(self.order["steady"]) if i % self.n == k][-1]
            eng.wait_ge(signal.sem, signal.at(batch, 0 if is_late else n))
        return self.bank(section, use)


def rowwise(v, tiles):
    return v.rearrange("(t p) -> p t", t=tiles)


def first_layer(nc, sems, x, ctx_in, pos, ident_in, W, hid, scratch_q, scratch_k, scratch_m):
    B, C, T = x.shape
    CT = C // P
    TT = T // P
    DH = C // HEADS
    F = W["W1"].shape[1]
    FT = F // P
    SCALE = float(DH) ** -0.5
    GROUP = P // 32
    NG = HEADS // GROUP
    RING = GROUP + 1
    Q_PARTS = (0, 0, 1, 1, 0, 2)
    K_PARTS = (0, 1, 0, 1, 2, 0)
    ROWS = len(Q_PARTS) * DH
    ROWS_M = ROWS + 3

    with ExitStack() as ctx:
        def sb(name, shape, dt=F32):
            return ctx.enter_context(nc.sbuf_tensor("a_" + name, shape, dt))

        def sig(name, per, unit=1):
            return Signal(sems, nc, "a_" + name, per, unit)

        wq, wk, wv, wo = (sb(n, [P, CT, C]) for n in ("wq", "wk", "wv", "wo"))
        w1 = sb("w1", [P, CT, F])
        w2 = sb("w2", [P, FT, C])
        gains = sb("gains", [P, 3, CT])
        shifts = sb("shifts", [P, 3, CT])
        b1 = sb("b1", [P, FT])
        b2 = sb("b2", [P, CT])
        ident = sb("ident", [P, P])
        half = sb("half", [P, 1])
        pe = sb("pe", [P, CT, T])
        xin = [sb(f"xin{s}", [P, CT, T]) for s in range(2)]
        tokn = [sb(f"tokn{s}", [P, TT, C]) for s in range(3)]
        stats = sb("stats", [P, 3, TT, 6])
        mv = sb("mv", [P, 3, TT, 2])
        vare = sb("vare", [P, 3, TT])
        rstd = sb("rstd", [P, 3, TT])
        qnT = sb("qnT", [P, CT, T])
        kvnT = sb("kvnT", [P, CT, T])
        rest = sb("rest", [P, CT, T])
        qparts = sb("qparts", [P, 3, CT, T], BF16)
        kparts = sb("kparts", [P, 3, CT, T], BF16)
        qst = sb("qst", [P, HEADS, T], BF16)
        kst = sb("kst", [P, HEADS, T], BF16)
        vaug = sb("vaug", [P, TT, HEADS, 32])
        mx = sb("mx", [P, TT, HEADS])
        mrest = sb("mrest", [HEADS, T])
        mparts = sb("mparts", [HEADS, 3, T], BF16)
        pt = sb("pt", [P, RING, TT, T])
        ctxr = sb("ctxr", [P, 2, T])
        rsum = sb("rsum", [P, NG, TT, GROUP])
        ctxt = sb("ctxt", [P, TT, C])
        ctxT = sb("ctxT", [P, CT, T])
        rT = sb("rT", [P, CT, T])
        hT = sb("hT", [P, CT, T])
        gT = sb("gT", [P, FT, T])
        outT = sb("outT", [P, CT, T])

        kinds = {}

        def filled(name, per):
            kinds[name] = sig(name + "_filled", per)
            return kinds[name]

        weights_in = sig("weights_in", 1, 16)
        consts = sig("consts", 1)
        half_set = sig("half_set", 1)
        x_in = [sig(f"x_in{s}", 1, 16) for s in range(2)]
        x_pe = [sig(f"x_pe{s}", 1) for s in range(2)]
        tok_filled = [sig(f"tok_filled{s}", 2) for s in range(3)]
        var_done = [sig(f"var_done{s}", 1) for s in range(3)]
        rstd_done = [sig(f"rstd_done{s}", 1) for s in range(3)]
        tok_done = [sig(f"tok_done{s}", 2) for s in range(3)]
        chan_filled = [sig(f"chan_filled{s}", CT) for s in range(3)]
        chan_done = [sig(f"chan_done{s}", CT) for s in range(3)]
        qk_filled = sig("qk_filled", 2 * CT)
        high = sig("high", 2 * CT)
        restd = sig("restd", 2 * CT)
        mid = sig("mid", 2 * CT)
        low = sig("low", 2 * CT)
        parts_out = [sig(f"parts_out{s}", 3, 16) for s in range(2)]
        stacked = sig("stacked", 2 * len(Q_PARTS), 16)
        v_filled = sig("v_filled", 2)
        v_done = sig("v_done", 2)
        score_filled = sig("score_filled", 4 * HEADS)
        max_done = sig("max_done", 2 * HEADS)
        m_filled = sig("m_filled", 1)
        m_high = sig("m_high", 1)
        m_rest = sig("m_rest", 1)
        m_mid = sig("m_mid", 1)
        m_low = sig("m_low", 1)
        m_out = sig("m_out", 1, 16)
        m_in = sig("m_in", 1, 16)
        exp_done = sig("exp_done", 2 * HEADS)
        pv_done = sig("pv_done", NG)
        ctx_raw = sig("ctx_raw", NG)
        ctx_filled = sig("ctx_filled", NG)
        ctx_sum = sig("ctx_sum", NG)
        ctx_tok = sig("ctx_tok", NG)
        ctxT_filled = sig("ctxT_filled", CT)
        ctx_chan = sig("ctx_chan", CT)
        y_filled = sig("y_filled", CT)
        r_done = sig("r_done", CT)
        f1_filled = sig("f1_filled", FT)
        g_done = sig("g_done", FT)
        f2_filled = sig("f2_filled", CT)
        o_done = sig("o_done", CT)
        o_out = sig("o_out", 1, 16)

        front = [("tok", s, u) for s in range(2) for u in range(2)]
        front2 = [("chan", s, c) for s in range(2) for c in range(CT)]
        front2 += [(n, m) for n in "qk" for m in range(CT)] + [("v", u) for u in range(2)]
        attn = [("m",)] + [("ctx", g) for g in range(NG - 1)]
        tail1 = [("ctx", NG - 1)] + [("ctxT", c) for c in range(CT)] + [("y", m) for m in range(CT)]
        tail2 = [("tok", 2, u) for u in range(2)] + [("chan", 2, c) for c in range(CT)]
        tail3 = [("f1", m) for m in range(FT)] + [("f2", m) for m in range(CT)]
        late = tail1 + tail2 + tail3
        read = {("m",): (m_rest, 1)}
        read |= {("tok", s, u): (tok_done[s], u + 1) for s in range(3) for u in range(2)}
        read |= {("chan", s, c): (chan_done[s], c + 1) for s in range(3) for c in range(CT)}
        read |= {(n, m): (restd, "qk".index(n) * CT + m + 1) for n in "qk" for m in range(CT)}
        read |= {("v", u): (v_done, u + 1) for u in range(2)}
        read |= {("ctx", g): (ctx_tok, g + 1) for g in range(NG)}
        read |= {("ctxT", c): (ctx_chan, c + 1) for c in range(CT)}
        read |= {("y", m): (r_done, m + 1) for m in range(CT)}
        read |= {("f1", m): (g_done, m + 1) for m in range(FT)}
        read |= {("f2", m): (o_done, m + 1) for m in range(CT)}
        read = {u: (*r, u in late) for u, r in read.items()}
        banks = Banks(ctx, nc, "a_d", 3, read, first=front + front2 + attn,
                      steady=front + tail1 + front2 + tail2 + tail3 + attn, last=late)
        score = ctx.enter_context(nc.psum_tensor("a_score", [P, 2, 2, BANK], F32))
        ctxp = ctx.enter_context(nc.psum_tensor("a_ctxp", [P, BANK], F32))
        WEIGHTS = 16

        block = ctx.enter_context(nc.Block())

        @block.sync
        def _(sp):
            def load(dst, src, columns=False):
                sp.dma_start(dst, src, allow_slow_non_contiguous=columns).then_inc(weights_in.sem, 16)

            for s, src in enumerate((x, ctx_in)):
                sp.dma_start(xin[s][:], src[0].rearrange("(c p) t -> p c t", p=P)).then_inc(x_in[s].sem, 16)
            load(pe[:], pos.rearrange("(c p) t -> p c t", p=P))
            load(ident[:], ident_in)
            for i, n in enumerate(("ln_q", "ln_kv", "ffn_ln")):
                load(gains[:, i, :], rowwise(W[n + "_g"], CT), True)
                load(shifts[:, i, :], rowwise(W[n + "_b"], CT), True)
            for dst, n in ((wq, "Wq"), (wk, "Wk"), (wv, "Wv"), (wo, "Wo"), (w1, "W1"), (w2, "W2")):
                load(dst[:], W[n].rearrange("(k p) n -> p k n", p=P))
            load(b1[:], rowwise(W["b1"], FT), True)
            load(b2[:], rowwise(W["b2"], CT), True)

            def steps(b, fetch):
                if fetch:
                    for s, src in enumerate((x, ctx_in)):
                        sp.wait_ge(tok_filled[s].sem, tok_filled[s].at(b, 2))
                        sp.dma_start(xin[s][:], src[b + 1].rearrange("(c p) t -> p c t", p=P)).then_inc(x_in[s].sem, 16)
                for s, (parts, scr) in enumerate(((qparts, scratch_q), (kparts, scratch_k))):
                    sp.wait_ge(low.sem, low.at(b, (s + 1) * CT))
                    for part in range(3):
                        sp.dma_start(scr[b, part].rearrange("(c p) n -> p c n", p=P), parts[:, part]).then_inc(parts_out[s].sem, 16)
                sp.wait_ge(score_filled.sem, score_filled.at(b, 0))
                for s, (st, scr, order) in enumerate(((qst, scratch_q, Q_PARTS), (kst, scratch_k, K_PARTS))):
                    sp.wait_ge(parts_out[s].sem, parts_out[s].at(b, 3))
                    for c, part in enumerate(order):
                        sp.dma_start(st[c * DH:(c + 1) * DH, :, :],
                                     scr[b, part].rearrange("(h d) n -> d h n", d=DH)).then_inc(stacked.sem, 16)

            def maxima(b):
                sp.wait_ge(m_low.sem, m_low.at(b, 1))
                sp.dma_start(scratch_m[b].rearrange("t h n -> h t n"), mparts[:]).then_inc(m_out.sem, 16)
                sp.wait_ge(m_out.sem, m_out.at(b, 1))
                sp.dma_start(qst[ROWS:ROWS_M, :, :], scratch_m[b]).then_inc(m_in.sem, 16)

            def store(b):
                sp.wait_ge(o_done.sem, o_done.at(b, CT))
                sp.dma_start(hid[b].rearrange("(c p) t -> p c t", p=P), outT[:]).then_inc(o_out.sem, 16)

            steps(0, True)
            maxima(0)
            with sp.Fori(0, B - 2) as i:
                steps(i + 1, True)
                store(i)
                maxima(i + 1)
            steps(B - 1, False)
            store(B - 2)
            maxima(B - 1)
            store(B - 1)
            sp.wait_ge(o_out.sem, o_out.at(B, 0))

        @block.gpsimd
        def _(pool):
            nc.gpsimd.memset(half[:], -0.5).then_inc(half_set.sem, 1)
            pool.wait_ge(half_set.sem, 1)
            pool.wait_ge(weights_in.sem, 16 * WEIGHTS)

            def add_positions(b):
                for s in range(2):
                    pool.wait_ge(x_in[s].sem, x_in[s].at(b, 1))
                    nc.gpsimd.tensor_tensor(xin[s][:], xin[s][:], pe[:], ALU.add).then_inc(x_pe[s].sem, 1)

            def rsqrt(b, s):
                pool.wait_ge(var_done[s].sem, var_done[s].at(b, 1))
                nc.gpsimd.tensor_tensor(rstd[:, s, :], vare[:, s, :], half[:].broadcast_to([P, TT]),
                                        ALU.pow).then_inc(rstd_done[s].sem, 1)

            def low_parts(b):
                for s, parts in enumerate((qparts, kparts)):
                    for m in range(CT):
                        pool.wait_ge(mid.sem, mid.at(b, s * CT + m + 1))
                        nc.gpsimd.tensor_tensor(parts[:, 2, m, :], rest[:, m, :], parts[:, 1, m, :],
                                                ALU.subtract).then_inc(low.sem, 1)

            def front(b):
                add_positions(b)
                rsqrt(b, 0)
                rsqrt(b, 1)
                low_parts(b)

            front(0)
            with pool.Fori(0, B - 1) as i:
                front(i + 1)
                rsqrt(i, 2)
            rsqrt(B - 1, 2)

        @block.tensor
        def _(pe_):
            def turn_to_tokens(sec, b, s, src):
                for u in range(2):
                    bank = banks.claim(pe_, sec, ("tok", s, u), b, late=(s == 2))
                    for t in range(2):
                        for c in range(CT):
                            at = (2 * u + t) * P
                            last = nc.tensor.transpose(bank[:, (t * CT + c) * P:(t * CT + c + 1) * P],
                                                       src[:, c, at:at + P], ident[:])
                    last.then_inc(tok_filled[s].sem, 1)

            def turn_to_channels(sec, b, s, src):
                pe_.wait_ge(tok_done[s].sem, tok_done[s].at(b, 2))
                for c in range(CT):
                    bank = banks.claim(pe_, sec, ("chan", s, c), b, late=(s == 2))
                    for t in range(TT):
                        last = nc.tensor.transpose(bank[:, t * P:(t + 1) * P], src[:, t, c * P:(c + 1) * P], ident[:])
                    last.then_inc(chan_filled[s].sem, 1)

            def front_a(sec, b):
                for s in range(2):
                    pe_.wait_ge(x_pe[s].sem, x_pe[s].at(b, 1))
                    turn_to_tokens(sec, b, s, xin[s])

            def front_b(sec, b):
                turn_to_channels(sec, b, 0, tokn[0])
                turn_to_channels(sec, b, 1, tokn[1])
                for s, (name, w, src) in enumerate((("q", wq, qnT), ("k", wk, kvnT))):
                    pe_.wait_ge(chan_done[s].sem, chan_done[s].at(b, CT))
                    for m in range(CT):
                        bank = banks.claim(pe_, sec, (name, m), b)
                        for k in range(CT):
                            mm = nc.tensor.matmul(bank, w[:, k, m * P:(m + 1) * P], src[:, k, :],
                                                  start=(k == 0), stop=(k == CT - 1))
                        mm.then_inc(qk_filled.sem, 1)
                for u in range(2):
                    bank = banks.claim(pe_, sec, ("v", u), b)
                    for t in range(2):
                        at = (2 * u + t) * P
                        for k in range(CT):
                            mm = nc.tensor.matmul(bank[:, t * C:(t + 1) * C], kvnT[:, k, at:at + P], wv[:, k, :],
                                                  start=(k == 0), stop=(k == CT - 1))
                    mm.then_inc(v_filled.sem, 1)

            def row_maxima(b, h):
                if h == 0:
                    pe_.wait_ge(stacked.sem, stacked.at(b, 2 * len(Q_PARTS)))
                for p in range(2):
                    if h == 0:
                        pe_.wait_ge(exp_done.sem, exp_done.at(b, 0))
                    else:
                        pe_.wait_ge(max_done.sem, max_done.at(b, 2 * h + p - 1))
                    for j in range(2):
                        q = (2 * p + j) * P
                        mm = nc.tensor.matmul(score[:, p, j, :], qst[0:ROWS, h, q:q + P], kst[0:ROWS, h, :],
                                              start=True, stop=True)
                    mm.then_inc(score_filled.sem, 1)

            def turn_maxima(sec, b):
                pe_.wait_ge(max_done.sem, max_done.at(b, 2 * HEADS))
                bank = banks.claim(pe_, sec, ("m",), b)
                for t in range(TT):
                    last = nc.tensor.transpose(bank[0:HEADS, t * P:(t + 1) * P], mx[:, t, :], ident[:])
                last.then_inc(m_filled.sem, 1)

            def shifted_scores(b, h):
                if h == 0:
                    pe_.wait_ge(m_in.sem, m_in.at(b, 1))
                for p in range(2):
                    if h:
                        pe_.wait_ge(exp_done.sem, exp_done.at(b, 2 * h + p - 1))
                    for j in range(2):
                        k = (2 * p + j) * P
                        mm = nc.tensor.matmul(score[:, p, j, :], kst[0:ROWS_M, h, k:k + P], qst[0:ROWS_M, h, :],
                                              start=True, stop=True)
                    mm.then_inc(score_filled.sem, 1)

            def weigh_values(b, g):
                pe_.wait_ge(exp_done.sem, exp_done.at(b, 2 * GROUP * (g + 1)))
                if g == 0:
                    pe_.wait_ge(v_done.sem, v_done.at(b, 2))
                pe_.wait_ge(ctx_raw.sem, ctx_raw.at(b, g))
                for k in range(TT):
                    for j in range(GROUP):
                        h = GROUP * g + j
                        mm = nc.tensor.matmul(ctxp[32 * j:32 * j + 32, :], vaug[:, k, h, :], pt[:, h % RING, k, :],
                                              start=(k == 0), stop=(k == TT - 1), tile_position=(0, 32 * j))
                mm.then_inc(pv_done.sem, 1)

            def turn_context(sec, b, g):
                pe_.wait_ge(ctx_raw.sem, ctx_raw.at(b, g + 1))
                bank = banks.claim(pe_, sec, ("ctx", g), b, late=(g == NG - 1))
                for t in range(TT):
                    last = nc.tensor.transpose(bank[:, t * P:(t + 1) * P], ctxr[:, g % 2, t * P:(t + 1) * P], ident[:])
                last.then_inc(ctx_filled.sem, 1)

            def attention(sec, b):
                turn_maxima(sec, b)
                for h in range(HEADS):
                    shifted_scores(b, h)
                    if h % GROUP == 0 and h:
                        weigh_values(b, h // GROUP - 1)
                    if h % GROUP == 1 and h > 1:
                        turn_context(sec, b, h // GROUP - 1)
                weigh_values(b, NG - 1)

            def tail_a(sec, b):
                turn_context(sec, b, NG - 1)
                pe_.wait_ge(ctx_tok.sem, ctx_tok.at(b, NG))
                for c in range(CT):
                    bank = banks.claim(pe_, sec, ("ctxT", c), b, late=True)
                    for t in range(TT):
                        last = nc.tensor.transpose(bank[:, t * P:(t + 1) * P], ctxt[:, t, c * P:(c + 1) * P], ident[:])
                    last.then_inc(ctxT_filled.sem, 1)
                pe_.wait_ge(ctx_chan.sem, ctx_chan.at(b, CT))
                for m in range(CT):
                    bank = banks.claim(pe_, sec, ("y", m), b, late=True)
                    for k in range(CT):
                        mm = nc.tensor.matmul(bank, wo[:, k, m * P:(m + 1) * P], ctxT[:, k, :],
                                              start=(k == 0), stop=(k == CT - 1))
                    mm.then_inc(y_filled.sem, 1)

            def tail_b(sec, b):
                pe_.wait_ge(r_done.sem, r_done.at(b, CT))
                turn_to_tokens(sec, b, 2, rT)
                turn_to_channels(sec, b, 2, tokn[2])

            def tail_c(sec, b, m):
                if m < FT:
                    if m == 0:
                        pe_.wait_ge(chan_done[2].sem, chan_done[2].at(b, CT))
                    bank = banks.claim(pe_, sec, ("f1", m), b, late=True)
                    for k in range(CT):
                        mm = nc.tensor.matmul(bank, w1[:, k, m * P:(m + 1) * P], hT[:, k, :],
                                              start=(k == 0), stop=(k == CT - 1))
                    mm.then_inc(f1_filled.sem, 1)
                else:
                    m -= FT
                    if m == 0:
                        pe_.wait_ge(g_done.sem, g_done.at(b, FT))
                    bank = banks.claim(pe_, sec, ("f2", m), b, late=True)
                    for k in range(FT):
                        mm = nc.tensor.matmul(bank, w2[:, k, m * P:(m + 1) * P], gT[:, k, :],
                                              start=(k == 0), stop=(k == FT - 1))
                    mm.then_inc(f2_filled.sem, 1)

            pe_.wait_ge(weights_in.sem, 16 * WEIGHTS)
            pe_.wait_ge(consts.sem, 2)
            front_a("first", 0)
            front_b("first", 0)
            for h in range(HEADS):
                row_maxima(0, h)
            attention("first", 0)
            with pe_.Fori(0, B - 1) as i:
                front_a("steady", i + 1)
                tail_a("steady", i)
                front_b("steady", i + 1)
                tail_b("steady", i)
                for h in range(HEADS):
                    row_maxima(i + 1, h)
                    if h % 2 == 1 and h // 2 < FT + CT:
                        tail_c("steady", i, h // 2)
                attention("steady", i + 1)
            tail_a("last", B - 1)
            tail_b("last", B - 1)
            for m in range(FT + CT):
                tail_c("last", B - 1, m)

        @block.scalar
        def _(act):
            def to_channels(sec, b, s, dst):
                for c in range(CT):
                    act.wait_ge(chan_filled[s].sem, chan_filled[s].at(b, c + 1))
                    nc.scalar.activation(dst[:, c, :], banks.bank(sec, ("chan", s, c)), ACT.Identity,
                                         bias=shifts[:, s, c:c + 1], scale=gains[:, s, c:c + 1]).then_inc(chan_done[s].sem, 1)

            def front_b(sec, b):
                act.wait_ge(r_done.sem, r_done.at(b, 0))
                to_channels(sec, b, 0, qnT)
                act.wait_ge(v_filled.sem, v_filled.at(b, 0))
                to_channels(sec, b, 1, kvnT)
                for s, (name, parts) in enumerate((("q", qparts), ("k", kparts))):
                    act.wait_ge(parts_out[s].sem, parts_out[s].at(b, 0))
                    for m in range(CT):
                        act.wait_ge(qk_filled.sem, qk_filled.at(b, s * CT + m + 1))
                        nc.scalar.activation(parts[:, 0, m, :], banks.bank(sec, (name, m)), ACT.Copy).then_inc(high.sem, 1)
                    for m in range(CT):
                        act.wait_ge(restd.sem, restd.at(b, s * CT + m + 1))
                        nc.scalar.activation(parts[:, 1, m, :], rest[:, m, :], ACT.Copy).then_inc(mid.sem, 1)
                act.wait_ge(pv_done.sem, pv_done.at(b, 0))
                for u in range(2):
                    act.wait_ge(v_filled.sem, v_filled.at(b, u + 1))
                    nc.scalar.activation(vaug[:, 2 * u:2 * u + 2, :, 0:DH],
                                         banks.bank(sec, ("v", u)).rearrange("p (t h d) -> p t h d", t=2, d=DH),
                                         ACT.Copy).then_inc(v_done.sem, 1)

            def attention(sec, b):
                act.wait_ge(m_filled.sem, m_filled.at(b, 1))
                act.wait_ge(m_out.sem, m_out.at(b, 0))
                nc.scalar.activation(mparts[:, 0, :], banks.bank(sec, ("m",))[0:HEADS, :], ACT.Copy,
                                     scale=-1.0).then_inc(m_high.sem, 1)
                for h in range(HEADS):
                    act.wait_ge(pv_done.sem, pv_done.at(b, 0 if h < RING else (h - RING) // GROUP + 1))
                    for p in range(2):
                        act.wait_ge(score_filled.sem, score_filled.at(b, 2 * HEADS + 2 * h + p + 1))
                        nc.scalar.activation(pt[:, h % RING, 2 * p:2 * p + 2, :], score[:, p, :, :], ACT.Exp,
                                             scale=SCALE).then_inc(exp_done.sem, 1)

            def tail_a(sec, b):
                act.wait_ge(y_filled.sem, y_filled.at(b, 0))
                for c in range(CT):
                    act.wait_ge(ctxT_filled.sem, ctxT_filled.at(b, c + 1))
                    nc.scalar.activation(ctxT[:, c, :], banks.bank(sec, ("ctxT", c)), ACT.Copy).then_inc(ctx_chan.sem, 1)

            def tail_b(sec, b):
                act.wait_ge(f1_filled.sem, f1_filled.at(b, 0))
                to_channels(sec, b, 2, hT)

            def tail_c(sec, b):
                act.wait_ge(f2_filled.sem, f2_filled.at(b, 0))
                for m in range(FT):
                    act.wait_ge(f1_filled.sem, f1_filled.at(b, m + 1))
                    nc.scalar.activation(gT[:, m, :], banks.bank(sec, ("f1", m)), ACT.Gelu,
                                         bias=b1[:, m:m + 1]).then_inc(g_done.sem, 1)

            act.wait_ge(weights_in.sem, 16 * WEIGHTS)
            act.wait_ge(consts.sem, 2)
            front_b("first", 0)
            attention("first", 0)
            with act.Fori(0, B - 1) as i:
                tail_a("steady", i)
                front_b("steady", i + 1)
                tail_b("steady", i)
                tail_c("steady", i)
                attention("steady", i + 1)
            tail_a("last", B - 1)
            tail_b("last", B - 1)
            tail_c("last", B - 1)

        @block.vector
        def _(dve):
            def normalise(sec, b, s):
                for u in range(2):
                    dve.wait_ge(tok_filled[s].sem, tok_filled[s].at(b, u + 1))
                    bank = banks.bank(sec, ("tok", s, u))
                    for t in range(2):
                        nc.vector.bn_stats(stats[:, s, 2 * u + t, :], bank[:, t * C:(t + 1) * C])
                nc.vector.drain()
                for t in range(TT):
                    last = nc.vector.bn_aggr(mv[:, s, t, :], stats[:, s, t, :])
                nc.vector.drain()
                nc.vector.tensor_scalar(vare[:, s, :], mv[:, s, :, 1], EPS, None, ALU.add).then_inc(var_done[s].sem, 1)

            def apply(sec, b, s):
                dve.wait_ge(rstd_done[s].sem, rstd_done[s].at(b, 1))
                dve.wait_ge(chan_filled[s].sem, chan_filled[s].at(b, 0))
                for u in range(2):
                    bank = banks.bank(sec, ("tok", s, u))
                    for t in range(2):
                        tt = 2 * u + t
                        last = nc.vector.tensor_scalar(tokn[s][:, tt, :], bank[:, t * C:(t + 1) * C], mv[:, s, tt, 0:1],
                                                       rstd[:, s, tt:tt + 1], ALU.subtract, ALU.mult)
                    last.then_inc(tok_done[s].sem, 1)

            def front_a(sec, b):
                normalise(sec, b, 0)
                apply(sec, b, 0)
                normalise(sec, b, 1)
                apply(sec, b, 1)

            def front_b(sec, b):
                for s, (name, parts) in enumerate((("q", qparts), ("k", kparts))):
                    for m in range(CT):
                        dve.wait_ge(low.sem, low.at(b, 0 if s == 0 else m + 1))
                        dve.wait_ge(high.sem, high.at(b, s * CT + m + 1))
                        nc.vector.tensor_tensor(rest[:, m, :], banks.bank(sec, (name, m)), parts[:, 0, m, :],
                                                ALU.subtract).then_inc(restd.sem, 1)

            def row_maximum(b, h):
                if h == 0:
                    dve.wait_ge(m_filled.sem, m_filled.at(b, 0))
                for p in range(2):
                    dve.wait_ge(score_filled.sem, score_filled.at(b, 2 * h + p + 1))
                    nc.vector.tensor_reduce(mx[:, 2 * p:2 * p + 2, h], score[:, p, :, :], AX_X, ALU.max).then_inc(max_done.sem, 1)

            def divide_context(sec, b, g):
                dve.wait_ge(ctx_filled.sem, ctx_filled.at(b, g + 1))
                bank = banks.bank(sec, ("ctx", g)).rearrange("p (t j c) -> p t j c", t=TT, c=32)
                nc.vector.reciprocal(rsum[:, g, :, :], bank[:, :, :, DH]).then_inc(ctx_sum.sem, 1)
                dve.wait_ge(ctx_sum.sem, ctx_sum.at(b, g + 1))
                if g == 0:
                    dve.wait_ge(ctxT_filled.sem, ctxT_filled.at(b, 0))
                out = ctxt[:, :, g * GROUP * DH:(g + 1) * GROUP * DH].rearrange("p t (j d) -> p t j d", d=DH)
                nc.vector.tensor_tensor(out, bank[:, :, :, 0:DH],
                                        rsum[:, g, :, :].unsqueeze(3).broadcast_to([P, TT, GROUP, DH]),
                                        ALU.mult).then_inc(ctx_tok.sem, 1)

            def attention(sec, b):
                dve.wait_ge(m_high.sem, m_high.at(b, 1))
                nc.vector.scalar_tensor_tensor(mrest[:], banks.bank(sec, ("m",))[0:HEADS, :], -1.0, mparts[:, 0, :],
                                               ALU.mult, ALU.subtract).then_inc(m_rest.sem, 1)
                dve.wait_ge(m_rest.sem, m_rest.at(b, 1))
                nc.vector.tensor_copy(mparts[:, 1, :], mrest[:]).then_inc(m_mid.sem, 1)
                dve.wait_ge(m_mid.sem, m_mid.at(b, 1))
                nc.vector.tensor_tensor(mparts[:, 2, :], mrest[:], mparts[:, 1, :], ALU.subtract).then_inc(m_low.sem, 1)
                for g in range(NG):
                    dve.wait_ge(pv_done.sem, pv_done.at(b, g + 1))
                    dve.wait_ge(ctx_filled.sem, ctx_filled.at(b, max(g - 1, 0)))
                    nc.vector.tensor_copy(ctxr[:, g % 2, :], ctxp[:]).then_inc(ctx_raw.sem, 1)
                    if g < NG - 1:
                        divide_context(sec, b, g)

            def tail_a(sec, b):
                divide_context(sec, b, NG - 1)
                for m in range(CT):
                    dve.wait_ge(y_filled.sem, y_filled.at(b, m + 1))
                    if m == 0:
                        dve.wait_ge(o_done.sem, o_done.at(b, 0))
                    nc.vector.tensor_tensor(rT[:, m, :], banks.bank(sec, ("y", m)), qnT[:, m, :], ALU.add).then_inc(r_done.sem, 1)

            def tail_b(sec, b):
                normalise(sec, b, 2)
                apply(sec, b, 2)

            def tail_c(sec, b, m):
                dve.wait_ge(f2_filled.sem, f2_filled.at(b, m + 1))
                if m == 0:
                    dve.wait_ge(o_out.sem, o_out.at(b, 0))
                nc.vector.scalar_tensor_tensor(outT[:, m, :], banks.bank(sec, ("f2", m)), b2[:, m:m + 1], rT[:, m, :],
                                               ALU.add, ALU.add).then_inc(o_done.sem, 1)

            nc.vector.memset(kst[ROWS:ROWS_M, :, :], 1.0)
            nc.vector.memset(vaug[:], 0.0).then_inc(consts.sem, 1)
            dve.wait_ge(consts.sem, 1)
            nc.vector.memset(vaug[:, :, :, DH:DH + 1], 1.0).then_inc(consts.sem, 1)
            dve.wait_ge(weights_in.sem, 16 * WEIGHTS)
            front_a("first", 0)
            front_b("first", 0)
            for h in range(HEADS):
                row_maximum(0, h)
            attention("first", 0)
            with dve.Fori(0, B - 1) as i:
                front_a("steady", i + 1)
                tail_a("steady", i)
                front_b("steady", i + 1)
                tail_b("steady", i)
                for h in range(HEADS):
                    row_maximum(i + 1, h)
                    if h in (HEADS - 4, HEADS - 2):
                        tail_c("steady", i, (h - HEADS + 4) // 2)
                attention("steady", i + 1)
            tail_a("last", B - 1)
            tail_b("last", B - 1)
            for m in range(CT):
                tail_c("last", B - 1, m)


def attention_layer(nc, sems, hid, enc_in, masks, ident_in, W, mid_out, scratch):
    B, S, D = hid.shape
    KT = D // P
    TT = S // P
    DH = D // HEADS
    SCALE = float(DH) ** -0.5
    MASKED = 10000.0
    Q_PARTS = (0, 0, 1, 1)
    K_PARTS = (0, 1, 0, 1)
    ROWS = len(Q_PARTS) * DH
    HH = HEADS // 2
    G = 4
    NU = HEADS // G * TT
    SELF, CROSS = 0, 1

    def unit(u):
        half, rest = divmod(u, NU // 2)
        tile, four = divmod(rest, HH // G)
        return half, tile, four

    with ExitStack() as ctx:
        def sb(name, shape, dt=F32):
            return ctx.enter_context(nc.sbuf_tensor("b_" + name, shape, dt))

        def sig(name, per, unit=1):
            return Signal(sems, nc, "b_" + name, per, unit)

        wqkv = sb("wqkv", [P, KT, 3 * D])
        wkv = sb("wkv", [P, KT, 2 * D])
        wq2 = sb("wq2", [P, KT, D])
        wout = [sb(f"wout{a}", [P, KT, D]) for a in range(2)]
        gains = sb("gains", [P, 2, KT])
        shifts = sb("shifts", [P, 2, KT])
        bqkv = sb("bqkv", [P, 3 * KT])
        bq2 = sb("bq2", [P, KT])
        bkv = sb("bkv", [P, 2 * KT])
        bqs = sb("bqs", [P, 2, KT])
        bout = [sb(f"bout{a}", [P, D]) for a in range(2)]
        ident = sb("ident", [P, P])
        half = sb("half", [P, 1])
        mask = [sb(f"mask{a}", [P, TT, S]) for a in range(2)]
        minus = [sb(f"minus{a}", [P, TT, S]) for a in range(2)]
        xt = sb("xt", [P, TT, D])
        x1 = sb("x1", [P, TT, D])
        xn = sb("xn", [P, TT, D])
        enc = sb("enc", [P, TT, D])
        lnT = sb("lnT", [P, KT, S])
        encT = sb("encT", [P, KT, S])
        stats = sb("stats", [P, 2, TT, 6])
        mv = sb("mv", [P, 2, TT, 2])
        vare = sb("vare", [P, 2, TT])
        rstd = sb("rstd", [P, 2, TT])
        full = sb("full", [P, KT, S])
        parts = sb("parts", [P, 2, KT, S], F32R)
        qst = sb("qst", [ROWS, 2, HH, S], F32R)
        kst = sb("kst", [ROWS, 2, HH, S], F32R)
        val = [sb(f"val{a}", [P, TT, D]) for a in range(2)]
        t = sb("t", [P, 2, G, S])
        nmax = sb("nmax", [P, 2, NU, G])
        pr = sb("pr", [P, 2, G, S])
        esum = sb("esum", [P, NU, G])
        rsum = sb("rsum", [P, NU, G])
        pt = sb("pt", [P, 2, TT, G * P])
        cx = sb("cx", [P, TT, D])
        cxT = sb("cxT", [P, KT, S])

        weights_in = sig("weights_in", 1, 16)
        x_in = sig("x_in", 1, 16)
        enc_load = sig("enc_load", 1, 16)
        mask_in = sig("mask_in", 1, 16)
        set_up = sig("set_up", 1)
        minus_half = sig("minus_half", 1)
        minus_done = sig("minus_done", 1)
        x_biased = [sig(f"x_biased{a}", 1) for a in range(2)]
        var_done = [sig(f"var_done{a}", 1) for a in range(2)]
        rstd_done = [sig(f"rstd_done{a}", 1) for a in range(2)]
        xn_done = [sig(f"xn_done{a}", 1) for a in range(2)]
        turn_filled = [sig(f"turn_filled{a}", 2) for a in range(2)]
        ln_done = [sig(f"ln_done{a}", KT) for a in range(2)]
        enc_filled = sig("enc_filled", 2)
        enc_done = sig("enc_done", 2)
        q_filled = [sig(f"q_filled{a}", 2) for a in range(2)]
        k_filled = [sig(f"k_filled{a}", 2) for a in range(2)]
        v_filled = [sig(f"v_filled{a}", TT) for a in range(2)]
        q_full = [sig(f"q_full{a}", KT) for a in range(2)]
        k_full = [sig(f"k_full{a}", KT) for a in range(2)]
        v_done = [sig(f"v_done{a}", TT) for a in range(2)]
        q_high = [sig(f"q_high{a}", 1) for a in range(2)]
        k_high = [sig(f"k_high{a}", 1) for a in range(2)]
        q_parts = [sig(f"q_parts{a}", 1) for a in range(2)]
        k_parts = [sig(f"k_parts{a}", 1) for a in range(2)]
        q_out = [sig(f"q_out{a}", 2, 16) for a in range(2)]
        k_out = [sig(f"k_out{a}", 2, 16) for a in range(2)]
        stacked = [[sig(f"stacked{a}{h}", 2 * len(Q_PARTS), 16) for h in range(2)] for a in range(2)]
        score_filled = [sig(f"score_filled{a}", NU) for a in range(2)]
        masked = [sig(f"masked{a}", NU) for a in range(2)]
        shifted = [sig(f"shifted{a}", NU) for a in range(2)]
        max_done = [sig(f"max_done{a}", NU) for a in range(2)]
        nmax_done = [sig(f"nmax_done{a}", NU) for a in range(2)]
        exp_done = [sig(f"exp_done{a}", NU) for a in range(2)]
        pt_filled = [sig(f"pt_filled{a}", NU * TT) for a in range(2)]
        pt_done = [sig(f"pt_done{a}", NU * TT) for a in range(2)]
        pv_done = [sig(f"pv_done{a}", NU) for a in range(2)]
        recip_done = [sig(f"recip_done{a}", NU // 2) for a in range(2)]
        cx_done = [sig(f"cx_done{a}", NU // 2) for a in range(2)]
        cxT_filled = [sig(f"cxT_filled{a}", 2) for a in range(2)]
        cxT_done = [sig(f"cxT_done{a}", KT) for a in range(2)]
        o_filled = [sig(f"o_filled{a}", TT) for a in range(2)]
        x_done = [sig(f"x_done{a}", TT) for a in range(2)]
        x_out = sig("x_out", 1, 16)

        front = [("turn", 0, u) for u in range(2)] + [("q", 0, u) for u in range(2)]
        front += [("k", 0, u) for u in range(2)] + [("v", 0, t_) for t_ in range(TT)]
        encode = [("enc", u) for u in range(2)]
        encode += [("k", 1, u) for u in range(2)] + [("v", 1, t_) for t_ in range(TT)]

        def attend_uses(a):
            return [("pt", a, u, k) for u in range(NU) for k in range(TT)]

        def output_uses(a):
            return [("cxT", a, u) for u in range(2)] + [("o", a, t_) for t_ in range(TT)]

        between = output_uses(0)
        second = [("turn", 1, u) for u in range(2)] + [("q", 1, u) for u in range(2)]
        late = encode + attend_uses(0) + between + second + attend_uses(1) + output_uses(1)
        order_last = late
        order_steady = encode + attend_uses(0) + between + front + second + attend_uses(1) + output_uses(1)
        read = {("enc", u): (enc_done, u + 1) for u in range(2)}
        for a in range(2):
            read |= {("turn", a, u): (ln_done[a], 2 * u + 2) for u in range(2)}
            read |= {("q", a, u): (q_full[a], 2 * u + 2) for u in range(2)}
            read |= {("k", a, u): (k_full[a], 2 * u + 2) for u in range(2)}
            read |= {("v", a, t_): (v_done[a], t_ + 1) for t_ in range(TT)}
            read |= {("pt", a, u, k): (pt_done[a], u * TT + k + 1) for u in range(NU) for k in range(TT)}
            read |= {("cxT", a, u): (cxT_done[a], 2 * u + 2) for u in range(2)}
            read |= {("o", a, t_): (x_done[a], t_ + 1) for t_ in range(TT)}
        read = {u: (*r, u in late) for u, r in read.items()}
        banks = Banks(ctx, nc, "b_d", 3, read, first=front, steady=order_steady, last=order_last)
        score = ctx.enter_context(nc.psum_tensor("b_score", [P, 2, 2, BANK], F32))
        ctxp = ctx.enter_context(nc.psum_tensor("b_ctxp", [P, BANK], F32))
        WEIGHTS = 16

        block = ctx.enter_context(nc.Block())

        @block.sync
        def _(sp):
            def load(dst, src, columns=False):
                sp.dma_start(dst, src, allow_slow_non_contiguous=columns).then_inc(weights_in.sem, 16)

            def tokens(v):
                return v.rearrange("(t p) n -> p t n", p=P)

            sp.dma_start(xt[:], tokens(hid[0])).then_inc(x_in.sem, 16)
            load(ident[:], ident_in)
            for a, n in enumerate(("ln1", "ln2")):
                load(gains[:, a, :], rowwise(W[n + "_s"], KT), True)
                load(shifts[:, a, :], rowwise(W[n + "_b"], KT), True)
            load(bqkv[:], rowwise(W["b_qkv"], 3 * KT), True)
            load(bq2[:], rowwise(W["b_q"], KT), True)
            load(bkv[:], rowwise(W["b_kv"], 2 * KT), True)
            for dst, n in ((wqkv, "w_qkv"), (wkv, "w_kv"), (wq2, "w_q"), (wout[0], "w_ao"), (wout[1], "w_co")):
                load(dst[:], W[n].rearrange("(k p) n -> p k n", p=P))
            for a, n in enumerate(("b_ao", "b_co")):
                load(bout[a][:], W[n].rearrange("(a n) -> a n", a=1).broadcast_to([P, D]))
            load(mask[0][:], tokens(masks[0][0, 0]))
            sp.dma_start(enc[:], tokens(enc_in[0])).then_inc(enc_load.sem, 16)
            sp.dma_start(mask[1][:], tokens(masks[1][0, 0])).then_inc(mask_in.sem, 16)

            def put(a, b, which):
                ready, out = (q_parts, q_out) if which == 0 else (k_parts, k_out)
                sp.wait_ge(ready[a].sem, ready[a].at(b, 1))
                for part in range(2):
                    sp.dma_start(scratch[a][which][b, part].rearrange("(k p) n -> p k n", p=P),
                                 parts[:, part].bitcast(F32)).then_inc(out[a].sem, 16)

            def stack(a, b, h):
                if a == SELF:
                    sp.wait_ge(score_filled[CROSS].sem, score_filled[CROSS].at(b, 0))
                else:
                    sp.wait_ge(score_filled[SELF].sem, score_filled[SELF].at(b, (h + 1) * NU // 2))
                sp.wait_ge(q_out[a].sem, q_out[a].at(b, 2))
                sp.wait_ge(k_out[a].sem, k_out[a].at(b, 2))
                for which, (st, order) in enumerate(((qst, Q_PARTS), (kst, K_PARTS))):
                    for c, part in enumerate(order):
                        sp.dma_start(st[c * DH:(c + 1) * DH, h, :, :].bitcast(F32),
                                     scratch[a][which][b, part, h * HH * DH:(h + 1) * HH * DH, :].rearrange(
                                         "(h d) n -> d h n", d=DH)).then_inc(stacked[a][h].sem, 16)

            def front_puts(b):
                put(SELF, b, 0)
                put(SELF, b, 1)

            def late_steps(b, more):
                stack(SELF, b, 0)
                stack(SELF, b, 1)
                put(CROSS, b, 1)
                if more:
                    sp.wait_ge(x_done[0].sem, x_done[0].at(b, TT))
                    sp.dma_start(xt[:], tokens(hid[b + 1])).then_inc(x_in.sem, 16)
                    front_puts(b + 1)
                put(CROSS, b, 0)
                stack(CROSS, b, 0)
                stack(CROSS, b, 1)
                if more:
                    sp.wait_ge(enc_filled.sem, enc_filled.at(b, 2))
                    sp.dma_start(enc[:], tokens(enc_in[b + 1])).then_inc(enc_load.sem, 16)
                    sp.wait_ge(masked[CROSS].sem, masked[CROSS].at(b, NU))
                    sp.wait_ge(shifted[CROSS].sem, shifted[CROSS].at(b, NU))
                    sp.dma_start(mask[1][:], tokens(masks[1][b + 1, 0])).then_inc(mask_in.sem, 16)
                sp.wait_ge(x_done[1].sem, x_done[1].at(b, TT))
                sp.dma_start(tokens(mid_out[b]), x1[:]).then_inc(x_out.sem, 16)

            front_puts(0)
            with sp.Fori(0, B - 1) as i:
                late_steps(i, True)
            late_steps(B - 1, False)
            sp.wait_ge(x_out.sem, x_out.at(B, 0))

        @block.gpsimd
        def _(pool):
            nc.gpsimd.memset(half[:], -0.5).then_inc(minus_half.sem, 1)
            pool.wait_ge(minus_half.sem, 1)
            pool.wait_ge(weights_in.sem, 16 * WEIGHTS)

            def rsqrt(b, a):
                pool.wait_ge(var_done[a].sem, var_done[a].at(b, 1))
                nc.gpsimd.tensor_tensor(rstd[:, a, :], vare[:, a, :], half[:].broadcast_to([P, TT]),
                                        ALU.pow).then_inc(rstd_done[a].sem, 1)

            def add_bias(b, a, x, src):
                pool.wait_ge(xn_done[a].sem, xn_done[a].at(b, 1))
                nc.gpsimd.tensor_tensor(x[:], x[:], bout[a][:].unsqueeze(1).broadcast_to([P, TT, D]),
                                        ALU.add).then_inc(x_biased[a].sem, 1)

            rsqrt(0, 0)
            add_bias(0, 0, xt, None)
            with pool.Fori(0, B - 1) as i:
                rsqrt(i + 1, 0)
                rsqrt(i, 1)
                add_bias(i + 1, 0, xt, None)
                add_bias(i, 1, x1, None)
            rsqrt(B - 1, 1)
            add_bias(B - 1, 1, x1, None)

        @block.tensor
        def _(pe):
            def turn(sec, b, use, src, filled):
                for u in range(2):
                    bank = banks.claim(pe, sec, use + (u,), b, late=use != ("turn", 0))
                    for j in range(2):
                        for t_ in range(TT):
                            k = 2 * u + j
                            last = nc.tensor.transpose(bank[:, (j * TT + t_) * P:(j * TT + t_ + 1) * P],
                                                       src[:, t_, k * P:(k + 1) * P], ident[:])
                    last.then_inc(filled.sem, 1)

            def project(sec, b, use, w, col, src, filled, is_late):
                for u in range(2):
                    bank = banks.claim(pe, sec, use + (u,), b, late=is_late)
                    for j in range(2):
                        m = col + (2 * u + j) * P
                        for k in range(KT):
                            mm = nc.tensor.matmul(bank[:, j * S:(j + 1) * S], w[:, k, m:m + P], src[:, k, :],
                                                  start=(k == 0), stop=(k == KT - 1))
                    mm.then_inc(filled.sem, 1)

            def by_token(sec, b, use, w, col, src, filled, is_late):
                for t_ in range(TT):
                    bank = banks.claim(pe, sec, use + (t_,), b, late=is_late)
                    for k in range(KT):
                        mm = nc.tensor.matmul(bank, src[:, k, t_ * P:(t_ + 1) * P], w[:, k, col:col + D],
                                              start=(k == 0), stop=(k == KT - 1))
                    mm.then_inc(filled.sem, 1)

            def front_turn(sec, b):
                pe.wait_ge(xn_done[0].sem, xn_done[0].at(b, 1))
                turn(sec, b, ("turn", 0), xn, turn_filled[0])

            def front_project(sec, b):
                pe.wait_ge(ln_done[0].sem, ln_done[0].at(b, KT))
                project(sec, b, ("q", 0), wqkv, 0, lnT, q_filled[0], False)
                project(sec, b, ("k", 0), wqkv, D, lnT, k_filled[0], False)
                by_token(sec, b, ("v", 0), wqkv, 2 * D, lnT, v_filled[0], False)

            def encode(sec, b):
                pe.wait_ge(enc_load.sem, enc_load.at(b, 1))
                turn(sec, b, ("enc",), enc, enc_filled)
                pe.wait_ge(enc_done.sem, enc_done.at(b, 2))
                project(sec, b, ("k", 1), wkv, 0, encT, k_filled[1], True)
                by_token(sec, b, ("v", 1), wkv, D, encT, v_filled[1], True)

            def attend(sec, b, a):
                def scores(u):
                    h, q, four = unit(u)
                    if u % (NU // 2) == 0:
                        pe.wait_ge(stacked[a][h].sem, stacked[a][h].at(b, 2 * len(Q_PARTS)))
                    if u >= 2:
                        pe.wait_ge(masked[a].sem, masked[a].at(b, u - 1))
                    elif a == CROSS:
                        pe.wait_ge(masked[SELF].sem, masked[SELF].at(b, NU))
                    else:
                        pe.wait_ge(masked[CROSS].sem, masked[CROSS].at(b, 0))
                    for j in range(G):
                        hh = four * G + j
                        mm = nc.tensor.matmul(score[:, u % 2, j // 2, (j % 2) * S:(j % 2 + 1) * S],
                                              qst[:, h, hh, q * P:(q + 1) * P], kst[:, h, hh, :],
                                              start=True, stop=True)
                    mm.then_inc(score_filled[a].sem, 1)

                def turn_probs(u):
                    pe.wait_ge(exp_done[a].sem, exp_done[a].at(b, u + 1))
                    for k in range(TT):
                        bank = banks.claim(pe, sec, ("pt", a, u, k), b, late=True)
                        for j in range(G):
                            last = nc.tensor.transpose(bank[:, j * P:(j + 1) * P], pr[:, u % 2, j, k * P:(k + 1) * P], ident[:])
                        last.then_inc(pt_filled[a].sem, 1)

                def weigh(u):
                    h, q, four = unit(u)
                    pe.wait_ge(pt_done[a].sem, pt_done[a].at(b, (u + 1) * TT))
                    if u == 0:
                        pe.wait_ge(v_done[a].sem, v_done[a].at(b, TT))
                    if four == 0:
                        if u:
                            pe.wait_ge(cx_done[a].sem, cx_done[a].at(b, u // 2))
                        elif a == CROSS:
                            pe.wait_ge(cx_done[SELF].sem, cx_done[SELF].at(b, NU // 2))
                        else:
                            pe.wait_ge(cx_done[CROSS].sem, cx_done[CROSS].at(b, 0))
                    for j in range(G):
                        head = (h * HH + four * G + j) * DH
                        for k in range(TT):
                            mm = nc.tensor.matmul(ctxp[:, (four * G + j) * DH:(four * G + j + 1) * DH],
                                                  pt[:, u % 2, k, j * P:(j + 1) * P], val[a][:, k, head:head + DH],
                                                  start=(k == 0), stop=(k == TT - 1))
                    mm.then_inc(pv_done[a].sem, 1)

                scores(0)
                for u in range(NU):
                    if u + 1 < NU:
                        scores(u + 1)
                    turn_probs(u)
                    if u:
                        weigh(u - 1)
                weigh(NU - 1)

            def output(sec, b, a):
                pe.wait_ge(cx_done[a].sem, cx_done[a].at(b, NU // 2))
                turn(sec, b, ("cxT", a), cx, cxT_filled[a])
                pe.wait_ge(cxT_done[a].sem, cxT_done[a].at(b, KT))
                by_token(sec, b, ("o", a), wout[a], 0, cxT, o_filled[a], True)

            def second(sec, b):
                pe.wait_ge(xn_done[1].sem, xn_done[1].at(b, 1))
                turn(sec, b, ("turn", 1), xn, turn_filled[1])
                pe.wait_ge(ln_done[1].sem, ln_done[1].at(b, KT))
                project(sec, b, ("q", 1), wq2, 0, lnT, q_filled[1], True)

            pe.wait_ge(weights_in.sem, 16 * WEIGHTS)
            front_turn("first", 0)
            front_project("first", 0)
            with pe.Fori(0, B - 1) as i:
                encode("steady", i)
                attend("steady", i, SELF)
                output("steady", i, SELF)
                front_turn("steady", i + 1)
                front_project("steady", i + 1)
                second("steady", i)
                attend("steady", i, CROSS)
                output("steady", i, CROSS)
            encode("last", B - 1)
            attend("last", B - 1, SELF)
            output("last", B - 1, SELF)
            second("last", B - 1)
            attend("last", B - 1, CROSS)
            output("last", B - 1, CROSS)

        @block.scalar
        def _(act):
            def turned(sec, b, a):
                for k in range(KT):
                    act.wait_ge(turn_filled[a].sem, turn_filled[a].at(b, k // 2 + 1))
                    bank = banks.bank(sec, ("turn", a, k // 2))
                    nc.scalar.activation(lnT[:, k, :], bank[:, (k % 2) * S:(k % 2 + 1) * S], ACT.Identity,
                                         bias=shifts[:, a, k:k + 1], scale=gains[:, a, k:k + 1]).then_inc(ln_done[a].sem, 1)

            def biased(sec, b, use, a, filled, done, bias, scale):
                for k in range(KT):
                    act.wait_ge(filled[a].sem, filled[a].at(b, k // 2 + 1))
                    bank = banks.bank(sec, (use, a, k // 2))
                    nc.scalar.activation(full[:, k, :], bank[:, (k % 2) * S:(k % 2 + 1) * S], ACT.Identity,
                                         bias=bias[:, k:k + 1], scale=scale).then_inc(done[a].sem, 1)

            def front(sec, b, first):
                if not first:
                    act.wait_ge(q_filled[1].sem, q_filled[1].at(b - 1, 0))
                turned(sec, b, 0)
                if not first:
                    act.wait_ge(k_parts[1].sem, k_parts[1].at(b - 1, 1))
                biased(sec, b, "q", 0, q_filled, q_full, bqs[:, 0, :], SCALE)
                act.wait_ge(q_parts[0].sem, q_parts[0].at(b, 1))
                biased(sec, b, "k", 0, k_filled, k_full, bqkv[:, KT:2 * KT], 1.0)
                values(sec, b, 0)

            def values(sec, b, a):
                act.wait_ge(pv_done[a].sem, pv_done[a].at(b, 0))
                for t_ in range(TT):
                    act.wait_ge(v_filled[a].sem, v_filled[a].at(b, t_ + 1))
                    nc.scalar.activation(val[a][:, t_, :], banks.bank(sec, ("v", a, t_)), ACT.Copy).then_inc(v_done[a].sem, 1)

            def encode(sec, b):
                act.wait_ge(v_filled[1].sem, v_filled[1].at(b, 0))
                for u in range(2):
                    act.wait_ge(enc_filled.sem, enc_filled.at(b, u + 1))
                    nc.scalar.activation(encT[:, 2 * u:2 * u + 2, :], banks.bank(sec, ("enc", u)).rearrange("p (k n) -> p k n", k=2),
                                         ACT.Copy).then_inc(enc_done.sem, 1)
                act.wait_ge(k_parts[0].sem, k_parts[0].at(b, 1))
                act.wait_ge(q_parts[1].sem, q_parts[1].at(b, 0))
                biased(sec, b, "k", 1, k_filled, k_full, bkv[:, 0:KT], 1.0)
                values(sec, b, 1)

            def attend(sec, b, a):
                def exponentials(u):
                    act.wait_ge(nmax_done[a].sem, nmax_done[a].at(b, u + 1))
                    if u >= 2:
                        act.wait_ge(pt_filled[a].sem, pt_filled[a].at(b, (u - 1) * TT))
                    elif a == CROSS:
                        act.wait_ge(pt_filled[SELF].sem, pt_filled[SELF].at(b, NU * TT))
                    else:
                        act.wait_ge(pt_filled[CROSS].sem, pt_filled[CROSS].at(b, 0))
                    if u == 0:
                        if a == CROSS:
                            act.wait_ge(recip_done[SELF].sem, recip_done[SELF].at(b, NU // 2))
                        else:
                            act.wait_ge(recip_done[CROSS].sem, recip_done[CROSS].at(b, 0))
                    for j in range(G):
                        last = nc.scalar.activation(pr[:, u % 2, j, :], t[:, u % 2, j, :], ACT.Exp,
                                                    bias=nmax[:, 1, u, j:j + 1], accum_out=esum[:, u, j:j + 1])
                    last.then_inc(exp_done[a].sem, 1)

                def keep(u):
                    for k in range(TT):
                        act.wait_ge(pt_filled[a].sem, pt_filled[a].at(b, u * TT + k + 1))
                        if k == 0:
                            if u >= 2:
                                act.wait_ge(pv_done[a].sem, pv_done[a].at(b, u - 1))
                            elif a == CROSS:
                                act.wait_ge(pv_done[SELF].sem, pv_done[SELF].at(b, NU))
                            else:
                                act.wait_ge(pv_done[CROSS].sem, pv_done[CROSS].at(b, 0))
                        nc.scalar.activation(pt[:, u % 2, k, :], banks.bank(sec, ("pt", a, u, k)), ACT.Copy).then_inc(pt_done[a].sem, 1)

                exponentials(0)
                for u in range(NU):
                    if u + 1 < NU:
                        exponentials(u + 1)
                    keep(u)

            def output(sec, b, a):
                bias = bqkv[:, 2 * KT:3 * KT] if a == SELF else bkv[:, KT:2 * KT]
                if a == CROSS:
                    act.wait_ge(o_filled[SELF].sem, o_filled[SELF].at(b, TT))
                else:
                    act.wait_ge(o_filled[CROSS].sem, o_filled[CROSS].at(b, 0))
                for k in range(KT):
                    act.wait_ge(cxT_filled[a].sem, cxT_filled[a].at(b, k // 2 + 1))
                    bank = banks.bank(sec, ("cxT", a, k // 2))
                    nc.scalar.activation(cxT[:, k, :], bank[:, (k % 2) * S:(k % 2 + 1) * S], ACT.Identity,
                                         bias=bias[:, k:k + 1]).then_inc(cxT_done[a].sem, 1)

            def second(sec, b, more):
                if more:
                    act.wait_ge(v_filled[0].sem, v_filled[0].at(b + 1, TT))
                else:
                    act.wait_ge(q_filled[1].sem, q_filled[1].at(b, 0))
                turned(sec, b, 1)
                if more:
                    act.wait_ge(k_parts[0].sem, k_parts[0].at(b + 1, 1))
                else:
                    act.wait_ge(k_parts[1].sem, k_parts[1].at(b, 1))
                biased(sec, b, "q", 1, q_filled, q_full, bqs[:, 1, :], SCALE)

            act.wait_ge(weights_in.sem, 16 * WEIGHTS)
            act.wait_ge(set_up.sem, 2)
            front("first", 0, True)
            with act.Fori(0, B - 1) as i:
                encode("steady", i)
                attend("steady", i, SELF)
                output("steady", i, SELF)
                front("steady", i + 1, False)
                second("steady", i, True)
                attend("steady", i, CROSS)
                output("steady", i, CROSS)
            encode("last", B - 1)
            attend("last", B - 1, SELF)
            output("last", B - 1, SELF)
            second("last", B - 1, False)
            attend("last", B - 1, CROSS)
            output("last", B - 1, CROSS)

        @block.vector
        def _(dve):
            def normalise(b, a, x):
                for t_ in range(TT):
                    nc.vector.bn_stats(stats[:, a, t_, :], x[:, t_, :])
                nc.vector.drain()
                for t_ in range(TT):
                    last = nc.vector.bn_aggr(mv[:, a, t_, :], stats[:, a, t_, :])
                nc.vector.drain()
                nc.vector.tensor_scalar(vare[:, a, :], mv[:, a, :, 1], EPS, None, ALU.add).then_inc(var_done[a].sem, 1)

            def apply(b, a, x):
                dve.wait_ge(rstd_done[a].sem, rstd_done[a].at(b, 1))
                for t_ in range(TT):
                    last = nc.vector.tensor_scalar(xn[:, t_, :], x[:, t_, :], mv[:, a, t_, 0:1], rstd[:, a, t_:t_ + 1],
                                                   ALU.subtract, ALU.mult)
                last.then_inc(xn_done[a].sem, 1)

            def split(b, full_done, high, ready, out, out_count):
                dve.wait_ge(full_done.sem, full_done.at(b, KT))
                dve.wait_ge(out.sem, out_count)
                nc.vector.tensor_copy(parts[:, 0], full[:]).then_inc(high.sem, 1)
                dve.wait_ge(high.sem, high.at(b, 1))
                nc.vector.tensor_tensor(parts[:, 1], full[:], parts[:, 0].bitcast(F32), ALU.subtract).then_inc(ready.sem, 1)

            def front_norm(b, first):
                dve.wait_ge(x_in.sem, x_in.at(b, 1))
                normalise(b, 0, xt)
                if not first:
                    dve.wait_ge(turn_filled[1].sem, turn_filled[1].at(b - 1, 0))
                apply(b, 0, xt)

            def front_split(b, first):
                if first:
                    split(b, q_full[0], q_high[0], q_parts[0], k_out[1], 0)
                else:
                    split(b, q_full[0], q_high[0], q_parts[0], k_out[1], k_out[1].at(b - 1, 2))
                split(b, k_full[0], k_high[0], k_parts[0], q_out[0], q_out[0].at(b, 2))

            def encode(b):
                dve.wait_ge(q_out[1].sem, q_out[1].at(b, 0))
                split(b, k_full[1], k_high[1], k_parts[1], k_out[0], k_out[0].at(b, 2))

            def negative(b):
                nc.vector.tensor_scalar(minus[1][:], mask[1][:], 1.0, MASKED, ALU.subtract, ALU.mult).then_inc(minus_done.sem, 1)

            def attend(b, a):
                def soften(u):
                    h, q, four = unit(u)
                    dve.wait_ge(score_filled[a].sem, score_filled[a].at(b, u + 1))
                    if u >= 2:
                        dve.wait_ge(exp_done[a].sem, exp_done[a].at(b, u - 1))
                    elif a == CROSS:
                        dve.wait_ge(exp_done[SELF].sem, exp_done[SELF].at(b, NU))
                    else:
                        dve.wait_ge(exp_done[CROSS].sem, exp_done[CROSS].at(b, 0))
                    nc.vector.tensor_tensor(t[:, u % 2], score[:, u % 2].rearrange("p x (y n) -> p (x y) n", y=2),
                                            mask[a][:, q, :].unsqueeze(1).broadcast_to([P, G, S]), ALU.mult).then_inc(masked[a].sem, 1)
                    dve.wait_ge(masked[a].sem, masked[a].at(b, u + 1))
                    nc.vector.tensor_tensor(t[:, u % 2], t[:, u % 2], minus[a][:, q, :].unsqueeze(1).broadcast_to([P, G, S]),
                                            ALU.add).then_inc(shifted[a].sem, 1)
                    dve.wait_ge(shifted[a].sem, shifted[a].at(b, u + 1))
                    nc.vector.tensor_reduce(nmax[:, 0, u, :], t[:, u % 2], AX_X, ALU.max).then_inc(max_done[a].sem, 1)
                    dve.wait_ge(max_done[a].sem, max_done[a].at(b, u + 1))
                    nc.vector.tensor_scalar(nmax[:, 1, u, :], nmax[:, 0, u, :], -1.0, None, ALU.mult).then_inc(nmax_done[a].sem, 1)

                def divide(n):
                    h, q, _ = unit(2 * n)
                    dve.wait_ge(pv_done[a].sem, pv_done[a].at(b, 2 * n + 2))
                    nc.vector.reciprocal(rsum[:, 2 * n:2 * n + 2, :], esum[:, 2 * n:2 * n + 2, :]).then_inc(recip_done[a].sem, 1)
                    dve.wait_ge(recip_done[a].sem, recip_done[a].at(b, n + 1))
                    if n == 0:
                        if a == CROSS:
                            dve.wait_ge(cxT_filled[SELF].sem, cxT_filled[SELF].at(b, 2))
                        else:
                            dve.wait_ge(cxT_filled[CROSS].sem, cxT_filled[CROSS].at(b, 0))
                    nc.vector.tensor_tensor(cx[:, q, h * HH * DH:(h + 1) * HH * DH].rearrange("p (h d) -> p h d", d=DH),
                                            ctxp[:, 0:HH * DH].rearrange("p (h d) -> p h d", d=DH),
                                            rsum[:, 2 * n:2 * n + 2, :].rearrange("p a b -> p (a b)").unsqueeze(2).broadcast_to([P, HH, DH]),
                                            ALU.mult).then_inc(cx_done[a].sem, 1)

                for u in range(NU):
                    soften(u)
                    if u % 2 == 1 and u >= 3:
                        divide(u // 2 - 1)
                divide(NU // 2 - 1)

            def output(sec, b, a):
                dve.wait_ge(x_biased[a].sem, x_biased[a].at(b, 1))
                if a == SELF:
                    dve.wait_ge(x_out.sem, x_out.at(b, 0))
                x = xt if a == SELF else x1
                for t_ in range(TT):
                    dve.wait_ge(o_filled[a].sem, o_filled[a].at(b, t_ + 1))
                    nc.vector.tensor_tensor(x1[:, t_, :], banks.bank(sec, ("o", a, t_)), x[:, t_, :], ALU.add).then_inc(x_done[a].sem, 1)

            def second_norm(b, more):
                dve.wait_ge(x_done[0].sem, x_done[0].at(b, TT))
                normalise(b, 1, x1)
                if more:
                    dve.wait_ge(turn_filled[0].sem, turn_filled[0].at(b + 1, 2))
                else:
                    dve.wait_ge(turn_filled[1].sem, turn_filled[1].at(b, 0))
                apply(b, 1, x1)

            def second_split(b, more):
                if more:
                    split(b, q_full[1], q_high[1], q_parts[1], k_out[0], k_out[0].at(b + 1, 2))
                else:
                    split(b, q_full[1], q_high[1], q_parts[1], k_out[1], k_out[1].at(b, 2))

            dve.wait_ge(weights_in.sem, 16 * WEIGHTS)
            nc.vector.tensor_scalar(minus[0][:], mask[0][:], 1.0, MASKED, ALU.subtract, ALU.mult)
            nc.vector.tensor_scalar(bqs[:, 0, :], bqkv[:, 0:KT], SCALE, None, ALU.mult).then_inc(set_up.sem, 1)
            nc.vector.tensor_scalar(bqs[:, 1, :], bq2[:], SCALE, None, ALU.mult).then_inc(set_up.sem, 1)
            dve.wait_ge(set_up.sem, 2)
            front_norm(0, True)
            front_split(0, True)

            def late_steps(sec, b, more):
                dve.wait_ge(mask_in.sem, mask_in.at(b, 1))
                negative(b)
                encode(b)
                attend(b, SELF)
                output(sec, b, SELF)
                if more:
                    front_norm(b + 1, False)
                    front_split(b + 1, False)
                second_norm(b, more)
                second_split(b, more)
                dve.wait_ge(minus_done.sem, minus_done.at(b, 1))
                attend(b, CROSS)
                output(sec, b, CROSS)

            with dve.Fori(0, B - 1) as i:
                late_steps("steady", i, True)
            late_steps("last", B - 1, False)


def network_layer(nc, sems, mid_in, ident_in, W, out):
    B, S, D = mid_in.shape
    KT = D // P
    TT = S // P
    F = W["w1"].shape[1]
    FT = F // P
    with ExitStack() as ctx:
        def sb(name, shape, dt=F32):
            return ctx.enter_context(nc.sbuf_tensor("c_" + name, shape, dt))

        def sig(name, per, unit=1):
            return Signal(sems, nc, "c_" + name, per, unit)

        w1 = sb("w1", [P, KT, F])
        w2 = sb("w2", [P, FT, D])
        gain = sb("gain", [P, KT])
        shift = sb("shift", [P, KT])
        b1 = sb("b1", [P, FT])
        b2 = sb("b2", [P, D])
        ident = sb("ident", [P, P])
        half = sb("half", [P, 1])
        xt = sb("xt", [P, TT, D])
        xn = sb("xn", [P, TT, D])
        xb = sb("xb", [P, TT, D])
        stats = sb("stats", [P, TT, 6])
        mv = sb("mv", [P, TT, 2])
        vare = sb("vare", [P, TT])
        rstd = sb("rstd", [P, TT])
        lnT = sb("lnT", [P, KT, S])
        gT = sb("gT", [P, FT, S])
        res = sb("res", [P, TT, D])

        weights_in = sig("weights_in", 1, 16)
        w2_in = sig("w2_in", 1, 16)
        x_in = sig("x_in", 1, 16)
        minus_half = sig("minus_half", 1)
        var_done = sig("var_done", 1)
        rstd_done = sig("rstd_done", 1)
        xn_done = sig("xn_done", 1)
        xb_done = sig("xb_done", 1)
        turn_filled = sig("turn_filled", 2)
        ln_done = sig("ln_done", KT)
        f1_filled = sig("f1_filled", FT // 2)
        g_done = sig("g_done", FT)
        f2_filled = sig("f2_filled", TT)
        res_done = sig("res_done", TT)
        x_out = sig("x_out", 1, 16)

        turns = [("turn", u) for u in range(2)]
        ups = [("f1", u) for u in range(FT // 2)]
        downs = [("f2", t_) for t_ in range(TT)]
        read = {("turn", u): (ln_done, 2 * u + 2, False) for u in range(2)}
        read |= {("f1", u): (g_done, 2 * u + 2, True) for u in range(FT // 2)}
        read |= {("f2", t_): (res_done, t_ + 1, True) for t_ in range(TT)}
        banks = Banks(ctx, nc, "c_d", 6, read, first=turns, steady=ups + turns + downs, last=ups + downs)

        block = ctx.enter_context(nc.Block())

        def tokens(v):
            return v.rearrange("(t p) n -> p t n", p=P)

        @block.sync
        def _(sp):
            def load(dst, src, columns=False):
                sp.dma_start(dst, src, allow_slow_non_contiguous=columns).then_inc(weights_in.sem, 16)

            sp.dma_start(xt[:], tokens(mid_in[0])).then_inc(x_in.sem, 16)
            load(ident[:], ident_in)
            load(gain[:], rowwise(W["ln3_s"], KT), True)
            load(shift[:], rowwise(W["ln3_b"], KT), True)
            load(b1[:], rowwise(W["b1"], FT), True)
            load(b2[:], W["b2"].rearrange("(a n) -> a n", a=1).broadcast_to([P, D]))
            load(w1[:], W["w1"].rearrange("(k p) n -> p k n", p=P))
            sp.dma_start(w2[:], W["w2"].rearrange("(k p) n -> p k n", p=P)).then_inc(w2_in.sem, 16)

            def store(b):
                sp.wait_ge(res_done.sem, res_done.at(b, TT))
                sp.dma_start(tokens(out[b]), res[:]).then_inc(x_out.sem, 16)

            with sp.Fori(0, B - 1) as i:
                sp.wait_ge(xb_done.sem, xb_done.at(i, 1))
                sp.dma_start(xt[:], tokens(mid_in[i + 1])).then_inc(x_in.sem, 16)
                store(i)
            store(B - 1)
            sp.wait_ge(x_out.sem, x_out.at(B, 0))

        @block.gpsimd
        def _(pool):
            nc.gpsimd.memset(half[:], -0.5).then_inc(minus_half.sem, 1)
            pool.wait_ge(minus_half.sem, 1)
            pool.wait_ge(weights_in.sem, 16 * 6)

            with pool.Fori(0, B) as b:
                pool.wait_ge(var_done.sem, var_done.at(b, 1))
                nc.gpsimd.tensor_tensor(rstd[:], vare[:], half[:].broadcast_to([P, TT]), ALU.pow).then_inc(rstd_done.sem, 1)
                pool.wait_ge(xn_done.sem, xn_done.at(b, 1))
                pool.wait_ge(res_done.sem, res_done.at(b, 0))
                nc.gpsimd.tensor_tensor(xb[:], xt[:], b2[:].unsqueeze(1).broadcast_to([P, TT, D]), ALU.add).then_inc(xb_done.sem, 1)

        @block.tensor
        def _(pe):
            def turn(sec, b):
                pe.wait_ge(xn_done.sem, xn_done.at(b, 1))
                for u in range(2):
                    bank = banks.claim(pe, sec, ("turn", u), b)
                    for j in range(2):
                        for t_ in range(TT):
                            k = 2 * u + j
                            last = nc.tensor.transpose(bank[:, (j * TT + t_) * P:(j * TT + t_ + 1) * P],
                                                       xn[:, t_, k * P:(k + 1) * P], ident[:])
                    last.then_inc(turn_filled.sem, 1)

            def up(sec, b):
                pe.wait_ge(ln_done.sem, ln_done.at(b, KT))
                for u in range(FT // 2):
                    bank = banks.claim(pe, sec, ("f1", u), b, late=True)
                    for j in range(2):
                        m = (2 * u + j) * P
                        for k in range(KT):
                            mm = nc.tensor.matmul(bank[:, j * S:(j + 1) * S], w1[:, k, m:m + P], lnT[:, k, :],
                                                  start=(k == 0), stop=(k == KT - 1))
                    mm.then_inc(f1_filled.sem, 1)

            def down(sec, b):
                pe.wait_ge(g_done.sem, g_done.at(b, FT))
                for t_ in range(TT):
                    bank = banks.claim(pe, sec, ("f2", t_), b, late=True)
                    for k in range(FT):
                        mm = nc.tensor.matmul(bank, gT[:, k, t_ * P:(t_ + 1) * P], w2[:, k, :],
                                              start=(k == 0), stop=(k == FT - 1))
                    mm.then_inc(f2_filled.sem, 1)

            pe.wait_ge(weights_in.sem, 16 * 6)
            turn("first", 0)
            pe.wait_ge(w2_in.sem, 16)
            with pe.Fori(0, B - 1) as i:
                up("steady", i)
                turn("steady", i + 1)
                down("steady", i)
            up("last", B - 1)
            down("last", B - 1)

        @block.scalar
        def _(act):
            def turned(sec, b):
                act.wait_ge(f1_filled.sem, f1_filled.at(b, 0))
                for k in range(KT):
                    act.wait_ge(turn_filled.sem, turn_filled.at(b, k // 2 + 1))
                    nc.scalar.activation(lnT[:, k, :], banks.bank(sec, ("turn", k // 2))[:, (k % 2) * S:(k % 2 + 1) * S],
                                         ACT.Identity, bias=shift[:, k:k + 1], scale=gain[:, k:k + 1]).then_inc(ln_done.sem, 1)

            def gelu(sec, b):
                act.wait_ge(f2_filled.sem, f2_filled.at(b, 0))
                for m in range(FT):
                    act.wait_ge(f1_filled.sem, f1_filled.at(b, m // 2 + 1))
                    nc.scalar.activation(gT[:, m, :], banks.bank(sec, ("f1", m // 2))[:, (m % 2) * S:(m % 2 + 1) * S],
                                         ACT.Gelu_apprx_tanh, bias=b1[:, m:m + 1]).then_inc(g_done.sem, 1)

            act.wait_ge(weights_in.sem, 16 * 6)
            turned("first", 0)
            with act.Fori(0, B - 1) as i:
                gelu("steady", i)
                turned("steady", i + 1)
            gelu("last", B - 1)

        @block.vector
        def _(dve):
            def normalise(b):
                dve.wait_ge(x_in.sem, x_in.at(b, 1))
                for t_ in range(TT):
                    nc.vector.bn_stats(stats[:, t_, :], xt[:, t_, :])
                nc.vector.drain()
                for t_ in range(TT):
                    last = nc.vector.bn_aggr(mv[:, t_, :], stats[:, t_, :])
                nc.vector.drain()
                nc.vector.tensor_scalar(vare[:], mv[:, :, 1], EPS, None, ALU.add).then_inc(var_done.sem, 1)
                dve.wait_ge(rstd_done.sem, rstd_done.at(b, 1))
                dve.wait_ge(turn_filled.sem, turn_filled.at(b, 0))
                for t_ in range(TT):
                    last = nc.vector.tensor_scalar(xn[:, t_, :], xt[:, t_, :], mv[:, t_, 0:1], rstd[:, t_:t_ + 1],
                                                   ALU.subtract, ALU.mult)
                last.then_inc(xn_done.sem, 1)

            def add(sec, b):
                dve.wait_ge(xb_done.sem, xb_done.at(b, 1))
                dve.wait_ge(x_out.sem, x_out.at(b, 0))
                for t_ in range(TT):
                    dve.wait_ge(f2_filled.sem, f2_filled.at(b, t_ + 1))
                    nc.vector.tensor_tensor(res[:, t_, :], banks.bank(sec, ("f2", t_)), xb[:, t_, :], ALU.add).then_inc(res_done.sem, 1)

            dve.wait_ge(weights_in.sem, 16 * 6)
            normalise(0)
            with dve.Fori(0, B - 1) as i:
                normalise(i + 1)
                add("steady", i)
            add("last", B - 1)


_L0 = ["Wq", "Wk", "Wv", "Wo", "ln_q_g", "ln_q_b", "ln_kv_g", "ln_kv_b", "ffn_ln_g", "ffn_ln_b", "W1", "b1", "W2", "b2"]
_L1 = ["ln1_s", "ln1_b", "w_qkv", "b_qkv", "w_ao", "b_ao", "ln2_s", "ln2_b", "w_q", "b_q", "w_kv", "b_kv", "w_co",
       "b_co", "ln3_s", "ln3_b", "w1", "b1", "w2", "b2"]
_IN = ["x", "ctx_2048", "mask_1x1xSxS2_fc1", "mask_Bx1xSxS2_ff1"]


def build(nc, a, out):
    x = a["x"]
    B, C, T = x.shape

    def scratch(name, shape, dt):
        return nc.dram_tensor(name, shape, dt, kind="Internal").ap()

    hid = scratch("hidden", [B, C, T], F32)
    mid = scratch("middle", [B, C, T], F32)
    with ExitStack() as sems:
        first_layer(nc, sems, x, a["ctx_2048"], a["positions"], a["identity"], {n: a["L0_xattn_" + n] for n in _L0}, hid,
                    scratch("a_q", [B, 3, C, T], BF16), scratch("a_k", [B, 3, C, T], BF16),
                    scratch("a_m", [B, 3, HEADS, T], BF16))
        W = {n: a["L1_xattn_" + n] for n in _L1}
        attention_layer(nc, sems, hid, a["ctx_2048"], (a["mask_1x1xSxS2_fc1"], a["mask_Bx1xSxS2_ff1"]), a["identity"],
                        W, mid, [[scratch(f"b_{n}{k}", [B, 2, T, C], F32) for n in "qk"] for k in range(2)])
        network_layer(nc, sems, mid, a["identity"], W, out)


def positions(c, t):
    import math
    import numpy as np
    pos = np.arange(t, dtype=np.float32)[:, None]
    div = np.exp(np.arange(0, c, 2, dtype=np.float32) * np.float32(-math.log(10000.0) / c))
    ang = pos * div
    pe = np.zeros((t, c), np.float32)
    pe[:, 0::2] = np.sin(ang)
    pe[:, 1::2] = np.cos(ang)
    return np.ascontiguousarray(pe.T)


def kernel(**inputs):
    import numpy as _np
    import concourse.bacc as _bacc
    from concourse import mybir as _mybir
    from concourse.bass_utils import run_bass_kernel_spmd as _run

    nc = _bacc.Bacc("TRN2", target_bir_lowering=False, num_devices=1)
    names = _IN + ["L0_xattn_" + n for n in _L0] + ["L1_xattn_" + n for n in _L1]
    given = {n: _np.ascontiguousarray(inputs[n]) for n in names}
    b, c, t = given["x"].shape
    given["positions"] = positions(c, t)
    given["identity"] = _np.eye(P, dtype=_np.float32)
    arrays, args = {}, {}
    for name, v in given.items():
        arrays[f"in_{name}"] = v
        args[name] = nc.dram_tensor(f"in_{name}", v.shape, _mybir.dt.from_np(v.dtype), kind="ExternalInput").ap()
    out = nc.dram_tensor("out_0", (b, c, t), F32, kind="ExternalOutput").ap()
    build(nc, args, out)
    r = _run(nc, [arrays], core_ids=[0])
    return r.results[0]["out_0"]
```

```python
from contextlib import ExitStack

import concourse.bass as bass
from concourse import mybir

F32 = mybir.dt.float32
F32R = mybir.dt.float32r
BF16 = mybir.dt.bfloat16
ALU = mybir.AluOpType
ACT = mybir.ActivationFunctionType
AX_X = mybir.AxisListType.X

P = 128
BANK = 512
EPS = 1e-5
HEADS = 16


class Signal:

    def __init__(self, ctx, nc, name, per, unit=1):
        self.sem = ctx.enter_context(nc.semaphore(name))
        self.per = per
        self.unit = unit

    def at(self, b, n):
        return b * (self.per * self.unit) + n * self.unit


class Banks:

    def __init__(self, ctx, nc, name, n, read, **order):
        self.n = n
        self.tile = ctx.enter_context(nc.psum_tensor(name, [P, n, BANK], F32))
        self.read = read
        self.order = order

    def bank(self, section, use):
        return self.tile[:, self.order[section].index(use) % self.n, :]

    def claim(self, eng, section, use, b, late=False):
        at = self.order[section].index(use)
        if late and section == "steady":
            b = b + 1
        if at >= self.n:
            signal, n, is_late = self.read[self.order[section][at - self.n]]
            batch = b - 1 if is_late and section == "steady" else b
            eng.wait_ge(signal.sem, signal.at(batch, n))
        elif section != "first":
            k = at % self.n
            batch = b - 1 if section == "steady" else b
            if section == "steady":
                for i, u in list(enumerate(self.order["first"]))[::-1]:
                    if i % self.n == k:
                        signal, n, _ = self.read[u]
                        eng.wait_ge(signal.sem, signal.at(0, n))
                        break
            signal, n, is_late = [self.read[u] for i, u in enumerate(self.order["steady"]) if i % self.n == k][-1]
            eng.wait_ge(signal.sem, signal.at(batch, 0 if is_late else n))
        return self.bank(section, use)


def rowwise(v, tiles):
    return v.rearrange("(t p) -> p t", t=tiles)


def first_layer(nc, sems, x, ctx_in, pos, ident_in, W, hid, scratch_q, scratch_k, scratch_m):
    B, C, T = x.shape
    CT = C // P
    TT = T // P
    DH = C // HEADS
    F = W["W1"].shape[1]
    FT = F // P
    SCALE = float(DH) ** -0.5
    GROUP = P // 32
    NG = HEADS // GROUP
    RING = GROUP + 1
    Q_PARTS = (0, 0, 1, 1, 0, 2)
    K_PARTS = (0, 1, 0, 1, 2, 0)
    ROWS = len(Q_PARTS) * DH
    ROWS_M = ROWS + 3

    with ExitStack() as ctx:
        def sb(name, shape, dt=F32):
            return ctx.enter_context(nc.sbuf_tensor("a_" + name, shape, dt))

        def sig(name, per, unit=1):
            return Signal(sems, nc, "a_" + name, per, unit)

        wq, wk, wv, wo = (sb(n, [P, CT, C]) for n in ("wq", "wk", "wv", "wo"))
        w1 = sb("w1", [P, CT, F])
        w2 = sb("w2", [P, FT, C])
        gains = sb("gains", [P, 3, CT])
        shifts = sb("shifts", [P, 3, CT])
        b1 = sb("b1", [P, FT])
        b2 = sb("b2", [P, CT])
        ident = sb("ident", [P, P])
        half = sb("half", [P, 1])
        pe = sb("pe", [P, CT, T])
        xin = [sb(f"xin{s}", [P, CT, T]) for s in range(2)]
        tokn = [sb(f"tokn{s}", [P, TT, C]) for s in range(3)]
        stats = sb("stats", [P, 3, TT, 6])
        mv = sb("mv", [P, 3, TT, 2])
        vare = sb("vare", [P, 3, TT])
        rstd = sb("rstd", [P, 3, TT])
        qnT = sb("qnT", [P, CT, T])
        kvnT = sb("kvnT", [P, CT, T])
        rest = sb("rest", [P, CT, T])
        qparts = sb("qparts", [P, 3, CT, T], BF16)
        kparts = sb("kparts", [P, 3, CT, T], BF16)
        qst = sb("qst", [P, HEADS, T], BF16)
        kst = sb("kst", [P, HEADS, T], BF16)
        vaug = sb("vaug", [P, TT, HEADS, 32])
        mx = sb("mx", [P, TT, HEADS])
        mrest = sb("mrest", [HEADS, T])
        mparts = sb("mparts", [HEADS, 3, T], BF16)
        pt = sb("pt", [P, RING, TT, T])
        ctxr = sb("ctxr", [P, 2, T])
        rsum = sb("rsum", [P, NG, TT, GROUP])
        ctxt = sb("ctxt", [P, TT, C])
        ctxT = sb("ctxT", [P, CT, T])
        rT = sb("rT", [P, CT, T])
        hT = sb("hT", [P, CT, T])
        gT = sb("gT", [P, FT, T])
        outT = sb("outT", [P, CT, T])

        kinds = {}

        def filled(name, per):
            kinds[name] = sig(name + "_filled", per)
            return kinds[name]

        weights_in = sig("weights_in", 1, 16)
        consts = sig("consts", 1)
        half_set = sig("half_set", 1)
        x_in = [sig(f"x_in{s}", 1, 16) for s in range(2)]
        x_pe = [sig(f"x_pe{s}", 1) for s in range(2)]
        tok_filled = [sig(f"tok_filled{s}", 2) for s in range(3)]
        var_done = [sig(f"var_done{s}", 1) for s in range(3)]
        rstd_done = [sig(f"rstd_done{s}", 1) for s in range(3)]
        tok_done = [sig(f"tok_done{s}", 2) for s in range(3)]
        chan_filled = [sig(f"chan_filled{s}", CT) for s in range(3)]
        chan_done = [sig(f"chan_done{s}", CT) for s in range(3)]
        qk_filled = sig("qk_filled", 2 * CT)
        high = sig("high", 2 * CT)
        restd = sig("restd", 2 * CT)
        mid = sig("mid", 2 * CT)
        low = sig("low", 2 * CT)
        parts_out = [sig(f"parts_out{s}", 3, 16) for s in range(2)]
        stacked = sig("stacked", 2 * len(Q_PARTS), 16)
        v_filled = sig("v_filled", 2)
        v_done = sig("v_done", 2)
        score_filled = sig("score_filled", 4 * HEADS)
        max_done = sig("max_done", 2 * HEADS)
        m_filled = sig("m_filled", 1)
        m_high = sig("m_high", 1)
        m_rest = sig("m_rest", 1)
        m_mid = sig("m_mid", 1)
        m_low = sig("m_low", 1)
        m_out = sig("m_out", 1, 16)
        m_in = sig("m_in", 1, 16)
        exp_done = sig("exp_done", 2 * HEADS)
        pv_done = sig("pv_done", NG)
        ctx_raw = sig("ctx_raw", NG)
        ctx_filled = sig("ctx_filled", NG)
        ctx_sum = sig("ctx_sum", NG)
        ctx_tok = sig("ctx_tok", NG)
        ctxT_filled = sig("ctxT_filled", CT)
        ctx_chan = sig("ctx_chan", CT)
        y_filled = sig("y_filled", CT)
        r_done = sig("r_done", CT)
        f1_filled = sig("f1_filled", FT)
        g_done = sig("g_done", FT)
        f2_filled = sig("f2_filled", CT)
        o_done = sig("o_done", CT)
        o_out = sig("o_out", 1, 16)

        front = [("tok", s, u) for s in range(2) for u in range(2)]
        front2 = [("chan", s, c) for s in range(2) for c in range(CT)]
        front2 += [(n, m) for n in "qk" for m in range(CT)] + [("v", u) for u in range(2)]
        attn = [("m",)] + [("ctx", g) for g in range(NG - 1)]
        tail1 = [("ctx", NG - 1)] + [("ctxT", c) for c in range(CT)] + [("y", m) for m in range(CT)]
        tail2 = [("tok", 2, u) for u in range(2)] + [("chan", 2, c) for c in range(CT)]
        tail3 = [("f1", m) for m in range(FT)] + [("f2", m) for m in range(CT)]
        late = tail1 + tail2 + tail3
        read = {("m",): (m_rest, 1)}
        read |= {("tok", s, u): (tok_done[s], u + 1) for s in range(3) for u in range(2)}
        read |= {("chan", s, c): (chan_done[s], c + 1) for s in range(3) for c in range(CT)}
        read |= {(n, m): (restd, "qk".index(n) * CT + m + 1) for n in "qk" for m in range(CT)}
        read |= {("v", u): (v_done, u + 1) for u in range(2)}
        read |= {("ctx", g): (ctx_tok, g + 1) for g in range(NG)}
        read |= {("ctxT", c): (ctx_chan, c + 1) for c in range(CT)}
        read |= {("y", m): (r_done, m + 1) for m in range(CT)}
        read |= {("f1", m): (g_done, m + 1) for m in range(FT)}
        read |= {("f2", m): (o_done, m + 1) for m in range(CT)}
        read = {u: (*r, u in late) for u, r in read.items()}
        banks = Banks(ctx, nc, "a_d", 3, read, first=front + front2 + attn,
                      steady=front + tail1 + front2 + tail2 + tail3 + attn, last=late)
        score = ctx.enter_context(nc.psum_tensor("a_score", [P, 2, 2, BANK], F32))
        ctxp = ctx.enter_context(nc.psum_tensor("a_ctxp", [P, BANK], F32))
        WEIGHTS = 16

        block = ctx.enter_context(nc.Block())

        @block.sync
        def _(sp):
            def load(dst, src, columns=False):
                sp.dma_start(dst, src, allow_slow_non_contiguous=columns).then_inc(weights_in.sem, 16)

            for s, src in enumerate((x, ctx_in)):
                sp.dma_start(xin[s][:], src[0].rearrange("(c p) t -> p c t", p=P)).then_inc(x_in[s].sem, 16)
            load(pe[:], pos.rearrange("(c p) t -> p c t", p=P))
            load(ident[:], ident_in)
            for i, n in enumerate(("ln_q", "ln_kv", "ffn_ln")):
                load(gains[:, i, :], rowwise(W[n + "_g"], CT), True)
                load(shifts[:, i, :], rowwise(W[n + "_b"], CT), True)
            for dst, n in ((wq, "Wq"), (wk, "Wk"), (wv, "Wv"), (wo, "Wo"), (w1, "W1"), (w2, "W2")):
                load(dst[:], W[n].rearrange("(k p) n -> p k n", p=P))
            load(b1[:], rowwise(W["b1"], FT), True)
            load(b2[:], rowwise(W["b2"], CT), True)

            def steps(b, fetch):
                if fetch:
                    for s, src in enumerate((x, ctx_in)):
                        sp.wait_ge(tok_filled[s].sem, tok_filled[s].at(b, 2))
                        sp.dma_start(xin[s][:], src[b + 1].rearrange("(c p) t -> p c t", p=P)).then_inc(x_in[s].sem, 16)
                for s, (parts, scr) in enumerate(((qparts, scratch_q), (kparts, scratch_k))):
                    sp.wait_ge(low.sem, low.at(b, (s + 1) * CT))
                    for part in range(3):
                        sp.dma_start(scr[b, part].rearrange("(c p) n -> p c n", p=P), parts[:, part]).then_inc(parts_out[s].sem, 16)
                sp.wait_ge(score_filled.sem, score_filled.at(b, 0))
                for s, (st, scr, order) in enumerate(((qst, scratch_q, Q_PARTS), (kst, scratch_k, K_PARTS))):
                    sp.wait_ge(parts_out[s].sem, parts_out[s].at(b, 3))
                    for c, part in enumerate(order):
                        sp.dma_start(st[c * DH:(c + 1) * DH, :, :],
                                     scr[b, part].rearrange("(h d) n -> d h n", d=DH)).then_inc(stacked.sem, 16)

            def maxima(b):
                sp.wait_ge(m_low.sem, m_low.at(b, 1))
                sp.dma_start(scratch_m[b].rearrange("t h n -> h t n"), mparts[:]).then_inc(m_out.sem, 16)
                sp.wait_ge(m_out.sem, m_out.at(b, 1))
                sp.dma_start(qst[ROWS:ROWS_M, :, :], scratch_m[b]).then_inc(m_in.sem, 16)

            def store(b):
                sp.wait_ge(o_done.sem, o_done.at(b, CT))
                sp.dma_start(hid[b].rearrange("(c p) t -> p c t", p=P), outT[:]).then_inc(o_out.sem, 16)

            steps(0, True)
            maxima(0)
            with sp.Fori(0, B - 2) as i:
                steps(i + 1, True)
                store(i)
                maxima(i + 1)
            steps(B - 1, False)
            store(B - 2)
            maxima(B - 1)
            store(B - 1)
            sp.wait_ge(o_out.sem, o_out.at(B, 0))

        @block.gpsimd
        def _(pool):
            nc.gpsimd.memset(half[:], -0.5).then_inc(half_set.sem, 1)
            pool.wait_ge(half_set.sem, 1)
            pool.wait_ge(weights_in.sem, 16 * WEIGHTS)

            def add_positions(b):
                for s in range(2):
                    pool.wait_ge(x_in[s].sem, x_in[s].at(b, 1))
                    nc.gpsimd.tensor_tensor(xin[s][:], xin[s][:], pe[:], ALU.add).then_inc(x_pe[s].sem, 1)

            def rsqrt(b, s):
                pool.wait_ge(var_done[s].sem, var_done[s].at(b, 1))
                nc.gpsimd.tensor_tensor(rstd[:, s, :], vare[:, s, :], half[:].broadcast_to([P, TT]),
                                        ALU.pow).then_inc(rstd_done[s].sem, 1)

            def low_parts(b):
                for s, parts in enumerate((qparts, kparts)):
                    for m in range(CT):
                        pool.wait_ge(mid.sem, mid.at(b, s * CT + m + 1))
                        nc.gpsimd.tensor_tensor(parts[:, 2, m, :], rest[:, m, :], parts[:, 1, m, :],
                                                ALU.subtract).then_inc(low.sem, 1)

            def front(b):
                add_positions(b)
                rsqrt(b, 0)
                rsqrt(b, 1)
                low_parts(b)

            front(0)
            with pool.Fori(0, B - 1) as i:
                front(i + 1)
                rsqrt(i, 2)
            rsqrt(B - 1, 2)

        @block.tensor
        def _(pe_):
            def turn_to_tokens(sec, b, s, src):
                for u in range(2):
                    bank = banks.claim(pe_, sec, ("tok", s, u), b, late=(s == 2))
                    for t in range(2):
                        for c in range(CT):
                            at = (2 * u + t) * P
                            last = nc.tensor.transpose(bank[:, (t * CT + c) * P:(t * CT + c + 1) * P],
                                                       src[:, c, at:at + P], ident[:])
                    last.then_inc(tok_filled[s].sem, 1)

            def turn_to_channels(sec, b, s, src):
                pe_.wait_ge(tok_done[s].sem, tok_done[s].at(b, 2))
                for c in range(CT):
                    bank = banks.claim(pe_, sec, ("chan", s, c), b, late=(s == 2))
                    for t in range(TT):
                        last = nc.tensor.transpose(bank[:, t * P:(t + 1) * P], src[:, t, c * P:(c + 1) * P], ident[:])
                    last.then_inc(chan_filled[s].sem, 1)

            def front_a(sec, b):
                for s in range(2):
                    pe_.wait_ge(x_pe[s].sem, x_pe[s].at(b, 1))
                    turn_to_tokens(sec, b, s, xin[s])

            def front_b(sec, b):
                turn_to_channels(sec, b, 0, tokn[0])
                turn_to_channels(sec, b, 1, tokn[1])
                for s, (name, w, src) in enumerate((("q", wq, qnT), ("k", wk, kvnT))):
                    pe_.wait_ge(chan_done[s].sem, chan_done[s].at(b, CT))
                    for m in range(CT):
                        bank = banks.claim(pe_, sec, (name, m), b)
                        for k in range(CT):
                            mm = nc.tensor.matmul(bank, w[:, k, m * P:(m + 1) * P], src[:, k, :],
                                                  start=(k == 0), stop=(k == CT - 1))
                        mm.then_inc(qk_filled.sem, 1)
                for u in range(2):
                    bank = banks.claim(pe_, sec, ("v", u), b)
                    for t in range(2):
                        at = (2 * u + t) * P
                        for k in range(CT):
                            mm = nc.tensor.matmul(bank[:, t * C:(t + 1) * C], kvnT[:, k, at:at + P], wv[:, k, :],
                                                  start=(k == 0), stop=(k == CT - 1))
                    mm.then_inc(v_filled.sem, 1)

            def row_maxima(b, h):
                if h == 0:
                    pe_.wait_ge(stacked.sem, stacked.at(b, 2 * len(Q_PARTS)))
                for p in range(2):
                    if h == 0:
                        pe_.wait_ge(exp_done.sem, exp_done.at(b, 0))
                    else:
                        pe_.wait_ge(max_done.sem, max_done.at(b, 2 * h + p - 1))
                    for j in range(2):
                        q = (2 * p + j) * P
                        mm = nc.tensor.matmul(score[:, p, j, :], qst[0:ROWS, h, q:q + P], kst[0:ROWS, h, :],
                                              start=True, stop=True)
                    mm.then_inc(score_filled.sem, 1)

            def turn_maxima(sec, b):
                pe_.wait_ge(max_done.sem, max_done.at(b, 2 * HEADS))
                bank = banks.claim(pe_, sec, ("m",), b)
                for t in range(TT):
                    last = nc.tensor.transpose(bank[0:HEADS, t * P:(t + 1) * P], mx[:, t, :], ident[:])
                last.then_inc(m_filled.sem, 1)

            def shifted_scores(b, h):
                if h == 0:
                    pe_.wait_ge(m_in.sem, m_in.at(b, 1))
                for p in range(2):
                    if h:
                        pe_.wait_ge(exp_done.sem, exp_done.at(b, 2 * h + p - 1))
                    for j in range(2):
                        k = (2 * p + j) * P
                        mm = nc.tensor.matmul(score[:, p, j, :], kst[0:ROWS_M, h, k:k + P], qst[0:ROWS_M, h, :],
                                              start=True, stop=True)
                    mm.then_inc(score_filled.sem, 1)

            def weigh_values(b, g):
                pe_.wait_ge(exp_done.sem, exp_done.at(b, 2 * GROUP * (g + 1)))
                if g == 0:
                    pe_.wait_ge(v_done.sem, v_done.at(b, 2))
                pe_.wait_ge(ctx_raw.sem, ctx_raw.at(b, g))
                for k in range(TT):
                    for j in range(GROUP):
                        h = GROUP * g + j
                        mm = nc.tensor.matmul(ctxp[32 * j:32 * j + 32, :], vaug[:, k, h, :], pt[:, h % RING, k, :],
                                              start=(k == 0), stop=(k == TT - 1), tile_position=(0, 32 * j))
                mm.then_inc(pv_done.sem, 1)

            def turn_context(sec, b, g):
                pe_.wait_ge(ctx_raw.sem, ctx_raw.at(b, g + 1))
                bank = banks.claim(pe_, sec, ("ctx", g), b, late=(g == NG - 1))
                for t in range(TT):
                    last = nc.tensor.transpose(bank[:, t * P:(t + 1) * P], ctxr[:, g % 2, t * P:(t + 1) * P], ident[:])
                last.then_inc(ctx_filled.sem, 1)

            def attention(sec, b):
                turn_maxima(sec, b)
                for h in range(HEADS):
                    shifted_scores(b, h)
                    if h % GROUP == 0 and h:
                        weigh_values(b, h // GROUP - 1)
                    if h % GROUP == 1 and h > 1:
                        turn_context(sec, b, h // GROUP - 1)
                weigh_values(b, NG - 1)

            def tail_a(sec, b):
                turn_context(sec, b, NG - 1)
                pe_.wait_ge(ctx_tok.sem, ctx_tok.at(b, NG))
                for c in range(CT):
                    bank = banks.claim(pe_, sec, ("ctxT", c), b, late=True)
                    for t in range(TT):
                        last = nc.tensor.transpose(bank[:, t * P:(t + 1) * P], ctxt[:, t, c * P:(c + 1) * P], ident[:])
                    last.then_inc(ctxT_filled.sem, 1)
                pe_.wait_ge(ctx_chan.sem, ctx_chan.at(b, CT))
                for m in range(CT):
                    bank = banks.claim(pe_, sec, ("y", m), b, late=True)
                    for k in range(CT):
                        mm = nc.tensor.matmul(bank, wo[:, k, m * P:(m + 1) * P], ctxT[:, k, :],
                                              start=(k == 0), stop=(k == CT - 1))
                    mm.then_inc(y_filled.sem, 1)

            def tail_b(sec, b):
                pe_.wait_ge(r_done.sem, r_done.at(b, CT))
                turn_to_tokens(sec, b, 2, rT)
                turn_to_channels(sec, b, 2, tokn[2])

            def tail_c(sec, b, m):
                if m < FT:
                    if m == 0:
                        pe_.wait_ge(chan_done[2].sem, chan_done[2].at(b, CT))
                    bank = banks.claim(pe_, sec, ("f1", m), b, late=True)
                    for k in range(CT):
                        mm = nc.tensor.matmul(bank, w1[:, k, m * P:(m + 1) * P], hT[:, k, :],
                                              start=(k == 0), stop=(k == CT - 1))
                    mm.then_inc(f1_filled.sem, 1)
                else:
                    m -= FT
                    if m == 0:
                        pe_.wait_ge(g_done.sem, g_done.at(b, FT))
                    bank = banks.claim(pe_, sec, ("f2", m), b, late=True)
                    for k in range(FT):
                        mm = nc.tensor.matmul(bank, w2[:, k, m * P:(m + 1) * P], gT[:, k, :],
                                              start=(k == 0), stop=(k == FT - 1))
                    mm.then_inc(f2_filled.sem, 1)

            pe_.wait_ge(weights_in.sem, 16 * WEIGHTS)
            pe_.wait_ge(consts.sem, 2)
            front_a("first", 0)
            front_b("first", 0)
            for h in range(HEADS):
                row_maxima(0, h)
            attention("first", 0)
            with pe_.Fori(0, B - 1) as i:
                front_a("steady", i + 1)
                tail_a("steady", i)
                front_b("steady", i + 1)
                tail_b("steady", i)
                for h in range(HEADS):
                    row_maxima(i + 1, h)
                    if h % 2 == 1 and h // 2 < FT + CT:
                        tail_c("steady", i, h // 2)
                attention("steady", i + 1)
            tail_a("last", B - 1)
            tail_b("last", B - 1)
            for m in range(FT + CT):
                tail_c("last", B - 1, m)

        @block.scalar
        def _(act):
            def to_channels(sec, b, s, dst):
                for c in range(CT):
                    act.wait_ge(chan_filled[s].sem, chan_filled[s].at(b, c + 1))
                    nc.scalar.activation(dst[:, c, :], banks.bank(sec, ("chan", s, c)), ACT.Identity,
                                         bias=shifts[:, s, c:c + 1], scale=gains[:, s, c:c + 1]).then_inc(chan_done[s].sem, 1)

            def front_b(sec, b):
                act.wait_ge(r_done.sem, r_done.at(b, 0))
                to_channels(sec, b, 0, qnT)
                act.wait_ge(v_filled.sem, v_filled.at(b, 0))
                to_channels(sec, b, 1, kvnT)
                for s, (name, parts) in enumerate((("q", qparts), ("k", kparts))):
                    act.wait_ge(parts_out[s].sem, parts_out[s].at(b, 0))
                    for m in range(CT):
                        act.wait_ge(qk_filled.sem, qk_filled.at(b, s * CT + m + 1))
                        nc.scalar.activation(parts[:, 0, m, :], banks.bank(sec, (name, m)), ACT.Copy).then_inc(high.sem, 1)
                    for m in range(CT):
                        act.wait_ge(restd.sem, restd.at(b, s * CT + m + 1))
                        nc.scalar.activation(parts[:, 1, m, :], rest[:, m, :], ACT.Copy).then_inc(mid.sem, 1)
                act.wait_ge(pv_done.sem, pv_done.at(b, 0))
                for u in range(2):
                    act.wait_ge(v_filled.sem, v_filled.at(b, u + 1))
                    nc.scalar.activation(vaug[:, 2 * u:2 * u + 2, :, 0:DH],
                                         banks.bank(sec, ("v", u)).rearrange("p (t h d) -> p t h d", t=2, d=DH),
                                         ACT.Copy).then_inc(v_done.sem, 1)

            def attention(sec, b):
                act.wait_ge(m_filled.sem, m_filled.at(b, 1))
                act.wait_ge(m_out.sem, m_out.at(b, 0))
                nc.scalar.activation(mparts[:, 0, :], banks.bank(sec, ("m",))[0:HEADS, :], ACT.Copy,
                                     scale=-1.0).then_inc(m_high.sem, 1)
                for h in range(HEADS):
                    act.wait_ge(pv_done.sem, pv_done.at(b, 0 if h < RING else (h - RING) // GROUP + 1))
                    for p in range(2):
                        act.wait_ge(score_filled.sem, score_filled.at(b, 2 * HEADS + 2 * h + p + 1))
                        nc.scalar.activation(pt[:, h % RING, 2 * p:2 * p + 2, :], score[:, p, :, :], ACT.Exp,
                                             scale=SCALE).then_inc(exp_done.sem, 1)

            def tail_a(sec, b):
                act.wait_ge(y_filled.sem, y_filled.at(b, 0))
                for c in range(CT):
                    act.wait_ge(ctxT_filled.sem, ctxT_filled.at(b, c + 1))
                    nc.scalar.activation(ctxT[:, c, :], banks.bank(sec, ("ctxT", c)), ACT.Copy).then_inc(ctx_chan.sem, 1)

            def tail_b(sec, b):
                act.wait_ge(f1_filled.sem, f1_filled.at(b, 0))
                to_channels(sec, b, 2, hT)

            def tail_c(sec, b):
                act.wait_ge(f2_filled.sem, f2_filled.at(b, 0))
                for m in range(FT):
                    act.wait_ge(f1_filled.sem, f1_filled.at(b, m + 1))
                    nc.scalar.activation(gT[:, m, :], banks.bank(sec, ("f1", m)), ACT.Gelu,
                                         bias=b1[:, m:m + 1]).then_inc(g_done.sem, 1)

            act.wait_ge(weights_in.sem, 16 * WEIGHTS)
            act.wait_ge(consts.sem, 2)
            front_b("first", 0)
            attention("first", 0)
            with act.Fori(0, B - 1) as i:
                tail_a("steady", i)
                front_b("steady", i + 1)
                tail_b("steady", i)
                tail_c("steady", i)
                attention("steady", i + 1)
            tail_a("last", B - 1)
            tail_b("last", B - 1)
            tail_c("last", B - 1)

        @block.vector
        def _(dve):
            def normalise(sec, b, s):
                for u in range(2):
                    dve.wait_ge(tok_filled[s].sem, tok_filled[s].at(b, u + 1))
                    bank = banks.bank(sec, ("tok", s, u))
                    for t in range(2):
                        nc.vector.bn_stats(stats[:, s, 2 * u + t, :], bank[:, t * C:(t + 1) * C])
                nc.vector.drain()
                for t in range(TT):
                    last = nc.vector.bn_aggr(mv[:, s, t, :], stats[:, s, t, :])
                nc.vector.drain()
                nc.vector.tensor_scalar(vare[:, s, :], mv[:, s, :, 1], EPS, None, ALU.add).then_inc(var_done[s].sem, 1)

            def apply(sec, b, s):
                dve.wait_ge(rstd_done[s].sem, rstd_done[s].at(b, 1))
                dve.wait_ge(chan_filled[s].sem, chan_filled[s].at(b, 0))
                for u in range(2):
                    bank = banks.bank(sec, ("tok", s, u))
                    for t in range(2):
                        tt = 2 * u + t
                        last = nc.vector.tensor_scalar(tokn[s][:, tt, :], bank[:, t * C:(t + 1) * C], mv[:, s, tt, 0:1],
                                                       rstd[:, s, tt:tt + 1], ALU.subtract, ALU.mult)
                    last.then_inc(tok_done[s].sem, 1)

            def front_a(sec, b):
                normalise(sec, b, 0)
                apply(sec, b, 0)
                normalise(sec, b, 1)
                apply(sec, b, 1)

            def front_b(sec, b):
                for s, (name, parts) in enumerate((("q", qparts), ("k", kparts))):
                    for m in range(CT):
                        dve.wait_ge(low.sem, low.at(b, 0 if s == 0 else m + 1))
                        dve.wait_ge(high.sem, high.at(b, s * CT + m + 1))
                        nc.vector.tensor_tensor(rest[:, m, :], banks.bank(sec, (name, m)), parts[:, 0, m, :],
                                                ALU.subtract).then_inc(restd.sem, 1)

            def row_maximum(b, h):
                if h == 0:
                    dve.wait_ge(m_filled.sem, m_filled.at(b, 0))
                for p in range(2):
                    dve.wait_ge(score_filled.sem, score_filled.at(b, 2 * h + p + 1))
                    nc.vector.tensor_reduce(mx[:, 2 * p:2 * p + 2, h], score[:, p, :, :], AX_X, ALU.max).then_inc(max_done.sem, 1)

            def divide_context(sec, b, g):
                dve.wait_ge(ctx_filled.sem, ctx_filled.at(b, g + 1))
                bank = banks.bank(sec, ("ctx", g)).rearrange("p (t j c) -> p t j c", t=TT, c=32)
                nc.vector.reciprocal(rsum[:, g, :, :], bank[:, :, :, DH]).then_inc(ctx_sum.sem, 1)
                dve.wait_ge(ctx_sum.sem, ctx_sum.at(b, g + 1))
                if g == 0:
                    dve.wait_ge(ctxT_filled.sem, ctxT_filled.at(b, 0))
                out = ctxt[:, :, g * GROUP * DH:(g + 1) * GROUP * DH].rearrange("p t (j d) -> p t j d", d=DH)
                nc.vector.tensor_tensor(out, bank[:, :, :, 0:DH],
                                        rsum[:, g, :, :].unsqueeze(3).broadcast_to([P, TT, GROUP, DH]),
                                        ALU.mult).then_inc(ctx_tok.sem, 1)

            def attention(sec, b):
                dve.wait_ge(m_high.sem, m_high.at(b, 1))
                nc.vector.scalar_tensor_tensor(mrest[:], banks.bank(sec, ("m",))[0:HEADS, :], -1.0, mparts[:, 0, :],
                                               ALU.mult, ALU.subtract).then_inc(m_rest.sem, 1)
                dve.wait_ge(m_rest.sem, m_rest.at(b, 1))
                nc.vector.tensor_copy(mparts[:, 1, :], mrest[:]).then_inc(m_mid.sem, 1)
                dve.wait_ge(m_mid.sem, m_mid.at(b, 1))
                nc.vector.tensor_tensor(mparts[:, 2, :], mrest[:], mparts[:, 1, :], ALU.subtract).then_inc(m_low.sem, 1)
                for g in range(NG):
                    dve.wait_ge(pv_done.sem, pv_done.at(b, g + 1))
                    dve.wait_ge(ctx_filled.sem, ctx_filled.at(b, max(g - 1, 0)))
                    nc.vector.tensor_copy(ctxr[:, g % 2, :], ctxp[:]).then_inc(ctx_raw.sem, 1)
                    if g < NG - 1:
                        divide_context(sec, b, g)

            def tail_a(sec, b):
                divide_context(sec, b, NG - 1)
                for m in range(CT):
                    dve.wait_ge(y_filled.sem, y_filled.at(b, m + 1))
                    if m == 0:
                        dve.wait_ge(o_done.sem, o_done.at(b, 0))
                    nc.vector.tensor_tensor(rT[:, m, :], banks.bank(sec, ("y", m)), qnT[:, m, :], ALU.add).then_inc(r_done.sem, 1)

            def tail_b(sec, b):
                normalise(sec, b, 2)
                apply(sec, b, 2)

            def tail_c(sec, b, m):
                dve.wait_ge(f2_filled.sem, f2_filled.at(b, m + 1))
                if m == 0:
                    dve.wait_ge(o_out.sem, o_out.at(b, 0))
                nc.vector.scalar_tensor_tensor(outT[:, m, :], banks.bank(sec, ("f2", m)), b2[:, m:m + 1], rT[:, m, :],
                                               ALU.add, ALU.add).then_inc(o_done.sem, 1)

            nc.vector.memset(kst[ROWS:ROWS_M, :, :], 1.0)
            nc.vector.memset(vaug[:], 0.0).then_inc(consts.sem, 1)
            dve.wait_ge(consts.sem, 1)
            nc.vector.memset(vaug[:, :, :, DH:DH + 1], 1.0).then_inc(consts.sem, 1)
            dve.wait_ge(weights_in.sem, 16 * WEIGHTS)
            front_a("first", 0)
            front_b("first", 0)
            for h in range(HEADS):
                row_maximum(0, h)
            attention("first", 0)
            with dve.Fori(0, B - 1) as i:
                front_a("steady", i + 1)
                tail_a("steady", i)
                front_b("steady", i + 1)
                tail_b("steady", i)
                for h in range(HEADS):
                    row_maximum(i + 1, h)
                    if h in (HEADS - 4, HEADS - 2):
                        tail_c("steady", i, (h - HEADS + 4) // 2)
                attention("steady", i + 1)
            tail_a("last", B - 1)
            tail_b("last", B - 1)
            for m in range(CT):
                tail_c("last", B - 1, m)


def attention_layer(nc, sems, hid, enc_in, masks, ident_in, W, mid_out, scratch):
    B, S, D = hid.shape
    KT = D // P
    TT = S // P
    DH = D // HEADS
    SCALE = float(DH) ** -0.5
    MASKED = 10000.0
    HUGE = 3.0e38
    Q_PARTS = (0, 0, 1)
    K_PARTS = (0, 1, 0)
    ROWS = len(Q_PARTS) * DH
    HH = HEADS // 2
    G = 4
    NU = HEADS // G * TT
    SELF, CROSS = 0, 1

    def unit(u):
        half, rest = divmod(u, NU // 2)
        tile, four = divmod(rest, HH // G)
        return half, tile, four

    with ExitStack() as ctx:
        def sb(name, shape, dt=F32):
            return ctx.enter_context(nc.sbuf_tensor("b_" + name, shape, dt))

        def sig(name, per, unit=1):
            return Signal(sems, nc, "b_" + name, per, unit)

        wqkv = sb("wqkv", [P, KT, 3 * D])
        wkv = sb("wkv", [P, KT, 2 * D])
        wq2 = sb("wq2", [P, KT, D])
        wout = [sb(f"wout{a}", [P, KT, D]) for a in range(2)]
        gains = sb("gains", [P, 2, KT])
        shifts = sb("shifts", [P, 2, KT])
        bqkv = sb("bqkv", [P, 3 * KT])
        bq2 = sb("bq2", [P, KT])
        bkv = sb("bkv", [P, 2 * KT])
        bqs = sb("bqs", [P, 2, KT])
        bout = [sb(f"bout{a}", [P, D]) for a in range(2)]
        ident = sb("ident", [P, P])
        half = sb("half", [P, 1])
        mask = [sb(f"mask{a}", [P, TT, S]) for a in range(2)]
        minus = [sb(f"minus{a}", [P, TT, S]) for a in range(2)]
        xt = sb("xt", [P, TT, D])
        x1 = sb("x1", [P, TT, D])
        xn = sb("xn", [P, TT, D])
        enc = sb("enc", [P, TT, D])
        lnT = sb("lnT", [P, KT, S])
        encT = sb("encT", [P, KT, S])
        stats = sb("stats", [P, 2, TT, 6])
        mv = sb("mv", [P, 2, TT, 2])
        vare = sb("vare", [P, 2, TT])
        rstd = sb("rstd", [P, 2, TT])
        full = sb("full", [P, KT, S])
        parts = sb("parts", [P, 2, KT, S], F32R)
        qst = sb("qst", [ROWS, 2, HH, S], F32R)
        kst = sb("kst", [ROWS, 2, HH, S], F32R)
        val = [sb(f"val{a}", [P, TT, D]) for a in range(2)]
        t = sb("t", [P, 2, G, S])
        nmax = sb("nmax", [P, NU, G])
        pr = sb("pr", [P, 3, G, S])
        esum = sb("esum", [P, NU, G])
        inverse = sb("inverse", [P, NU, G])
        spread = sb("spread", [P, 2, P])
        pt = sb("pt", [P, 2, TT, G * P])
        cxT = sb("cxT", [P, KT, S])

        weights_in = sig("weights_in", 1, 16)
        x_in = sig("x_in", 1, 16)
        enc_load = sig("enc_load", 1, 16)
        mask_in = sig("mask_in", 1, 16)
        set_up = sig("set_up", 1)
        minus_half = sig("minus_half", 1)
        minus_done = sig("minus_done", 1)
        x_biased = [sig(f"x_biased{a}", 1) for a in range(2)]
        var_done = [sig(f"var_done{a}", 1) for a in range(2)]
        rstd_done = [sig(f"rstd_done{a}", 1) for a in range(2)]
        xn_done = [sig(f"xn_done{a}", 1) for a in range(2)]
        turn_filled = [sig(f"turn_filled{a}", 2) for a in range(2)]
        ln_done = [sig(f"ln_done{a}", KT) for a in range(2)]
        enc_filled = sig("enc_filled", 2)
        enc_done = sig("enc_done", 2)
        q_filled = [sig(f"q_filled{a}", 2) for a in range(2)]
        k_filled = [sig(f"k_filled{a}", 2) for a in range(2)]
        v_filled = [sig(f"v_filled{a}", TT) for a in range(2)]
        q_full = [sig(f"q_full{a}", KT) for a in range(2)]
        k_full = [sig(f"k_full{a}", KT) for a in range(2)]
        v_done = [sig(f"v_done{a}", TT) for a in range(2)]
        q_parts = [sig(f"q_parts{a}", 1) for a in range(2)]
        k_parts = [sig(f"k_parts{a}", 1) for a in range(2)]
        q_out = [[sig(f"q_out{a}{h}", 2, 16) for h in range(2)] for a in range(2)]
        k_out = [[sig(f"k_out{a}{h}", 2, 16) for h in range(2)] for a in range(2)]
        stacked = [[sig(f"stacked{a}{h}", 2 * len(Q_PARTS), 16) for h in range(2)] for a in range(2)]
        score_filled = [sig(f"score_filled{a}", NU) for a in range(2)]
        masked = [sig(f"masked{a}", NU) for a in range(2)]
        max_done = [sig(f"max_done{a}", NU) for a in range(2)]
        exp_done = [sig(f"exp_done{a}", NU) for a in range(2)]
        pt_filled = [sig(f"pt_filled{a}", NU * TT) for a in range(2)]
        pt_done = [sig(f"pt_done{a}", NU * TT) for a in range(2)]
        pv_done = [sig(f"pv_done{a}", NU) for a in range(2)]
        inverse_done = [sig(f"inverse_done{a}", NU) for a in range(2)]
        cx_done = [sig(f"cx_done{a}", NU) for a in range(2)]
        cxT_done = [sig(f"cxT_done{a}", KT) for a in range(2)]
        o_filled = [sig(f"o_filled{a}", TT) for a in range(2)]
        x_done = [sig(f"x_done{a}", TT) for a in range(2)]
        x_out = sig("x_out", 1, 16)

        front = [("turn", 0, u) for u in range(2)] + [("q", 0, u) for u in range(2)]
        front += [("k", 0, u) for u in range(2)]
        front_values = [("v", 0, t_) for t_ in range(TT)]
        encode = [("v", 1, t_) for t_ in range(TT)]

        def attend_uses(a, fill):
            uses = []
            for u in range(NU):
                uses += [("pt", a, u, k) for k in range(TT)] + ([("w", a, u - 1)] if u else [])
                uses += [f for f, at in fill.items() if at == u]
            return uses + [("w", a, NU - 1)]

        SELF_FILL = {("enc", 0): 0, ("enc", 1): 1, ("k", 1, 0): 2, ("k", 1, 1): 4}

        def output_uses(a):
            return [("o", a, t_) for t_ in range(TT)]

        second = [("turn", 1, u) for u in range(2)] + [("q", 1, u) for u in range(2)]
        before = attend_uses(0, SELF_FILL) + output_uses(0) + encode + second
        late = before + attend_uses(1, {}) + output_uses(1)
        order_last = late
        order_steady = before + front + front_values + attend_uses(1, {}) + output_uses(1)
        read = {("enc", u): (enc_done, u + 1) for u in range(2)}
        for a in range(2):
            read |= {("turn", a, u): (ln_done[a], 2 * u + 2) for u in range(2)}
            read |= {("q", a, u): (q_full[a], 2 * u + 2) for u in range(2)}
            read |= {("k", a, u): (k_full[a], 2 * u + 2) for u in range(2)}
            read |= {("v", a, t_): (v_done[a], t_ + 1) for t_ in range(TT)}
            read |= {("pt", a, u, k): (pt_done[a], u * TT + k + 1) for u in range(NU) for k in range(TT)}
            read |= {("w", a, u): (cx_done[a], u + 1) for u in range(NU)}
            read |= {("o", a, t_): (x_done[a], t_ + 1) for t_ in range(TT)}
        read = {u: (*r, u in late) for u, r in read.items()}
        banks = Banks(ctx, nc, "b_d", 4, read, first=front + front_values, steady=order_steady, last=order_last)
        score = ctx.enter_context(nc.psum_tensor("b_score", [P, 2, 2, BANK], F32))
        WEIGHTS = 16

        block = ctx.enter_context(nc.Block())

        @block.sync
        def _(sp):
            def load(dst, src, columns=False):
                sp.dma_start(dst, src, allow_slow_non_contiguous=columns).then_inc(weights_in.sem, 16)

            def tokens(v):
                return v.rearrange("(t p) n -> p t n", p=P)

            sp.dma_start(xt[:], tokens(hid[0])).then_inc(x_in.sem, 16)
            load(ident[:], ident_in)
            for a, n in enumerate(("ln1", "ln2")):
                load(gains[:, a, :], rowwise(W[n + "_s"], KT), True)
                load(shifts[:, a, :], rowwise(W[n + "_b"], KT), True)
            load(bqkv[:], rowwise(W["b_qkv"], 3 * KT), True)
            load(bq2[:], rowwise(W["b_q"], KT), True)
            load(bkv[:], rowwise(W["b_kv"], 2 * KT), True)
            for dst, n in ((wqkv, "w_qkv"), (wkv, "w_kv"), (wq2, "w_q"), (wout[0], "w_ao"), (wout[1], "w_co")):
                load(dst[:], W[n].rearrange("(k p) n -> p k n", p=P))
            for a, n in enumerate(("b_ao", "b_co")):
                load(bout[a][:], W[n].rearrange("(a n) -> a n", a=1).broadcast_to([P, D]))
            load(mask[0][:], tokens(masks[0][0, 0]))
            sp.dma_start(enc[:], tokens(enc_in[0])).then_inc(enc_load.sem, 16)
            sp.dma_start(mask[1][:], tokens(masks[1][0, 0])).then_inc(mask_in.sem, 16)

            def put(a, b, which, h):
                ready, out = (q_parts, q_out) if which == 0 else (k_parts, k_out)
                tiles = slice(h * KT // 2, (h + 1) * KT // 2)
                sp.wait_ge(ready[a].sem, ready[a].at(b, 1))
                for part in range(2):
                    sp.dma_start(scratch[a][which][b, part].rearrange("(k p) n -> p k n", p=P)[:, tiles, :],
                                 parts[:, part, tiles, :].bitcast(F32)).then_inc(out[a][h].sem, 16)

            def stack(a, b, which, h, first=False):
                if a == SELF:
                    if not first:
                        sp.wait_ge(score_filled[CROSS].sem, score_filled[CROSS].at(b - 1, (h + 1) * NU // 2))
                else:
                    sp.wait_ge(score_filled[SELF].sem, score_filled[SELF].at(b, (h + 1) * NU // 2))
                out, st, order = ((q_out, qst, Q_PARTS), (k_out, kst, K_PARTS))[which]
                sp.wait_ge(out[a][h].sem, out[a][h].at(b, 2))
                for c, part in enumerate(order):
                    sp.dma_start(st[c * DH:(c + 1) * DH, h, :, :].bitcast(F32),
                                 scratch[a][which][b, part, h * HH * DH:(h + 1) * HH * DH, :].rearrange(
                                     "(h d) n -> d h n", d=DH)).then_inc(stacked[a][h].sem, 16)

            def put_and_stack(a, b, which):
                for h in range(2):
                    put(a, b, which, h)
                for h in range(2):
                    stack(a, b, which, h)

            def front_puts(b):
                for which in range(2):
                    for h in range(2):
                        put(SELF, b, which, h)

            def late_steps(b, more):
                put_and_stack(CROSS, b, 1)
                if more:
                    sp.wait_ge(enc_filled.sem, enc_filled.at(b, 2))
                    sp.dma_start(enc[:], tokens(enc_in[b + 1])).then_inc(enc_load.sem, 16)
                    sp.wait_ge(x_done[0].sem, x_done[0].at(b, TT))
                    sp.dma_start(xt[:], tokens(hid[b + 1])).then_inc(x_in.sem, 16)
                put_and_stack(CROSS, b, 0)
                if more:
                    front_puts(b + 1)
                    for h in range(2):
                        for which in range(2):
                            stack(SELF, b + 1, which, h)
                    sp.wait_ge(max_done[CROSS].sem, max_done[CROSS].at(b, NU))
                    sp.dma_start(mask[1][:], tokens(masks[1][b + 1, 0])).then_inc(mask_in.sem, 16)
                sp.wait_ge(x_done[1].sem, x_done[1].at(b, TT))
                sp.dma_start(tokens(mid_out[b]), x1[:]).then_inc(x_out.sem, 16)

            front_puts(0)
            for h in range(2):
                for which in range(2):
                    stack(SELF, 0, which, h, first=True)
            with sp.Fori(0, B - 1) as i:
                late_steps(i, True)
            late_steps(B - 1, False)
            sp.wait_ge(x_out.sem, x_out.at(B, 0))

        @block.gpsimd
        def _(pool):
            nc.gpsimd.memset(half[:], -0.5).then_inc(minus_half.sem, 1)
            pool.wait_ge(minus_half.sem, 1)
            pool.wait_ge(weights_in.sem, 16 * WEIGHTS)

            def rsqrt(b, a):
                pool.wait_ge(var_done[a].sem, var_done[a].at(b, 1))
                nc.gpsimd.tensor_tensor(rstd[:, a, :], vare[:, a, :], half[:].broadcast_to([P, TT]),
                                        ALU.pow).then_inc(rstd_done[a].sem, 1)

            def add_bias(b, a, x):
                pool.wait_ge(xn_done[a].sem, xn_done[a].at(b, 1))
                nc.gpsimd.tensor_tensor(x[:], x[:], bout[a][:].unsqueeze(1).broadcast_to([P, TT, D]),
                                        ALU.add).then_inc(x_biased[a].sem, 1)

            rsqrt(0, 0)
            add_bias(0, 0, xt)
            with pool.Fori(0, B - 1) as i:
                rsqrt(i, 1)
                add_bias(i, 1, x1)
                rsqrt(i + 1, 0)
                add_bias(i + 1, 0, xt)
            rsqrt(B - 1, 1)
            add_bias(B - 1, 1, x1)

        @block.tensor
        def _(pe):
            def turn(sec, b, use, src, filled, us=range(2)):
                for u in us:
                    bank = banks.claim(pe, sec, use + (u,), b, late=use != ("turn", 0))
                    for j in range(2):
                        for t_ in range(TT):
                            k = 2 * u + j
                            last = nc.tensor.transpose(bank[:, (j * TT + t_) * P:(j * TT + t_ + 1) * P],
                                                       src[:, t_, k * P:(k + 1) * P], ident[:])
                    last.then_inc(filled.sem, 1)

            def project(sec, b, use, w, col, src, filled, is_late, steps=range(4)):
                for n in steps:
                    u, j = divmod(n, 2)
                    bank = banks.claim(pe, sec, use + (u,), b, late=is_late) if j == 0 else banks.bank(sec, use + (u,))
                    m = col + n * P
                    for k in range(KT):
                        mm = nc.tensor.matmul(bank[:, j * S:(j + 1) * S], w[:, k, m:m + P], src[:, k, :],
                                              start=(k == 0), stop=(k == KT - 1))
                    if j == 1:
                        mm.then_inc(filled.sem, 1)

            def by_token(sec, b, use, w, col, src, filled, is_late):
                for t_ in range(TT):
                    bank = banks.claim(pe, sec, use + (t_,), b, late=is_late)
                    for k in range(KT):
                        mm = nc.tensor.matmul(bank, src[:, k, t_ * P:(t_ + 1) * P], w[:, k, col:col + D],
                                              start=(k == 0), stop=(k == KT - 1))
                    mm.then_inc(filled.sem, 1)

            def front_turn(sec, b):
                pe.wait_ge(xn_done[0].sem, xn_done[0].at(b, 1))
                turn(sec, b, ("turn", 0), xn, turn_filled[0])

            def front_project(sec, b):
                pe.wait_ge(ln_done[0].sem, ln_done[0].at(b, KT))
                project(sec, b, ("q", 0), wqkv, 0, lnT, q_filled[0], False)
                project(sec, b, ("k", 0), wqkv, D, lnT, k_filled[0], False)

            def front_values(sec, b):
                by_token(sec, b, ("v", 0), wqkv, 2 * D, lnT, v_filled[0], False)

            def self_fill(sec, b, u):
                if u < 2:
                    if u == 0:
                        pe.wait_ge(enc_load.sem, enc_load.at(b, 1))
                    turn(sec, b, ("enc",), enc, enc_filled, (u,))
                elif u < 6:
                    if u == 2:
                        pe.wait_ge(enc_done.sem, enc_done.at(b, 2))
                    project(sec, b, ("k", 1), wkv, 0, encT, k_filled[1], True, (u - 2,))

            def encode(sec, b):
                by_token(sec, b, ("v", 1), wkv, D, encT, v_filled[1], True)

            def scores(b, a, u, first=False):
                h, q, four = unit(u)
                if u % (NU // 2) == 0:
                    pe.wait_ge(stacked[a][h].sem, stacked[a][h].at(b, 2 * len(Q_PARTS)))
                if u >= 2:
                    pe.wait_ge(masked[a].sem, masked[a].at(b, u - 1))
                elif a == CROSS:
                    pe.wait_ge(masked[SELF].sem, masked[SELF].at(b, NU - 1 + u))
                elif not first:
                    pe.wait_ge(masked[CROSS].sem, masked[CROSS].at(b - 1, NU - 1 + u))
                for j in range(G):
                    hh = four * G + j
                    mm = nc.tensor.matmul(score[:, u % 2, j // 2, (j % 2) * S:(j % 2 + 1) * S],
                                          qst[:, h, hh, q * P:(q + 1) * P], kst[:, h, hh, :],
                                          start=True, stop=True)
                mm.then_inc(score_filled[a].sem, 1)

            def attend(sec, b, a, fill=None):
                def turn_probs(u):
                    pe.wait_ge(exp_done[a].sem, exp_done[a].at(b, u + 1))
                    for k in range(TT):
                        bank = banks.claim(pe, sec, ("pt", a, u, k), b, late=True)
                        for j in range(G):
                            last = nc.tensor.transpose(bank[:, j * P:(j + 1) * P], pr[:, u % 3, j, k * P:(k + 1) * P], ident[:])
                        last.then_inc(pt_filled[a].sem, 1)

                def weigh(u):
                    h, q, four = unit(u)
                    pe.wait_ge(pt_done[a].sem, pt_done[a].at(b, (u + 1) * TT))
                    if u == 0:
                        pe.wait_ge(v_done[a].sem, v_done[a].at(b, TT))
                    bank = banks.claim(pe, sec, ("w", a, u), b, late=True)
                    for k in range(TT):
                        for j in range(G):
                            head = (h * HH + four * G + j) * DH
                            nc.tensor.matmul(bank[j * DH:(j + 1) * DH, 0:P], val[a][:, k, head:head + DH],
                                             pt[:, u % 2, k, j * P:(j + 1) * P],
                                             start=(k == 0), stop=(k == TT - 1), tile_position=(0, j * DH))
                    pe.wait_ge(inverse_done[a].sem, inverse_done[a].at(b, u + 1))
                    for j in range(G):
                        mm = nc.tensor.matmul(bank[j * DH:(j + 1) * DH, P:2 * P], inverse[:, u, j:j + 1].broadcast_to([P, DH]), ident[:],
                                              start=True, stop=True, tile_position=(0, j * DH))
                    mm.then_inc(pv_done[a].sem, 1)

                for u in range(NU):
                    if u + 2 < NU:
                        scores(b, a, u + 2)
                    turn_probs(u)
                    if u:
                        weigh(u - 1)
                    if fill:
                        fill(sec, b, u)
                weigh(NU - 1)

            def output(sec, b, a):
                pe.wait_ge(cxT_done[a].sem, cxT_done[a].at(b, KT))
                by_token(sec, b, ("o", a), wout[a], 0, cxT, o_filled[a], True)

            def second(sec, b):
                pe.wait_ge(xn_done[1].sem, xn_done[1].at(b, 1))
                turn(sec, b, ("turn", 1), xn, turn_filled[1])
                pe.wait_ge(ln_done[1].sem, ln_done[1].at(b, KT))
                project(sec, b, ("q", 1), wq2, 0, lnT, q_filled[1], True)

            pe.wait_ge(weights_in.sem, 16 * WEIGHTS)
            front_turn("first", 0)
            front_project("first", 0)
            front_values("first", 0)
            scores(0, SELF, 0, first=True)
            scores(0, SELF, 1, first=True)

            def late_steps(sec, b, more):
                attend(sec, b, SELF, self_fill)
                output(sec, b, SELF)
                encode(sec, b)
                second(sec, b)
                if more:
                    front_turn(sec, b + 1)
                    front_project(sec, b + 1)
                scores(b, CROSS, 0)
                scores(b, CROSS, 1)
                if more:
                    front_values(sec, b + 1)
                attend(sec, b, CROSS)
                if more:
                    scores(b + 1, SELF, 0)
                    scores(b + 1, SELF, 1)
                output(sec, b, CROSS)

            with pe.Fori(0, B - 1) as i:
                late_steps("steady", i, True)
            late_steps("last", B - 1, False)

        @block.scalar
        def _(act):
            def turned(sec, b, a):
                for k in range(KT):
                    act.wait_ge(turn_filled[a].sem, turn_filled[a].at(b, k // 2 + 1))
                    bank = banks.bank(sec, ("turn", a, k // 2))
                    nc.scalar.activation(lnT[:, k, :], bank[:, (k % 2) * S:(k % 2 + 1) * S], ACT.Identity,
                                         bias=shifts[:, a, k:k + 1], scale=gains[:, a, k:k + 1]).then_inc(ln_done[a].sem, 1)

            def biased(sec, b, use, a, filled, done, bias, scale, tiles=range(KT)):
                for k in tiles:
                    act.wait_ge(filled[a].sem, filled[a].at(b, k // 2 + 1))
                    bank = banks.bank(sec, (use, a, k // 2))
                    nc.scalar.activation(full[:, k, :], bank[:, (k % 2) * S:(k % 2 + 1) * S], ACT.Identity,
                                         bias=bias[:, k:k + 1], scale=scale).then_inc(done[a].sem, 1)

            def front(sec, b, first):
                if not first:
                    act.wait_ge(q_filled[1].sem, q_filled[1].at(b - 1, 2))
                turned(sec, b, 0)
                if not first:
                    act.wait_ge(q_parts[1].sem, q_parts[1].at(b - 1, 1))
                biased(sec, b, "q", 0, q_filled, q_full, bqs[:, 0, :], SCALE)
                act.wait_ge(q_parts[0].sem, q_parts[0].at(b, 1))
                biased(sec, b, "k", 0, k_filled, k_full, bqkv[:, KT:2 * KT], 1.0)

            def values(sec, b, a, tiles=range(TT)):
                for t_ in tiles:
                    act.wait_ge(v_filled[a].sem, v_filled[a].at(b, t_ + 1))
                    nc.scalar.activation(val[a][:, t_, :], banks.bank(sec, ("v", a, t_)), ACT.Copy).then_inc(v_done[a].sem, 1)

            def self_fill(sec, b, u):
                if u < 2:
                    act.wait_ge(enc_filled.sem, enc_filled.at(b, u + 1))
                    nc.scalar.activation(encT[:, 2 * u:2 * u + 2, :], banks.bank(sec, ("enc", u)).rearrange("p (k n) -> p k n", k=2),
                                         ACT.Copy).then_inc(enc_done.sem, 1)
                elif u in (3, 5):
                    if u == 3:
                        act.wait_ge(k_parts[0].sem, k_parts[0].at(b, 1))
                    biased(sec, b, "k", 1, k_filled, k_full, bkv[:, 0:KT], 1.0, (u - 3, u - 2))

            def exponentials(b, a, u, first=False):
                act.wait_ge(max_done[a].sem, max_done[a].at(b, u + 1))
                if u >= 3:
                    act.wait_ge(pt_filled[a].sem, pt_filled[a].at(b, (u - 2) * TT))
                elif a == CROSS:
                    act.wait_ge(pt_filled[SELF].sem, pt_filled[SELF].at(b, NU * TT))
                elif not first:
                    act.wait_ge(pt_filled[CROSS].sem, pt_filled[CROSS].at(b - 1, NU * TT))
                for j in range(G):
                    last = nc.scalar.activation(pr[:, u % 3, j, :], t[:, u % 2, j, :], ACT.Exp, scale=-1.0,
                                                bias=nmax[:, u, j:j + 1], accum_out=esum[:, u, j:j + 1])
                last.then_inc(exp_done[a].sem, 1)

            def attend(sec, b, a, fill=None):
                def keep(u):
                    for k in range(TT):
                        act.wait_ge(pt_filled[a].sem, pt_filled[a].at(b, u * TT + k + 1))
                        if k == 0:
                            if u >= 2:
                                act.wait_ge(pv_done[a].sem, pv_done[a].at(b, u - 1))
                        nc.scalar.activation(pt[:, u % 2, k, :], banks.bank(sec, ("pt", a, u, k)), ACT.Copy).then_inc(pt_done[a].sem, 1)

                exponentials(b, a, 1)
                for u in range(NU):
                    if u + 2 < NU:
                        exponentials(b, a, u + 2)
                    keep(u)
                    if fill:
                        fill(sec, b, u)

            def output(sec, b, a):
                bias = bqkv[:, 2 * KT:3 * KT] if a == SELF else bkv[:, KT:2 * KT]
                for k in range(KT):
                    act.wait_ge(cx_done[a].sem, cx_done[a].at(b, k // 2 * (NU // 2) + NU // 2 - 1 + k % 2))
                    nc.scalar.activation(cxT[:, k, :], cxT[:, k, :], ACT.Identity, bias=bias[:, k:k + 1]).then_inc(cxT_done[a].sem, 1)

            def second(sec, b):
                turned(sec, b, 1)
                act.wait_ge(k_parts[1].sem, k_parts[1].at(b, 1))
                biased(sec, b, "q", 1, q_filled, q_full, bqs[:, 1, :], SCALE)

            act.wait_ge(weights_in.sem, 16 * WEIGHTS)
            act.wait_ge(set_up.sem, 2)
            front("first", 0, True)
            values("first", 0, 0)
            exponentials(0, SELF, 0, first=True)

            def late_steps(sec, b, more):
                attend(sec, b, SELF, self_fill)
                output(sec, b, SELF)
                values(sec, b, 1)
                second(sec, b)
                if more:
                    front(sec, b + 1, False)
                exponentials(b, CROSS, 0)
                if more:
                    values(sec, b + 1, 0)
                attend(sec, b, CROSS)
                output(sec, b, CROSS)
                if more:
                    exponentials(b + 1, SELF, 0)

            with act.Fori(0, B - 1) as i:
                late_steps("steady", i, True)
            late_steps("last", B - 1, False)

        @block.vector
        def _(dve):
            def normalise(b, a, x):
                for t_ in range(TT):
                    nc.vector.bn_stats(stats[:, a, t_, :], x[:, t_, :])
                nc.vector.drain()
                for t_ in range(TT):
                    last = nc.vector.bn_aggr(mv[:, a, t_, :], stats[:, a, t_, :])
                nc.vector.drain()
                nc.vector.tensor_scalar(vare[:, a, :], mv[:, a, :, 1], EPS, None, ALU.add).then_inc(var_done[a].sem, 1)

            def apply(b, a, x):
                dve.wait_ge(rstd_done[a].sem, rstd_done[a].at(b, 1))
                for t_ in range(TT):
                    last = nc.vector.tensor_scalar(xn[:, t_, :], x[:, t_, :], mv[:, a, t_, 0:1], rstd[:, a, t_:t_ + 1],
                                                   ALU.subtract, ALU.mult)
                last.then_inc(xn_done[a].sem, 1)

            def split(b, full_done, ready, out=None, out_b=None):
                dve.wait_ge(full_done.sem, full_done.at(b, KT))
                if out is not None:
                    for half_out in out:
                        dve.wait_ge(half_out.sem, half_out.at(out_b, 2))
                nc.vector.tensor_copy(parts[:, 0], full[:])
                nc.vector.drain()
                nc.vector.tensor_tensor(parts[:, 1], full[:], parts[:, 0].bitcast(F32), ALU.subtract).then_inc(ready.sem, 1)

            def front_norm(b):
                dve.wait_ge(x_in.sem, x_in.at(b, 1))
                normalise(b, 0, xt)

            def front_apply(b, first):
                if not first:
                    dve.wait_ge(turn_filled[1].sem, turn_filled[1].at(b - 1, 2))
                apply(b, 0, xt)

            def front_split(b, first):
                if first:
                    split(b, q_full[0], q_parts[0])
                else:
                    split(b, q_full[0], q_parts[0], q_out[1], b - 1)
                split(b, k_full[0], k_parts[0], q_out[0], b)

            def negative(b):
                nc.vector.tensor_scalar(minus[1][:], mask[1][:], 1.0, MASKED, ALU.subtract, ALU.mult).then_inc(minus_done.sem, 1)

            def soften(b, a, u, first=False):
                h, q, four = unit(u)
                dve.wait_ge(score_filled[a].sem, score_filled[a].at(b, u + 1))
                if u >= 2:
                    dve.wait_ge(exp_done[a].sem, exp_done[a].at(b, u - 1))
                elif a == CROSS:
                    dve.wait_ge(exp_done[SELF].sem, exp_done[SELF].at(b, NU - 1 + u))
                elif not first:
                    dve.wait_ge(exp_done[CROSS].sem, exp_done[CROSS].at(b - 1, NU - 1 + u))
                nc.vector.tensor_tensor(t[:, u % 2], score[:, u % 2].rearrange("p x (y n) -> p (x y) n", y=2),
                                        mask[a][:, q, :].unsqueeze(1).broadcast_to([P, G, S]), ALU.mult).then_inc(masked[a].sem, 1)
                nc.vector.drain()
                for j in range(G):
                    last = nc.vector.tensor_tensor_reduce(t[:, u % 2, j, :], t[:, u % 2, j, :], minus[a][:, q, :], -1.0, HUGE,
                                                          ALU.add, ALU.min, accum_out=nmax[:, u, j:j + 1])
                last.then_inc(max_done[a].sem, 1)

            def attend(sec, b, a):
                def invert(u):
                    dve.wait_ge(exp_done[a].sem, exp_done[a].at(b, u + 1))
                    nc.vector.reciprocal(inverse[:, u, :], esum[:, u, :]).then_inc(inverse_done[a].sem, 1)

                def divide(u):
                    h, q, four = unit(u)
                    dve.wait_ge(pv_done[a].sem, pv_done[a].at(b, u + 1))
                    if u == 0 and a == CROSS:
                        dve.wait_ge(o_filled[SELF].sem, o_filled[SELF].at(b, TT))
                    bank = banks.bank(sec, ("w", a, u))
                    nc.vector.tensor_copy(spread[:, u % 2, :], bank[:, P:2 * P])
                    nc.vector.drain()
                    nc.vector.tensor_tensor(cxT[:, 2 * h + four, q * P:(q + 1) * P], bank[:, 0:P], spread[:, u % 2, :],
                                            ALU.mult).then_inc(cx_done[a].sem, 1)

                invert(0)
                for u in range(2, NU):
                    soften(b, a, u)
                    if u > 2:
                        divide(u - 3)
                    invert(u - 1)
                divide(NU - 3)
                if a == SELF:
                    split(b, k_full[1], k_parts[1], k_out[0], b)
                divide(NU - 2)
                invert(NU - 1)
                divide(NU - 1)

            def output(sec, b, a):
                dve.wait_ge(x_biased[a].sem, x_biased[a].at(b, 1))
                if a == SELF:
                    dve.wait_ge(x_out.sem, x_out.at(b, 0))
                x = xt if a == SELF else x1
                for t_ in range(TT):
                    dve.wait_ge(o_filled[a].sem, o_filled[a].at(b, t_ + 1))
                    nc.vector.tensor_tensor(x1[:, t_, :], banks.bank(sec, ("o", a, t_)), x[:, t_, :], ALU.add).then_inc(x_done[a].sem, 1)

            def second_norm(b):
                dve.wait_ge(x_done[0].sem, x_done[0].at(b, TT))
                normalise(b, 1, x1)
                apply(b, 1, x1)

            dve.wait_ge(weights_in.sem, 16 * WEIGHTS)
            nc.vector.tensor_scalar(minus[0][:], mask[0][:], 1.0, MASKED, ALU.subtract, ALU.mult)
            nc.vector.tensor_scalar(bqs[:, 0, :], bqkv[:, 0:KT], SCALE, None, ALU.mult).then_inc(set_up.sem, 1)
            nc.vector.tensor_scalar(bqs[:, 1, :], bq2[:], SCALE, None, ALU.mult).then_inc(set_up.sem, 1)
            dve.wait_ge(set_up.sem, 2)
            front_norm(0)
            front_apply(0, True)
            front_split(0, True)
            soften(0, SELF, 0, first=True)
            soften(0, SELF, 1, first=True)

            def late_steps(sec, b, more):
                attend(sec, b, SELF)
                output(sec, b, SELF)
                second_norm(b)
                dve.wait_ge(mask_in.sem, mask_in.at(b, 1))
                negative(b)
                if more:
                    front_norm(b + 1)
                if more:
                    front_apply(b + 1, False)
                split(b, q_full[1], q_parts[1], k_out[1], b)
                if more:
                    front_split(b + 1, False)
                dve.wait_ge(minus_done.sem, minus_done.at(b, 1))
                soften(b, CROSS, 0)
                soften(b, CROSS, 1)
                attend(sec, b, CROSS)
                if more:
                    soften(b + 1, SELF, 0)
                    soften(b + 1, SELF, 1)
                output(sec, b, CROSS)

            with dve.Fori(0, B - 1) as i:
                late_steps("steady", i, True)
            late_steps("last", B - 1, False)


def network_layer(nc, sems, mid_in, ident_in, W, out):
    B, S, D = mid_in.shape
    KT = D // P
    TT = S // P
    F = W["w1"].shape[1]
    FT = F // P
    with ExitStack() as ctx:
        def sb(name, shape, dt=F32):
            return ctx.enter_context(nc.sbuf_tensor("c_" + name, shape, dt))

        def sig(name, per, unit=1):
            return Signal(sems, nc, "c_" + name, per, unit)

        w1 = sb("w1", [P, KT, F])
        w2 = sb("w2", [P, FT, D])
        gain = sb("gain", [P, KT])
        shift = sb("shift", [P, KT])
        b1 = sb("b1", [P, FT])
        b2 = sb("b2", [P, D])
        ident = sb("ident", [P, P])
        half = sb("half", [P, 1])
        xt = sb("xt", [P, TT, D])
        xn = sb("xn", [P, TT, D])
        xb = sb("xb", [P, TT, D])
        stats = sb("stats", [P, TT, 6])
        mv = sb("mv", [P, TT, 2])
        vare = sb("vare", [P, TT])
        rstd = sb("rstd", [P, TT])
        lnT = sb("lnT", [P, KT, S])
        gT = sb("gT", [P, FT, S])
        res = sb("res", [P, TT, D])

        weights_in = sig("weights_in", 1, 16)
        w2_in = sig("w2_in", 1, 16)
        x_in = sig("x_in", 1, 16)
        minus_half = sig("minus_half", 1)
        var_done = sig("var_done", 1)
        rstd_done = sig("rstd_done", 1)
        xn_done = sig("xn_done", 1)
        xb_done = sig("xb_done", 1)
        turn_filled = sig("turn_filled", 2)
        ln_done = sig("ln_done", KT)
        f1_filled = sig("f1_filled", FT // 2)
        g_done = sig("g_done", FT)
        f2_filled = sig("f2_filled", TT)
        res_done = sig("res_done", TT)
        x_out = sig("x_out", 1, 16)

        turns = [("turn", u) for u in range(2)]
        ups = [("f1", u) for u in range(FT // 2)]
        downs = [("f2", t_) for t_ in range(TT)]
        read = {("turn", u): (ln_done, 2 * u + 2, False) for u in range(2)}
        read |= {("f1", u): (g_done, 2 * u + 2, True) for u in range(FT // 2)}
        read |= {("f2", t_): (res_done, t_ + 1, True) for t_ in range(TT)}
        banks = Banks(ctx, nc, "c_d", 6, read, first=turns, steady=ups + turns + downs, last=ups + downs)

        block = ctx.enter_context(nc.Block())

        def tokens(v):
            return v.rearrange("(t p) n -> p t n", p=P)

        @block.sync
        def _(sp):
            def load(dst, src, columns=False):
                sp.dma_start(dst, src, allow_slow_non_contiguous=columns).then_inc(weights_in.sem, 16)

            sp.dma_start(xt[:], tokens(mid_in[0])).then_inc(x_in.sem, 16)
            load(ident[:], ident_in)
            load(gain[:], rowwise(W["ln3_s"], KT), True)
            load(shift[:], rowwise(W["ln3_b"], KT), True)
            load(b1[:], rowwise(W["b1"], FT), True)
            load(b2[:], W["b2"].rearrange("(a n) -> a n", a=1).broadcast_to([P, D]))
            load(w1[:], W["w1"].rearrange("(k p) n -> p k n", p=P))
            sp.dma_start(w2[:], W["w2"].rearrange("(k p) n -> p k n", p=P)).then_inc(w2_in.sem, 16)

            def store(b):
                sp.wait_ge(res_done.sem, res_done.at(b, TT))
                sp.dma_start(tokens(out[b]), res[:]).then_inc(x_out.sem, 16)

            with sp.Fori(0, B - 1) as i:
                sp.wait_ge(xb_done.sem, xb_done.at(i, 1))
                sp.dma_start(xt[:], tokens(mid_in[i + 1])).then_inc(x_in.sem, 16)
                store(i)
            store(B - 1)
            sp.wait_ge(x_out.sem, x_out.at(B, 0))

        @block.gpsimd
        def _(pool):
            nc.gpsimd.memset(half[:], -0.5).then_inc(minus_half.sem, 1)
            pool.wait_ge(minus_half.sem, 1)
            pool.wait_ge(weights_in.sem, 16 * 6)

            with pool.Fori(0, B) as b:
                pool.wait_ge(var_done.sem, var_done.at(b, 1))
                nc.gpsimd.tensor_tensor(rstd[:], vare[:], half[:].broadcast_to([P, TT]), ALU.pow).then_inc(rstd_done.sem, 1)
                pool.wait_ge(xn_done.sem, xn_done.at(b, 1))
                pool.wait_ge(res_done.sem, res_done.at(b, 0))
                nc.gpsimd.tensor_tensor(xb[:], xt[:], b2[:].unsqueeze(1).broadcast_to([P, TT, D]), ALU.add).then_inc(xb_done.sem, 1)

        @block.tensor
        def _(pe):
            def turn(sec, b):
                pe.wait_ge(xn_done.sem, xn_done.at(b, 1))
                for u in range(2):
                    bank = banks.claim(pe, sec, ("turn", u), b)
                    for j in range(2):
                        for t_ in range(TT):
                            k = 2 * u + j
                            last = nc.tensor.transpose(bank[:, (j * TT + t_) * P:(j * TT + t_ + 1) * P],
                                                       xn[:, t_, k * P:(k + 1) * P], ident[:])
                    last.then_inc(turn_filled.sem, 1)

            def up(sec, b):
                pe.wait_ge(ln_done.sem, ln_done.at(b, KT))
                for u in range(FT // 2):
                    bank = banks.claim(pe, sec, ("f1", u), b, late=True)
                    for j in range(2):
                        m = (2 * u + j) * P
                        for k in range(KT):
                            mm = nc.tensor.matmul(bank[:, j * S:(j + 1) * S], w1[:, k, m:m + P], lnT[:, k, :],
                                                  start=(k == 0), stop=(k == KT - 1))
                    mm.then_inc(f1_filled.sem, 1)

            def down(sec, b):
                pe.wait_ge(g_done.sem, g_done.at(b, FT))
                for t_ in range(TT):
                    bank = banks.claim(pe, sec, ("f2", t_), b, late=True)
                    for k in range(FT):
                        mm = nc.tensor.matmul(bank, gT[:, k, t_ * P:(t_ + 1) * P], w2[:, k, :],
                                              start=(k == 0), stop=(k == FT - 1))
                    mm.then_inc(f2_filled.sem, 1)

            pe.wait_ge(weights_in.sem, 16 * 6)
            turn("first", 0)
            pe.wait_ge(w2_in.sem, 16)
            with pe.Fori(0, B - 1) as i:
                up("steady", i)
                turn("steady", i + 1)
                down("steady", i)
            up("last", B - 1)
            down("last", B - 1)

        @block.scalar
        def _(act):
            def turned(sec, b):
                act.wait_ge(f1_filled.sem, f1_filled.at(b, 0))
                for k in range(KT):
                    act.wait_ge(turn_filled.sem, turn_filled.at(b, k // 2 + 1))
                    nc.scalar.activation(lnT[:, k, :], banks.bank(sec, ("turn", k // 2))[:, (k % 2) * S:(k % 2 + 1) * S],
                                         ACT.Identity, bias=shift[:, k:k + 1], scale=gain[:, k:k + 1]).then_inc(ln_done.sem, 1)

            def gelu(sec, b):
                act.wait_ge(f2_filled.sem, f2_filled.at(b, 0))
                for m in range(FT):
                    act.wait_ge(f1_filled.sem, f1_filled.at(b, m // 2 + 1))
                    nc.scalar.activation(gT[:, m, :], banks.bank(sec, ("f1", m // 2))[:, (m % 2) * S:(m % 2 + 1) * S],
                                         ACT.Gelu_apprx_tanh, bias=b1[:, m:m + 1]).then_inc(g_done.sem, 1)

            act.wait_ge(weights_in.sem, 16 * 6)
            turned("first", 0)
            with act.Fori(0, B - 1) as i:
                gelu("steady", i)
                turned("steady", i + 1)
            gelu("last", B - 1)

        @block.vector
        def _(dve):
            def normalise(b):
                dve.wait_ge(x_in.sem, x_in.at(b, 1))
                for t_ in range(TT):
                    nc.vector.bn_stats(stats[:, t_, :], xt[:, t_, :])
                nc.vector.drain()
                for t_ in range(TT):
                    last = nc.vector.bn_aggr(mv[:, t_, :], stats[:, t_, :])
                nc.vector.drain()
                nc.vector.tensor_scalar(vare[:], mv[:, :, 1], EPS, None, ALU.add).then_inc(var_done.sem, 1)
                dve.wait_ge(rstd_done.sem, rstd_done.at(b, 1))
                dve.wait_ge(turn_filled.sem, turn_filled.at(b, 0))
                for t_ in range(TT):
                    last = nc.vector.tensor_scalar(xn[:, t_, :], xt[:, t_, :], mv[:, t_, 0:1], rstd[:, t_:t_ + 1],
                                                   ALU.subtract, ALU.mult)
                last.then_inc(xn_done.sem, 1)

            def add(sec, b):
                dve.wait_ge(xb_done.sem, xb_done.at(b, 1))
                dve.wait_ge(x_out.sem, x_out.at(b, 0))
                for t_ in range(TT):
                    dve.wait_ge(f2_filled.sem, f2_filled.at(b, t_ + 1))
                    nc.vector.tensor_tensor(res[:, t_, :], banks.bank(sec, ("f2", t_)), xb[:, t_, :], ALU.add).then_inc(res_done.sem, 1)

            dve.wait_ge(weights_in.sem, 16 * 6)
            normalise(0)
            with dve.Fori(0, B - 1) as i:
                normalise(i + 1)
                add("steady", i)
            add("last", B - 1)


_L0 = ["Wq", "Wk", "Wv", "Wo", "ln_q_g", "ln_q_b", "ln_kv_g", "ln_kv_b", "ffn_ln_g", "ffn_ln_b", "W1", "b1", "W2", "b2"]
_L1 = ["ln1_s", "ln1_b", "w_qkv", "b_qkv", "w_ao", "b_ao", "ln2_s", "ln2_b", "w_q", "b_q", "w_kv", "b_kv", "w_co",
       "b_co", "ln3_s", "ln3_b", "w1", "b1", "w2", "b2"]
_IN = ["x", "ctx_2048", "mask_1x1xSxS2_fc1", "mask_Bx1xSxS2_ff1"]


def build(nc, a, out):
    x = a["x"]
    B, C, T = x.shape

    def scratch(name, shape, dt):
        return nc.dram_tensor(name, shape, dt, kind="Internal").ap()

    hid = scratch("hidden", [B, C, T], F32)
    mid = scratch("middle", [B, C, T], F32)
    with ExitStack() as sems:
        first_layer(nc, sems, x, a["ctx_2048"], a["positions"], a["identity"], {n: a["L0_xattn_" + n] for n in _L0}, hid,
                    scratch("a_q", [B, 3, C, T], BF16), scratch("a_k", [B, 3, C, T], BF16),
                    scratch("a_m", [B, 3, HEADS, T], BF16))
        W = {n: a["L1_xattn_" + n] for n in _L1}
        attention_layer(nc, sems, hid, a["ctx_2048"], (a["mask_1x1xSxS2_fc1"], a["mask_Bx1xSxS2_ff1"]), a["identity"],
                        W, mid, [[scratch(f"b_{n}{k}", [B, 2, T, C], F32) for n in "qk"] for k in range(2)])
        network_layer(nc, sems, mid, a["identity"], W, out)


def positions(c, t):
    import math
    import numpy as np
    pos = np.arange(t, dtype=np.float32)[:, None]
    div = np.exp(np.arange(0, c, 2, dtype=np.float32) * np.float32(-math.log(10000.0) / c))
    ang = pos * div
    pe = np.zeros((t, c), np.float32)
    pe[:, 0::2] = np.sin(ang)
    pe[:, 1::2] = np.cos(ang)
    return np.ascontiguousarray(pe.T)


def kernel(**inputs):
    import numpy as _np
    import concourse.bacc as _bacc
    from concourse import mybir as _mybir
    from concourse.bass_utils import run_bass_kernel_spmd as _run

    nc = _bacc.Bacc("TRN2", target_bir_lowering=False, num_devices=1)
    names = _IN + ["L0_xattn_" + n for n in _L0] + ["L1_xattn_" + n for n in _L1]
    given = {n: _np.ascontiguousarray(inputs[n]) for n in names}
    b, c, t = given["x"].shape
    given["positions"] = positions(c, t)
    given["identity"] = _np.eye(P, dtype=_np.float32)
    arrays, args = {}, {}
    for name, v in given.items():
        arrays[f"in_{name}"] = v
        args[name] = nc.dram_tensor(f"in_{name}", v.shape, _mybir.dt.from_np(v.dtype), kind="ExternalInput").ap()
    out = nc.dram_tensor("out_0", (b, c, t), F32, kind="ExternalOutput").ap()
    build(nc, args, out)
    r = _run(nc, [arrays], core_ids=[0])
    return r.results[0]["out_0"]
```

```python
from contextlib import ExitStack

import concourse.bass as bass
from concourse import mybir

F32 = mybir.dt.float32
F32R = mybir.dt.float32r
BF16 = mybir.dt.bfloat16
ALU = mybir.AluOpType
ACT = mybir.ActivationFunctionType
AX_X = mybir.AxisListType.X

P = 128
BANK = 512
EPS = 1e-5
HEADS = 16


class Signal:

    def __init__(self, ctx, nc, name, per, unit=1):
        self.sem = ctx.enter_context(nc.semaphore(name))
        self.per = per
        self.unit = unit

    def at(self, b, n):
        return b * (self.per * self.unit) + n * self.unit


class Banks:

    def __init__(self, ctx, nc, name, n, read, **order):
        self.n = n
        self.tile = ctx.enter_context(nc.psum_tensor(name, [P, n, BANK], F32))
        self.read = read
        self.order = order | {"peeled": order["steady"]}

    def bank(self, section, use):
        return self.tile[:, self.order[section].index(use) % self.n, :]

    def claim(self, eng, section, use, b, late=False):
        at = self.order[section].index(use)
        turn = section in ("peeled", "steady")
        if late and turn:
            b = b + 1
        if at >= self.n:
            before, batch = self.order[section][at - self.n], b
        elif section == "first":
            return self.bank(section, use)
        else:
            k = at % self.n
            order, batch = self.order["first" if section == "peeled" else "steady"], b - 1 if turn else b
            befores = [u for i, u in enumerate(order) if i % self.n == k]
            if not befores:
                return self.bank(section, use)
            before = befores[-1]
            turn = section != "peeled"
        signal, n, is_late = self.read[before]
        eng.wait_ge(signal.sem, signal.at(batch - 1 if is_late and turn else batch, n))
        return self.bank(section, use)


def rowwise(v, tiles):
    return v.rearrange("(t p) -> p t", t=tiles)


def first_layer(nc, sems, x, ctx_in, pos, ident_in, W, hid, scratch_q, scratch_k, scratch_m):
    B, C, T = x.shape
    CT = C // P
    TT = T // P
    DH = C // HEADS
    F = W["W1"].shape[1]
    FT = F // P
    SCALE = float(DH) ** -0.5
    GROUP = P // 32
    NG = HEADS // GROUP
    RING = GROUP + 1
    Q_PARTS = (0, 0, 1, 1, 0, 2)
    K_PARTS = (0, 1, 0, 1, 2, 0)
    ROWS = len(Q_PARTS) * DH
    ROWS_M = ROWS + 3

    with ExitStack() as ctx:
        def sb(name, shape, dt=F32):
            return ctx.enter_context(nc.sbuf_tensor("a_" + name, shape, dt))

        def sig(name, per, unit=1):
            return Signal(sems, nc, "a_" + name, per, unit)

        wq, wk, wv, wo = (sb(n, [P, CT, C]) for n in ("wq", "wk", "wv", "wo"))
        w1 = sb("w1", [P, CT, F])
        w2 = sb("w2", [P, FT, C])
        gains = sb("gains", [P, 3, CT])
        shifts = sb("shifts", [P, 3, CT])
        b1 = sb("b1", [P, FT])
        b2 = sb("b2", [P, CT])
        ident = sb("ident", [P, P])
        half = sb("half", [P, 1])
        pe = sb("pe", [P, CT, T])
        xin = [sb(f"xin{s}", [P, CT, T]) for s in range(2)]
        tokn = [sb(f"tokn{s}", [P, TT, C]) for s in range(3)]
        stats = sb("stats", [P, 3, TT, 6])
        mv = sb("mv", [P, 3, TT, 2])
        vare = sb("vare", [P, 3, TT])
        rstd = sb("rstd", [P, 3, TT])
        qnT = sb("qnT", [P, CT, T])
        kvnT = sb("kvnT", [P, CT, T])
        rest = sb("rest", [P, CT, T])
        qparts = sb("qparts", [P, 3, CT, T], BF16)
        kparts = sb("kparts", [P, 3, CT, T], BF16)
        qst = sb("qst", [P, HEADS, T], BF16)
        kst = sb("kst", [P, HEADS, T], BF16)
        vaug = sb("vaug", [P, TT, HEADS, 32])
        mx = sb("mx", [P, TT, HEADS])
        mrest = sb("mrest", [HEADS, T])
        mparts = sb("mparts", [HEADS, 3, T], BF16)
        pt = sb("pt", [P, RING, TT, T])
        ctxr = sb("ctxr", [P, 2, T])
        rsum = sb("rsum", [P, NG, TT, GROUP])
        ctxt = sb("ctxt", [P, TT, C])
        ctxT = sb("ctxT", [P, CT, T])
        rT = sb("rT", [P, CT, T])
        hT = sb("hT", [P, CT, T])
        gT = sb("gT", [P, FT, T])
        outT = sb("outT", [P, CT, T])

        pos_in = sig("pos_in", 1, 16)
        consts_in = sig("consts_in", 1, 16)
        qkv_in = sig("qkv_in", 1, 16)
        late_in = sig("late_in", 1, 16)
        ones_set = sig("ones_set", 1)
        x_in = [sig(f"x_in{s}", 1, 16) for s in range(2)]
        x_pe = [sig(f"x_pe{s}", 1) for s in range(2)]
        tok_filled = [sig(f"tok_filled{s}", 2) for s in range(3)]
        var_done = [sig(f"var_done{s}", 1) for s in range(3)]
        rstd_done = [sig(f"rstd_done{s}", 1) for s in range(3)]
        tok_done = [sig(f"tok_done{s}", 2) for s in range(3)]
        chan_filled = [sig(f"chan_filled{s}", CT) for s in range(3)]
        chan_done = [sig(f"chan_done{s}", CT) for s in range(3)]
        qk_filled = sig("qk_filled", 2 * CT)
        restd = sig("restd", 2 * CT)
        mid = sig("mid", 2 * CT)
        low = sig("low", 2 * CT)
        parts_out = [sig(f"parts_out{s}", 3, 16) for s in range(2)]
        stacked = [sig(f"stacked{h}", 2 * len(Q_PARTS), 16) for h in range(2)]
        v_filled = sig("v_filled", 2)
        v_done = sig("v_done", 2)
        score_filled = sig("score_filled", 4 * HEADS)
        max_done = sig("max_done", 2 * HEADS)
        m_filled = sig("m_filled", 1)
        m_high = sig("m_high", 1)
        m_rest = sig("m_rest", 1)
        m_low = sig("m_low", 1)
        m_out = sig("m_out", 1, 16)
        m_in = sig("m_in", 1, 16)
        exp_done = sig("exp_done", 2 * HEADS)
        pv_done = sig("pv_done", NG)
        ctx_raw = sig("ctx_raw", NG)
        ctx_filled = sig("ctx_filled", NG)
        ctx_tok = sig("ctx_tok", NG)
        ctxT_filled = sig("ctxT_filled", CT)
        ctx_chan = sig("ctx_chan", CT)
        y_filled = sig("y_filled", CT)
        r_done = sig("r_done", CT)
        f1_filled = sig("f1_filled", FT)
        g_done = sig("g_done", FT)
        f2_filled = sig("f2_filled", CT)
        o_done = sig("o_done", CT)
        o_out = sig("o_out", 1, 16)

        FRONT_FILL = {0: "tok0", 2: "tok1", 5: "chan0", 7: "chan1", 9: "q0", 10: "q1", 11: "k0", 12: "k1"}
        LATE_FILL = {0: "tok2", 2: "v0", 4: "chan2", 6: "v1", 8: "f10", 10: "f11", 12: "f12", 14: "f13"}

        def stages(fill):
            name, n = fill[:-1], int(fill[-1])
            return [(name, n, u) for u in range(2)] if name in ("tok", "chan") else [(name, n)]

        def attention_uses(fills):
            uses = []
            for h in range(HEADS):
                if h % GROUP == 2 and h > GROUP:
                    uses.append(("ctx", h // GROUP - 1))
                if h in fills:
                    uses += stages(fills[h])
            return uses

        front = [u for f in FRONT_FILL.values() for u in stages(f)]
        values = [("v", u) for u in range(2)]
        tail_a = [("ctx", NG - 1)] + [("ctxT", c) for c in range(CT)] + [("y", m) for m in range(CT)]
        late_fill = [u for f in LATE_FILL.values() for u in stages(f)]
        tail_c = [("f2", m) for m in range(CT)]
        last_fill = [u for u in late_fill if u not in values]
        late = [("ctx", g) for g in range(NG)] + tail_a + last_fill + tail_c
        read = {("m",): (m_rest, 1)}
        read |= {("tok", s, u): (tok_done[s], u + 1) for s in range(3) for u in range(2)}
        read |= {("chan", s, c): (chan_done[s], c + 1) for s in range(3) for c in range(CT)}
        read |= {(n, m): (restd, "qk".index(n) * CT + m + 1) for n in "qk" for m in range(CT)}
        read |= {("v", u): (v_done, u + 1) for u in range(2)}
        read |= {("ctx", g): (ctx_tok, g + 1) for g in range(NG)}
        read |= {("ctxT", c): (ctx_chan, c + 1) for c in range(CT)}
        read |= {("y", m): (r_done, m + 1) for m in range(CT)}
        read |= {("f1", m): (g_done, m + 1) for m in range(FT)}
        read |= {("f2", m): (o_done, m + 1) for m in range(CT)}
        read = {u: (*r, u in late) for u, r in read.items()}
        banks = Banks(ctx, nc, "a_d", 3, read, first=front + values + [("m",)],
                      steady=attention_uses(FRONT_FILL) + tail_a + late_fill + [("m",)] + tail_c,
                      last=attention_uses({}) + tail_a + last_fill + tail_c)
        score = ctx.enter_context(nc.psum_tensor("a_score", [P, 2, 2, BANK], F32))
        ctxp = ctx.enter_context(nc.psum_tensor("a_ctxp", [P, BANK], F32))
        CONSTS, QKV, LATE = 7, 3, 5

        block = ctx.enter_context(nc.Block())

        @block.sync
        def _(sp):
            def load(signal, dst, src, columns=False):
                sp.dma_start(dst, src, allow_slow_non_contiguous=columns).then_inc(signal.sem, 16)

            def matrix(w):
                return w.rearrange("(k p) n -> p k n", p=P)

            load(pos_in, pe[:], pos.rearrange("(c p) t -> p c t", p=P))
            for s, src in enumerate((x, ctx_in)):
                sp.dma_start(xin[s][:], src[0].rearrange("(c p) t -> p c t", p=P)).then_inc(x_in[s].sem, 16)
            load(consts_in, ident[:], ident_in)
            for i, n in enumerate(("ln_q", "ln_kv", "ffn_ln")):
                load(consts_in, gains[:, i, :], rowwise(W[n + "_g"], CT), True)
                load(consts_in, shifts[:, i, :], rowwise(W[n + "_b"], CT), True)
            for dst, n in ((wq, "Wq"), (wk, "Wk"), (wv, "Wv")):
                load(qkv_in, dst[:], matrix(W[n]))
            for dst, n in ((wo, "Wo"), (w1, "W1"), (w2, "W2")):
                load(late_in, dst[:], matrix(W[n]))
            load(late_in, b1[:], rowwise(W["b1"], FT), True)
            load(late_in, b2[:], rowwise(W["b2"], CT), True)

            def fetch(b):
                for s, src in enumerate((x, ctx_in)):
                    sp.wait_ge(tok_filled[s].sem, tok_filled[s].at(b - 1, 2))
                    sp.dma_start(xin[s][:], src[b].rearrange("(c p) t -> p c t", p=P)).then_inc(x_in[s].sem, 16)

            def stack(b, first=False):
                for s, (parts, scr) in enumerate(((qparts, scratch_q), (kparts, scratch_k))):
                    sp.wait_ge(low.sem, low.at(b, (s + 1) * CT))
                    for part in range(3):
                        sp.dma_start(scr[b, part].rearrange("(c p) n -> p c n", p=P), parts[:, part]).then_inc(parts_out[s].sem, 16)
                for half in range(2):
                    if not first:
                        sp.wait_ge(score_filled.sem, score_filled.at(b - 1, 2 * HEADS + (half + 1) * HEADS))
                    heads = slice(half * HEADS // 2, (half + 1) * HEADS // 2)
                    for s, (st, scr, order) in enumerate(((qst, scratch_q, Q_PARTS), (kst, scratch_k, K_PARTS))):
                        if half == 0:
                            sp.wait_ge(parts_out[s].sem, parts_out[s].at(b, 3))
                        for c, part in enumerate(order):
                            sp.dma_start(st[c * DH:(c + 1) * DH, heads, :],
                                         scr[b, part].rearrange("(h d) n -> d h n", d=DH)[:, heads, :]).then_inc(stacked[half].sem, 16)

            def maxima(b):
                sp.wait_ge(m_low.sem, m_low.at(b, 1))
                sp.dma_start(scratch_m[b].rearrange("t h n -> h t n"), mparts[:]).then_inc(m_out.sem, 16)
                sp.wait_ge(m_out.sem, m_out.at(b, 1))
                sp.dma_start(qst[ROWS:ROWS_M, :, :], scratch_m[b]).then_inc(m_in.sem, 16)

            def store(b):
                sp.wait_ge(o_done.sem, o_done.at(b, CT))
                sp.dma_start(hid[b].rearrange("(c p) t -> p c t", p=P), outT[:]).then_inc(o_out.sem, 16)

            def steps(b, more):
                if more:
                    fetch(b + 2)
                stack(b + 1)
                maxima(b + 1)
                store(b)

            fetch(1)
            stack(0, first=True)
            maxima(0)
            steps(0, True)
            with sp.Fori(1, B - 2) as i:
                steps(i, True)
            steps(B - 2, False)
            store(B - 1)
            sp.wait_ge(o_out.sem, o_out.at(B, 0))

        @block.gpsimd
        def _(pool):
            nc.gpsimd.memset(half[:], -0.5)
            nc.gpsimd.drain()
            pool.wait_ge(pos_in.sem, 16)

            def add_positions(b):
                for s in range(2):
                    pool.wait_ge(x_in[s].sem, x_in[s].at(b, 1))
                    nc.gpsimd.tensor_tensor(xin[s][:], xin[s][:], pe[:], ALU.add).then_inc(x_pe[s].sem, 1)

            def rsqrt(b, s):
                pool.wait_ge(var_done[s].sem, var_done[s].at(b, 1))
                nc.gpsimd.tensor_tensor(rstd[:, s, :], vare[:, s, :], half[:].broadcast_to([P, TT]),
                                        ALU.pow).then_inc(rstd_done[s].sem, 1)

            def low_parts(b):
                for s, parts in enumerate((qparts, kparts)):
                    for m in range(CT):
                        pool.wait_ge(mid.sem, mid.at(b, s * CT + m + 1))
                        nc.gpsimd.tensor_tensor(parts[:, 2, m, :], rest[:, m, :], parts[:, 1, m, :],
                                                ALU.subtract).then_inc(low.sem, 1)

            add_positions(0)
            rsqrt(0, 0)
            rsqrt(0, 1)
            low_parts(0)
            add_positions(1)

            def steps(b, more):
                rsqrt(b + 1, 0)
                rsqrt(b + 1, 1)
                low_parts(b + 1)
                rsqrt(b, 2)
                if more:
                    add_positions(b + 2)

            steps(0, True)
            with pool.Fori(1, B - 2) as i:
                steps(i, True)
            steps(B - 2, False)
            rsqrt(B - 1, 2)

        @block.tensor
        def _(pe_):
            def turn_to_tokens(sec, b, s, src, us=range(2)):
                for u in us:
                    bank = banks.claim(pe_, sec, ("tok", s, u), b, late=(s == 2))
                    for t in range(2):
                        for c in range(CT):
                            at = (2 * u + t) * P
                            last = nc.tensor.transpose(bank[:, (t * CT + c) * P:(t * CT + c + 1) * P],
                                                       src[:, c, at:at + P], ident[:])
                    last.then_inc(tok_filled[s].sem, 1)

            def turn_to_channels(sec, b, s, src, cs=range(CT)):
                pe_.wait_ge(tok_done[s].sem, tok_done[s].at(b, 2))
                for c in cs:
                    bank = banks.claim(pe_, sec, ("chan", s, c), b, late=(s == 2))
                    for t in range(TT):
                        last = nc.tensor.transpose(bank[:, t * P:(t + 1) * P], src[:, t, c * P:(c + 1) * P], ident[:])
                    last.then_inc(chan_filled[s].sem, 1)

            def project(sec, b, name, m):
                s, w, src = (0, wq, qnT) if name == "q" else (1, wk, kvnT)
                bank = banks.claim(pe_, sec, (name, m), b)
                for k in range(CT):
                    if m == 0:
                        pe_.wait_ge(chan_done[s].sem, chan_done[s].at(b, k + 1))
                    mm = nc.tensor.matmul(bank, w[:, k, m * P:(m + 1) * P], src[:, k, :],
                                          start=(k == 0), stop=(k == CT - 1))
                mm.then_inc(qk_filled.sem, 1)

            def front_step(sec, b, fill):
                name, n = fill[:-1], int(fill[-1])
                if name == "tok":
                    pe_.wait_ge(x_pe[n].sem, x_pe[n].at(b, 1))
                    turn_to_tokens(sec, b, n, xin[n])
                elif name == "chan":
                    turn_to_channels(sec, b, n, tokn[n])
                else:
                    project(sec, b, name, n)

            def values(sec, b, u, halves=range(2)):
                for t in halves:
                    bank = banks.bank(sec, ("v", u)) if t else banks.claim(pe_, sec, ("v", u), b)
                    at = (2 * u + t) * P
                    for k in range(CT):
                        mm = nc.tensor.matmul(bank[:, t * C:(t + 1) * C], kvnT[:, k, at:at + P], wv[:, k, :],
                                              start=(k == 0), stop=(k == CT - 1))
                    if t:
                        mm.then_inc(v_filled.sem, 1)

            def late_step(sec, b, fill, halves=range(2)):
                name, m = fill[:-1], int(fill[-1])
                for half in halves:
                    if name == "tok":
                        pe_.wait_ge(r_done.sem, r_done.at(b, CT))
                        turn_to_tokens(sec, b, 2, rT, (half,))
                    elif name == "chan":
                        turn_to_channels(sec, b, 2, tokn[2], (half,))
                    elif name == "v":
                        values(sec, b + 1, m, (half,))
                    else:
                        bank = banks.bank(sec, ("f1", m)) if half else banks.claim(pe_, sec, ("f1", m), b, late=True)
                        for k in range(half * CT // 2, (half + 1) * CT // 2):
                            if m == 0:
                                pe_.wait_ge(chan_done[2].sem, chan_done[2].at(b, k + 1))
                            mm = nc.tensor.matmul(bank, w1[:, k, m * P:(m + 1) * P], hT[:, k, :],
                                                  start=(k == 0), stop=(k == CT - 1))
                        if half:
                            mm.then_inc(f1_filled.sem, 1)

            def row_maxima(sec, b, h, first=False, fill=None):
                if h % (HEADS // 2) == 0:
                    half_in = stacked[h // (HEADS // 2)]
                    pe_.wait_ge(half_in.sem, half_in.at(b, 2 * len(Q_PARTS)))
                for p in range(2):
                    if h == 0 and not first:
                        pe_.wait_ge(exp_done.sem, exp_done.at(b - 1, 2 * HEADS - 1 + p))
                    elif h:
                        pe_.wait_ge(max_done.sem, max_done.at(b, 2 * h + p - 1))
                    for j in range(2):
                        q = (2 * p + j) * P
                        mm = nc.tensor.matmul(score[:, p, j, :], qst[0:ROWS, h, q:q + P], kst[0:ROWS, h, :],
                                              start=True, stop=True)
                    mm.then_inc(score_filled.sem, 1)
                    if fill:
                        late_step(sec, b - 1, fill, (p,))

            def turn_maxima(sec, b):
                pe_.wait_ge(max_done.sem, max_done.at(b, 2 * HEADS))
                bank = banks.claim(pe_, sec, ("m",), b)
                for t in range(TT):
                    last = nc.tensor.transpose(bank[0:HEADS, t * P:(t + 1) * P], mx[:, t, :], ident[:])
                last.then_inc(m_filled.sem, 1)

            def shifted_scores(b, h):
                if h == 0:
                    pe_.wait_ge(m_in.sem, m_in.at(b, 1))
                for p in range(2):
                    if h:
                        pe_.wait_ge(exp_done.sem, exp_done.at(b, 2 * h + p - 1))
                    for j in range(2):
                        k = (2 * p + j) * P
                        mm = nc.tensor.matmul(score[:, p, j, :], kst[0:ROWS_M, h, k:k + P], qst[0:ROWS_M, h, :],
                                              start=True, stop=True)
                    mm.then_inc(score_filled.sem, 1)

            def weigh_values(b, g):
                pe_.wait_ge(exp_done.sem, exp_done.at(b, 2 * GROUP * (g + 1)))
                if g == 0:
                    pe_.wait_ge(v_done.sem, v_done.at(b, 2))
                else:
                    pe_.wait_ge(ctx_raw.sem, ctx_raw.at(b, g))
                for k in range(TT):
                    for j in range(GROUP):
                        h = GROUP * g + j
                        mm = nc.tensor.matmul(ctxp[32 * j:32 * j + 32, :], vaug[:, k, h, :], pt[:, h % RING, k, :],
                                              start=(k == 0), stop=(k == TT - 1), tile_position=(0, 32 * j))
                mm.then_inc(pv_done.sem, 1)

            def turn_context(sec, b, g):
                pe_.wait_ge(ctx_raw.sem, ctx_raw.at(b, g + 1))
                bank = banks.claim(pe_, sec, ("ctx", g), b, late=True)
                for t in range(TT):
                    last = nc.tensor.transpose(bank[:, t * P:(t + 1) * P], ctxr[:, g % 2, t * P:(t + 1) * P], ident[:])
                last.then_inc(ctx_filled.sem, 1)

            def attention(sec, b, fills):
                for h in range(HEADS):
                    shifted_scores(b, h)
                    if h % GROUP == 0 and h:
                        weigh_values(b, h // GROUP - 1)
                    if h % GROUP == 2 and h > GROUP:
                        turn_context(sec, b, h // GROUP - 1)
                    if h in fills:
                        front_step(sec, b + 1, fills[h])
                weigh_values(b, NG - 1)

            def tail(sec, b):
                turn_context(sec, b, NG - 1)
                pe_.wait_ge(ctx_tok.sem, ctx_tok.at(b, NG))
                for c in range(CT):
                    bank = banks.claim(pe_, sec, ("ctxT", c), b, late=True)
                    for t in range(TT):
                        last = nc.tensor.transpose(bank[:, t * P:(t + 1) * P], ctxt[:, t, c * P:(c + 1) * P], ident[:])
                    last.then_inc(ctxT_filled.sem, 1)
                for m in range(CT):
                    bank = banks.claim(pe_, sec, ("y", m), b, late=True)
                    for k in range(CT):
                        if m == 0:
                            pe_.wait_ge(ctx_chan.sem, ctx_chan.at(b, k + 1))
                        mm = nc.tensor.matmul(bank, wo[:, k, m * P:(m + 1) * P], ctxT[:, k, :],
                                              start=(k == 0), stop=(k == CT - 1))
                    mm.then_inc(y_filled.sem, 1)

            def network_out(sec, b):
                for m in range(CT):
                    bank = banks.claim(pe_, sec, ("f2", m), b, late=True)
                    for k in range(FT):
                        if m == 0:
                            pe_.wait_ge(g_done.sem, g_done.at(b, k + 1))
                        mm = nc.tensor.matmul(bank, w2[:, k, m * P:(m + 1) * P], gT[:, k, :],
                                              start=(k == 0), stop=(k == FT - 1))
                    mm.then_inc(f2_filled.sem, 1)

            pe_.wait_ge(consts_in.sem, 16 * CONSTS)
            for fill in FRONT_FILL.values():
                if fill == "q0":
                    pe_.wait_ge(qkv_in.sem, 16 * QKV)
                front_step("first", 0, fill)
            for u in range(2):
                values("first", 0, u)
            for h in range(HEADS):
                row_maxima("first", 0, h, first=True)
            turn_maxima("first", 0)
            pe_.wait_ge(late_in.sem, 16 * LATE)

            def body(sec, i):
                attention(sec, i, FRONT_FILL)
                tail(sec, i)
                for h in range(HEADS):
                    row_maxima(sec, i + 1, h, fill=LATE_FILL.get(h))
                turn_maxima(sec, i + 1)
                network_out(sec, i)

            body("peeled", 0)
            with pe_.Fori(1, B - 1) as i:
                body("steady", i)
            attention("last", B - 1, {})
            tail("last", B - 1)
            for fill in LATE_FILL.values():
                if fill[:-1] != "v":
                    late_step("last", B - 1, fill)
            network_out("last", B - 1)

        @block.scalar
        def _(act):
            def values(sec, b, us=range(2)):
                for u in us:
                    act.wait_ge(v_filled.sem, v_filled.at(b, u + 1))
                    nc.scalar.activation(vaug[:, 2 * u:2 * u + 2, :, 0:DH],
                                         banks.bank(sec, ("v", u)).rearrange("p (t h d) -> p t h d", t=2, d=DH),
                                         ACT.Copy).then_inc(v_done.sem, 1)

            def maxima(sec, b):
                act.wait_ge(m_filled.sem, m_filled.at(b, 1))
                nc.scalar.activation(mparts[:, 0, :], banks.bank(sec, ("m",))[0:HEADS, :], ACT.Copy,
                                     scale=-1.0).then_inc(m_high.sem, 1)

            def attention(sec, b):
                for h in range(HEADS):
                    if h >= RING:
                        act.wait_ge(pv_done.sem, pv_done.at(b, (h - RING) // GROUP + 1))
                    for p in range(2):
                        act.wait_ge(score_filled.sem, score_filled.at(b, 2 * HEADS + 2 * h + p + 1))
                        nc.scalar.activation(pt[:, h % RING, 2 * p:2 * p + 2, :], score[:, p, :, :], ACT.Exp,
                                             scale=SCALE).then_inc(exp_done.sem, 1)

            def context(sec, b):
                for c in range(CT):
                    act.wait_ge(ctxT_filled.sem, ctxT_filled.at(b, c + 1))
                    nc.scalar.activation(ctxT[:, c, :], banks.bank(sec, ("ctxT", c)), ACT.Copy).then_inc(ctx_chan.sem, 1)

            def network(sec, b, more):
                if more:
                    values(sec, b + 1, (0,))
                for c in range(CT):
                    act.wait_ge(chan_filled[2].sem, chan_filled[2].at(b, c + 1))
                    nc.scalar.activation(hT[:, c, :], banks.bank(sec, ("chan", 2, c)), ACT.Identity,
                                         bias=shifts[:, 2, c:c + 1], scale=gains[:, 2, c:c + 1]).then_inc(chan_done[2].sem, 1)
                if more:
                    values(sec, b + 1, (1,))
                for m in range(FT):
                    act.wait_ge(f1_filled.sem, f1_filled.at(b, m + 1))
                    nc.scalar.activation(gT[:, m, :], banks.bank(sec, ("f1", m)), ACT.Gelu,
                                         bias=b1[:, m:m + 1]).then_inc(g_done.sem, 1)

            act.wait_ge(consts_in.sem, 16 * CONSTS)
            act.wait_ge(late_in.sem, 16 * LATE)
            act.wait_ge(ones_set.sem, 2)
            values("first", 0)
            maxima("first", 0)

            def body(sec, i):
                attention(sec, i)
                context(sec, i)
                network(sec, i, True)
                maxima(sec, i + 1)

            body("peeled", 0)
            with act.Fori(1, B - 1) as i:
                body("steady", i)
            attention("last", B - 1)
            context("last", B - 1)
            network("last", B - 1, False)

        @block.vector
        def _(dve):
            def normalise(sec, b, s):
                for u in range(2):
                    dve.wait_ge(tok_filled[s].sem, tok_filled[s].at(b, u + 1))
                    bank = banks.bank(sec, ("tok", s, u))
                    for t in range(2):
                        nc.vector.bn_stats(stats[:, s, 2 * u + t, :], bank[:, t * C:(t + 1) * C])
                nc.vector.drain()
                for t in range(TT):
                    nc.vector.bn_aggr(mv[:, s, t, :], stats[:, s, t, :])
                nc.vector.drain()
                nc.vector.tensor_scalar(vare[:, s, :], mv[:, s, :, 1], EPS, None, ALU.add).then_inc(var_done[s].sem, 1)

            def apply(sec, b, s):
                dve.wait_ge(rstd_done[s].sem, rstd_done[s].at(b, 1))
                for u in range(2):
                    bank = banks.bank(sec, ("tok", s, u))
                    for t in range(2):
                        tt = 2 * u + t
                        last = nc.vector.tensor_scalar(tokn[s][:, tt, :], bank[:, t * C:(t + 1) * C], mv[:, s, tt, 0:1],
                                                       rstd[:, s, tt:tt + 1], ALU.subtract, ALU.mult)
                    last.then_inc(tok_done[s].sem, 1)

            def to_channels(sec, b, s, dst):
                for c in range(CT):
                    dve.wait_ge(chan_filled[s].sem, chan_filled[s].at(b, c + 1))
                    nc.vector.tensor_scalar(dst[:, c, :], banks.bank(sec, ("chan", s, c)), gains[:, s, c:c + 1],
                                            shifts[:, s, c:c + 1], ALU.mult, ALU.add).then_inc(chan_done[s].sem, 1)

            def split(sec, b, name, m):
                s = "qk".index(name)
                parts = (qparts, kparts)[s]
                dve.wait_ge(qk_filled.sem, qk_filled.at(b, s * CT + m + 1))
                bank = banks.bank(sec, (name, m))
                if s == 1:
                    dve.wait_ge(low.sem, low.at(b, m + 1))
                nc.vector.tensor_copy(parts[:, 0, m, :], bank)
                nc.vector.drain()
                nc.vector.tensor_tensor(rest[:, m, :], bank, parts[:, 0, m, :], ALU.subtract).then_inc(restd.sem, 1)
                nc.vector.drain()
                nc.vector.tensor_copy(parts[:, 1, m, :], rest[:, m, :]).then_inc(mid.sem, 1)

            def front_step(sec, b, fill):
                name, n = fill[:-1], int(fill[-1])
                if name == "tok":
                    normalise(sec, b, n)
                    apply(sec, b, n)
                elif name == "chan":
                    to_channels(sec, b, n, (qnT, kvnT)[n])
                else:
                    split(sec, b, name, n)

            def row_maximum(b, h):
                for p in range(2):
                    dve.wait_ge(score_filled.sem, score_filled.at(b, 2 * h + p + 1))
                    nc.vector.tensor_reduce(mx[:, 2 * p:2 * p + 2, h], score[:, p, :, :], AX_X, ALU.max).then_inc(max_done.sem, 1)

            def divide_context(sec, b, g):
                dve.wait_ge(ctx_filled.sem, ctx_filled.at(b, g + 1))
                bank = banks.bank(sec, ("ctx", g)).rearrange("p (t j c) -> p t j c", t=TT, c=32)
                nc.vector.reciprocal(rsum[:, g, :, :], bank[:, :, :, DH])
                nc.vector.drain()
                out = ctxt[:, :, g * GROUP * DH:(g + 1) * GROUP * DH].rearrange("p t (j d) -> p t j d", d=DH)
                nc.vector.tensor_tensor(out, bank[:, :, :, 0:DH],
                                        rsum[:, g, :, :].unsqueeze(3).broadcast_to([P, TT, GROUP, DH]),
                                        ALU.mult).then_inc(ctx_tok.sem, 1)

            def maxima(sec, b):
                dve.wait_ge(m_high.sem, m_high.at(b, 1))
                nc.vector.scalar_tensor_tensor(mrest[:], banks.bank(sec, ("m",))[0:HEADS, :], -1.0, mparts[:, 0, :],
                                               ALU.mult, ALU.subtract).then_inc(m_rest.sem, 1)
                nc.vector.drain()
                nc.vector.tensor_copy(mparts[:, 1, :], mrest[:])
                nc.vector.drain()
                nc.vector.tensor_tensor(mparts[:, 2, :], mrest[:], mparts[:, 1, :], ALU.subtract).then_inc(m_low.sem, 1)

            def attention(sec, b, fills):
                nc.vector.drain()
                nc.vector.tensor_copy(rT[:], qnT[:])
                for h in range(HEADS + 1):
                    if h % GROUP == 0 and h:
                        g = h // GROUP - 1
                        dve.wait_ge(pv_done.sem, pv_done.at(b, g + 1))
                        if g > 1:
                            dve.wait_ge(ctx_filled.sem, ctx_filled.at(b, g - 1))
                        nc.vector.tensor_copy(ctxr[:, g % 2, :], ctxp[:]).then_inc(ctx_raw.sem, 1)
                    if h % GROUP == 2 and h > GROUP:
                        divide_context(sec, b, h // GROUP - 1)
                    if h in fills:
                        front_step(sec, b + 1, fills[h])

            def residual_sum(sec, b):
                divide_context(sec, b, NG - 1)
                for m in range(CT):
                    dve.wait_ge(y_filled.sem, y_filled.at(b, m + 1))
                    nc.vector.tensor_tensor(rT[:, m, :], banks.bank(sec, ("y", m)), rT[:, m, :], ALU.add).then_inc(r_done.sem, 1)

            def network_out(sec, b):
                dve.wait_ge(o_out.sem, o_out.at(b, 0))
                for m in range(CT):
                    dve.wait_ge(f2_filled.sem, f2_filled.at(b, m + 1))
                    nc.vector.scalar_tensor_tensor(outT[:, m, :], banks.bank(sec, ("f2", m)), b2[:, m:m + 1], rT[:, m, :],
                                                   ALU.add, ALU.add).then_inc(o_done.sem, 1)

            nc.vector.memset(kst[ROWS:ROWS_M, :, :], 1.0)
            nc.vector.memset(vaug[:], 0.0).then_inc(ones_set.sem, 1)
            dve.wait_ge(ones_set.sem, 1)
            nc.vector.memset(vaug[:, :, :, DH:DH + 1], 1.0).then_inc(ones_set.sem, 1)
            dve.wait_ge(consts_in.sem, 16 * CONSTS)
            for fill in FRONT_FILL.values():
                front_step("first", 0, fill)
            dve.wait_ge(late_in.sem, 16 * LATE)
            for h in range(HEADS):
                row_maximum(0, h)
            maxima("first", 0)

            def body(sec, i):
                attention(sec, i, FRONT_FILL)
                residual_sum(sec, i)
                for h in range(HEADS):
                    row_maximum(i + 1, h)
                    if h == 1:
                        normalise(sec, i, 2)
                    if h == 3:
                        apply(sec, i, 2)
                maxima(sec, i + 1)
                network_out(sec, i)

            body("peeled", 0)
            with dve.Fori(1, B - 1) as i:
                body("steady", i)
            attention("last", B - 1, {})
            residual_sum("last", B - 1)
            normalise("last", B - 1, 2)
            apply("last", B - 1, 2)
            network_out("last", B - 1)


def attention_layer(nc, sems, hid, enc_in, masks, ident_in, W, mid_out, scratch):
    B, S, D = hid.shape
    KT = D // P
    TT = S // P
    DH = D // HEADS
    SCALE = float(DH) ** -0.5
    MASKED = 10000.0
    HUGE = 3.0e38
    Q_PARTS = (0, 0, 1)
    K_PARTS = (0, 1, 0)
    ROWS = len(Q_PARTS) * DH
    HH = HEADS // 2
    G = 4
    NU = HEADS // G * TT
    SELF, CROSS = 0, 1

    def unit(u):
        half, rest = divmod(u, NU // 2)
        tile, four = divmod(rest, HH // G)
        return half, tile, four

    with ExitStack() as ctx:
        def sb(name, shape, dt=F32):
            return ctx.enter_context(nc.sbuf_tensor("b_" + name, shape, dt))

        def sig(name, per, unit=1):
            return Signal(sems, nc, "b_" + name, per, unit)

        wqkv = sb("wqkv", [P, KT, 3 * D])
        wkv = sb("wkv", [P, KT, 2 * D])
        wq2 = sb("wq2", [P, KT, D])
        wout = [sb(f"wout{a}", [P, KT, D]) for a in range(2)]
        gains = sb("gains", [P, 2, KT])
        shifts = sb("shifts", [P, 2, KT])
        bqkv = sb("bqkv", [P, 3 * KT])
        bq2 = sb("bq2", [P, KT])
        bkv = sb("bkv", [P, 2 * KT])
        bqs = sb("bqs", [P, 2, KT])
        bout = [sb(f"bout{a}", [P, D]) for a in range(2)]
        ident = sb("ident", [P, P])
        half = sb("half", [P, 1])
        mask = [sb(f"mask{a}", [P, TT, S]) for a in range(2)]
        minus = [sb(f"minus{a}", [P, TT, S]) for a in range(2)]
        xt = sb("xt", [P, TT, D])
        x1 = sb("x1", [P, TT, D])
        xn = sb("xn", [P, TT, D])
        enc = sb("enc", [P, TT, D])
        lnT = sb("lnT", [P, KT, S])
        encT = sb("encT", [P, KT, S])
        stats = sb("stats", [P, 2, TT, 6])
        mv = sb("mv", [P, 2, TT, 2])
        vare = sb("vare", [P, 2, TT])
        rstd = sb("rstd", [P, 2, TT])
        full = sb("full", [P, KT, S])
        parts = sb("parts", [P, 2, KT, S], F32R)
        qst = sb("qst", [ROWS, 2, HH, S], F32R)
        kst = sb("kst", [ROWS, 2, HH, S], F32R)
        val = [sb(f"val{a}", [P, TT, D]) for a in range(2)]
        t = sb("t", [P, 2, G, S])
        nmax = sb("nmax", [P, NU, G])
        pr = sb("pr", [P, 3, G, S])
        esum = sb("esum", [P, NU, G])
        inverse = sb("inverse", [P, NU, G])
        spread = sb("spread", [P, 2, P])
        pt = sb("pt", [P, 2, TT, G * P])
        cxT = sb("cxT", [P, KT, S])

        consts_in = sig("consts_in", 1, 16)
        qk_in = sig("qk_in", 1, 16)
        v_in = sig("v_in", 1, 16)
        mask0_in = sig("mask0_in", 1, 16)
        late_in = sig("late_in", 1, 16)
        x_in = sig("x_in", 1, 16)
        enc_load = sig("enc_load", 1, 16)
        mask_in = sig("mask_in", 1, 16)
        set_up = sig("set_up", 1)
        x_biased = [sig(f"x_biased{a}", 1) for a in range(2)]
        var_done = [sig(f"var_done{a}", 1) for a in range(2)]
        rstd_done = [sig(f"rstd_done{a}", 1) for a in range(2)]
        xn_done = [sig(f"xn_done{a}", 1) for a in range(2)]
        turn_filled = [sig(f"turn_filled{a}", 2) for a in range(2)]
        ln_done = [sig(f"ln_done{a}", KT) for a in range(2)]
        enc_filled = sig("enc_filled", 2)
        enc_done = sig("enc_done", 2)
        q_filled = [sig(f"q_filled{a}", 2) for a in range(2)]
        k_filled = [sig(f"k_filled{a}", 2) for a in range(2)]
        v_filled = [sig(f"v_filled{a}", TT) for a in range(2)]
        q_full = [sig(f"q_full{a}", KT) for a in range(2)]
        k_full = [sig(f"k_full{a}", KT) for a in range(2)]
        v_done = [sig(f"v_done{a}", TT) for a in range(2)]
        q_parts = [sig(f"q_parts{a}", 1) for a in range(2)]
        k_parts = [sig(f"k_parts{a}", 1) for a in range(2)]
        q_out = [[sig(f"q_out{a}{h}", 2, 16) for h in range(2)] for a in range(2)]
        k_out = [[sig(f"k_out{a}{h}", 2, 16) for h in range(2)] for a in range(2)]
        stacked = [[sig(f"stacked{a}{h}", 2 * len(Q_PARTS), 16) for h in range(2)] for a in range(2)]
        score_filled = [sig(f"score_filled{a}", NU) for a in range(2)]
        masked = [sig(f"masked{a}", NU) for a in range(2)]
        max_done = [sig(f"max_done{a}", NU) for a in range(2)]
        exp_done = [sig(f"exp_done{a}", NU) for a in range(2)]
        pt_filled = [sig(f"pt_filled{a}", NU * TT) for a in range(2)]
        pt_done = [sig(f"pt_done{a}", NU * TT) for a in range(2)]
        pv_done = [sig(f"pv_done{a}", NU) for a in range(2)]
        inverse_done = [sig(f"inverse_done{a}", NU) for a in range(2)]
        cx_done = [sig(f"cx_done{a}", NU) for a in range(2)]
        cxT_done = [sig(f"cxT_done{a}", KT) for a in range(2)]
        o_filled = [sig(f"o_filled{a}", TT) for a in range(2)]
        x_done = [sig(f"x_done{a}", TT) for a in range(2)]
        x_out = sig("x_out", 1, 16)

        front = [("turn", 0, u) for u in range(2)] + [("q", 0, u) for u in range(2)]
        front += [("k", 0, u) for u in range(2)]
        front_values = [("v", 0, t_) for t_ in range(TT)]
        encode = [("v", 1, t_) for t_ in range(TT)]

        def attend_uses(a, fill):
            uses = []
            for u in range(NU):
                uses += [("pt", a, u, k) for k in range(TT)] + ([("w", a, u - 1)] if u else [])
                uses += [f for f, at in fill.items() if at == u]
            return uses + [("w", a, NU - 1)]

        FILL = {("enc", 0): 1, ("enc", 1): 2, ("k", 1, 0): 3, ("k", 1, 1): 5}
        FILL_FROM = 1
        FILL_STEPS = 6

        def output_uses(a):
            return [("o", a, t_) for t_ in range(TT)]

        second = [("turn", 1, u) for u in range(2)] + [("q", 1, u) for u in range(2)]
        before = attend_uses(0, {}) + output_uses(0) + encode + second
        late = before + attend_uses(1, {}) + output_uses(1)
        order_last = late
        order_steady = before + front + front_values + attend_uses(1, FILL) + output_uses(1)
        read = {("enc", u): (enc_done, u + 1) for u in range(2)}
        for a in range(2):
            read |= {("turn", a, u): (ln_done[a], 2 * u + 2) for u in range(2)}
            read |= {("q", a, u): (q_full[a], 2 * u + 2) for u in range(2)}
            read |= {("k", a, u): (k_full[a], 2 * u + 2) for u in range(2)}
            read |= {("v", a, t_): (v_done[a], t_ + 1) for t_ in range(TT)}
            read |= {("pt", a, u, k): (pt_done[a], u * TT + k + 1) for u in range(NU) for k in range(TT)}
            read |= {("w", a, u): (cx_done[a], u + 1) for u in range(NU)}
            read |= {("o", a, t_): (x_done[a], t_ + 1) for t_ in range(TT)}
        read = {u: (*r, u in late) for u, r in read.items()}
        banks = Banks(ctx, nc, "b_d", 4, read, first=front + front_values + list(FILL), steady=order_steady, last=order_last)
        score = ctx.enter_context(nc.psum_tensor("b_score", [P, 2, 2, BANK], F32))
        CONSTS, LATE = 8, 6

        block = ctx.enter_context(nc.Block())

        @block.sync
        def _(sp):
            def load(dst, src, columns=False, signal=consts_in):
                sp.dma_start(dst, src, allow_slow_non_contiguous=columns).then_inc(signal.sem, 16)

            def tokens(v):
                return v.rearrange("(t p) n -> p t n", p=P)

            sp.dma_start(xt[:], tokens(hid[0])).then_inc(x_in.sem, 16)
            load(ident[:], ident_in)
            for a, n in enumerate(("ln1", "ln2")):
                load(gains[:, a, :], rowwise(W[n + "_s"], KT), True)
                load(shifts[:, a, :], rowwise(W[n + "_b"], KT), True)
            load(bqkv[:], rowwise(W["b_qkv"], 3 * KT), True)
            load(bq2[:], rowwise(W["b_q"], KT), True)
            load(bkv[:], rowwise(W["b_kv"], 2 * KT), True)
            for n in range(3):
                columns = slice(n * D, (n + 1) * D)
                load(wqkv[:, :, columns], W["w_qkv"].rearrange("(k p) n -> p k n", p=P)[:, :, columns], signal=(qk_in, qk_in, v_in)[n])
            load(mask[0][:], tokens(masks[0][0, 0]), signal=mask0_in)
            for dst, n in ((wkv, "w_kv"), (wout[0], "w_ao"), (wq2, "w_q"), (wout[1], "w_co")):
                load(dst[:], W[n].rearrange("(k p) n -> p k n", p=P), signal=late_in)
            for a, n in enumerate(("b_ao", "b_co")):
                load(bout[a][:], W[n].rearrange("(a n) -> a n", a=1).broadcast_to([P, D]), signal=late_in)
            sp.dma_start(enc[:], tokens(enc_in[0])).then_inc(enc_load.sem, 16)
            sp.dma_start(mask[1][:], tokens(masks[1][0, 0])).then_inc(mask_in.sem, 16)

            def put(a, b, which, h):
                ready, out = (q_parts, q_out) if which == 0 else (k_parts, k_out)
                tiles = slice(h * KT // 2, (h + 1) * KT // 2)
                sp.wait_ge(ready[a].sem, ready[a].at(b, 1))
                for part in range(2):
                    sp.dma_start(scratch[a][which][b, part].rearrange("(k p) n -> p k n", p=P)[:, tiles, :],
                                 parts[:, part, tiles, :].bitcast(F32)).then_inc(out[a][h].sem, 16)

            def stack(a, b, which, h, first=False):
                if a == SELF:
                    if not first:
                        sp.wait_ge(score_filled[CROSS].sem, score_filled[CROSS].at(b - 1, (h + 1) * NU // 2))
                else:
                    sp.wait_ge(score_filled[SELF].sem, score_filled[SELF].at(b, (h + 1) * NU // 2))
                out, st, order = ((q_out, qst, Q_PARTS), (k_out, kst, K_PARTS))[which]
                sp.wait_ge(out[a][h].sem, out[a][h].at(b, 2))
                for c, part in enumerate(order):
                    sp.dma_start(st[c * DH:(c + 1) * DH, h, :, :].bitcast(F32),
                                 scratch[a][which][b, part, h * HH * DH:(h + 1) * HH * DH, :].rearrange(
                                     "(h d) n -> d h n", d=DH)).then_inc(stacked[a][h].sem, 16)

            def front_puts(b):
                for which in range(2):
                    for h in range(2):
                        put(SELF, b, which, h)

            def late_steps(b, more):
                if more:
                    sp.wait_ge(enc_filled.sem, enc_filled.at(b, 2))
                    sp.dma_start(enc[:], tokens(enc_in[b + 1])).then_inc(enc_load.sem, 16)
                for h in range(2):
                    stack(CROSS, b, 1, h)
                if more:
                    sp.wait_ge(x_done[0].sem, x_done[0].at(b, TT))
                    sp.dma_start(xt[:], tokens(hid[b + 1])).then_inc(x_in.sem, 16)
                for h in range(2):
                    put(CROSS, b, 0, h)
                for h in range(2):
                    stack(CROSS, b, 0, h)
                if more:
                    front_puts(b + 1)
                    for h in range(2):
                        if h == 1:
                            keys_puts(b + 1)
                        for which in range(2):
                            stack(SELF, b + 1, which, h)
                    sp.wait_ge(max_done[CROSS].sem, max_done[CROSS].at(b, NU))
                    sp.dma_start(mask[1][:], tokens(masks[1][b + 1, 0])).then_inc(mask_in.sem, 16)
                sp.wait_ge(x_done[1].sem, x_done[1].at(b, TT))
                sp.dma_start(tokens(mid_out[b]), x1[:]).then_inc(x_out.sem, 16)

            def keys_puts(b):
                for h in range(2):
                    put(CROSS, b, 1, h)

            front_puts(0)
            for h in range(2):
                for which in range(2):
                    stack(SELF, 0, which, h, first=True)
            keys_puts(0)
            late_steps(0, True)
            with sp.Fori(1, B - 1) as i:
                late_steps(i, True)
            late_steps(B - 1, False)
            sp.wait_ge(x_out.sem, x_out.at(B, 0))

        @block.gpsimd
        def _(pool):
            nc.gpsimd.memset(half[:], -0.5)
            nc.gpsimd.drain()

            def rsqrt(b, a):
                pool.wait_ge(var_done[a].sem, var_done[a].at(b, 1))
                nc.gpsimd.tensor_tensor(rstd[:, a, :], vare[:, a, :], half[:].broadcast_to([P, TT]),
                                        ALU.pow).then_inc(rstd_done[a].sem, 1)

            def add_bias(b, a, x):
                pool.wait_ge(xn_done[a].sem, xn_done[a].at(b, 1))
                nc.gpsimd.tensor_tensor(x[:], x[:], bout[a][:].unsqueeze(1).broadcast_to([P, TT, D]),
                                        ALU.add).then_inc(x_biased[a].sem, 1)

            rsqrt(0, 0)
            pool.wait_ge(late_in.sem, 16 * LATE)
            add_bias(0, 0, xt)

            def body(sec, i):
                rsqrt(i, 1)
                add_bias(i, 1, x1)
                rsqrt(i + 1, 0)
                add_bias(i + 1, 0, xt)

            body("peeled", 0)
            with pool.Fori(1, B - 1) as i:
                body("steady", i)
            rsqrt(B - 1, 1)
            add_bias(B - 1, 1, x1)

        @block.tensor
        def _(pe):
            def turn(sec, b, use, src, filled, us=range(2)):
                for u in us:
                    bank = banks.claim(pe, sec, use + (u,), b, late=use == ("turn", 1))
                    for j in range(2):
                        for t_ in range(TT):
                            k = 2 * u + j
                            last = nc.tensor.transpose(bank[:, (j * TT + t_) * P:(j * TT + t_ + 1) * P],
                                                       src[:, t_, k * P:(k + 1) * P], ident[:])
                    last.then_inc(filled.sem, 1)

            def project(sec, b, use, w, col, src, filled, is_late, steps=range(4), ready=None):
                for n in steps:
                    u, j = divmod(n, 2)
                    bank = banks.claim(pe, sec, use + (u,), b, late=is_late) if j == 0 else banks.bank(sec, use + (u,))
                    m = col + n * P
                    for k in range(KT):
                        if n == 0 and ready:
                            pe.wait_ge(ready.sem, ready.at(b, k + 1))
                        mm = nc.tensor.matmul(bank[:, j * S:(j + 1) * S], w[:, k, m:m + P], src[:, k, :],
                                              start=(k == 0), stop=(k == KT - 1))
                    if j == 1:
                        mm.then_inc(filled.sem, 1)

            def by_token(sec, b, use, w, col, src, filled, is_late, ready=None):
                for t_ in range(TT):
                    bank = banks.claim(pe, sec, use + (t_,), b, late=is_late)
                    for k in range(KT):
                        if t_ == 0 and ready:
                            pe.wait_ge(ready.sem, ready.at(b, k + 1))
                        mm = nc.tensor.matmul(bank, src[:, k, t_ * P:(t_ + 1) * P], w[:, k, col:col + D],
                                              start=(k == 0), stop=(k == KT - 1))
                    mm.then_inc(filled.sem, 1)

            def front_turn(sec, b):
                pe.wait_ge(xn_done[0].sem, xn_done[0].at(b, 1))
                turn(sec, b, ("turn", 0), xn, turn_filled[0])

            def front_project(sec, b):
                project(sec, b, ("q", 0), wqkv, 0, lnT, q_filled[0], False, ready=ln_done[0])
                project(sec, b, ("k", 0), wqkv, D, lnT, k_filled[0], False)

            def front_values(sec, b):
                by_token(sec, b, ("v", 0), wqkv, 2 * D, lnT, v_filled[0], False)

            def encoder_step(sec, b, u):
                if 0 <= u < 2:
                    if u == 0:
                        pe.wait_ge(enc_load.sem, enc_load.at(b, 1))
                    turn(sec, b, ("enc",), enc, enc_filled, (u,))
                elif 2 <= u < 6:
                    if u == 2:
                        pe.wait_ge(enc_done.sem, enc_done.at(b, 2))
                    project(sec, b, ("k", 1), wkv, 0, encT, k_filled[1], False, (u - 2,))

            def cross_values(sec, b):
                by_token(sec, b, ("v", 1), wkv, D, encT, v_filled[1], True)

            def scores(b, a, u, first=False):
                h, q, four = unit(u)
                if u % (NU // 2) == 0:
                    pe.wait_ge(stacked[a][h].sem, stacked[a][h].at(b, 2 * len(Q_PARTS)))
                if u >= 2:
                    pe.wait_ge(masked[a].sem, masked[a].at(b, u - 1))
                elif a == CROSS:
                    pe.wait_ge(masked[SELF].sem, masked[SELF].at(b, NU - 1 + u))
                elif not first:
                    pe.wait_ge(masked[CROSS].sem, masked[CROSS].at(b - 1, NU - 1 + u))
                for j in range(G):
                    hh = four * G + j
                    mm = nc.tensor.matmul(score[:, u % 2, j // 2, (j % 2) * S:(j % 2 + 1) * S],
                                          qst[:, h, hh, q * P:(q + 1) * P], kst[:, h, hh, :],
                                          start=True, stop=True)
                mm.then_inc(score_filled[a].sem, 1)

            def attend(sec, b, a, fill=None):
                def turn_probs(u):
                    pe.wait_ge(exp_done[a].sem, exp_done[a].at(b, u + 1))
                    for k in range(TT):
                        bank = banks.claim(pe, sec, ("pt", a, u, k), b, late=True)
                        for j in range(G):
                            last = nc.tensor.transpose(bank[:, j * P:(j + 1) * P], pr[:, u % 3, j, k * P:(k + 1) * P], ident[:])
                        last.then_inc(pt_filled[a].sem, 1)

                def weigh(u):
                    h, q, four = unit(u)
                    pe.wait_ge(pt_done[a].sem, pt_done[a].at(b, (u + 1) * TT))
                    if u == 0:
                        pe.wait_ge(v_done[a].sem, v_done[a].at(b, TT))
                    bank = banks.claim(pe, sec, ("w", a, u), b, late=True)
                    for k in range(TT):
                        for j in range(G):
                            head = (h * HH + four * G + j) * DH
                            nc.tensor.matmul(bank[j * DH:(j + 1) * DH, 0:P], val[a][:, k, head:head + DH],
                                             pt[:, u % 2, k, j * P:(j + 1) * P],
                                             start=(k == 0), stop=(k == TT - 1), tile_position=(0, j * DH))
                    pe.wait_ge(inverse_done[a].sem, inverse_done[a].at(b, u + 1))
                    for j in range(G):
                        mm = nc.tensor.matmul(bank[j * DH:(j + 1) * DH, P:2 * P], inverse[:, u, j:j + 1].broadcast_to([P, DH]), ident[:],
                                              start=True, stop=True, tile_position=(0, j * DH))
                    mm.then_inc(pv_done[a].sem, 1)

                for u in range(NU):
                    if u + 2 < NU:
                        scores(b, a, u + 2)
                    turn_probs(u)
                    if u:
                        weigh(u - 1)
                    if fill:
                        fill(sec, b + 1, u - FILL_FROM)
                weigh(NU - 1)

            def output(sec, b, a):
                by_token(sec, b, ("o", a), wout[a], 0, cxT, o_filled[a], True, ready=cxT_done[a])

            def second(sec, b):
                pe.wait_ge(xn_done[1].sem, xn_done[1].at(b, 1))
                turn(sec, b, ("turn", 1), xn, turn_filled[1])
                project(sec, b, ("q", 1), wq2, 0, lnT, q_filled[1], True, ready=ln_done[1])

            pe.wait_ge(consts_in.sem, 16 * CONSTS)
            front_turn("first", 0)
            pe.wait_ge(qk_in.sem, 32)
            front_project("first", 0)
            pe.wait_ge(v_in.sem, 16)
            front_values("first", 0)
            pe.wait_ge(late_in.sem, 16 * LATE)
            for u in range(FILL_STEPS):
                encoder_step("first", 0, u)
            scores(0, SELF, 0, first=True)
            scores(0, SELF, 1, first=True)

            def late_steps(sec, b, more):
                attend(sec, b, SELF)
                output(sec, b, SELF)
                cross_values(sec, b)
                second(sec, b)
                if more:
                    front_turn(sec, b + 1)
                    front_project(sec, b + 1)
                scores(b, CROSS, 0)
                scores(b, CROSS, 1)
                if more:
                    front_values(sec, b + 1)
                attend(sec, b, CROSS, encoder_step if more else None)
                if more:
                    scores(b + 1, SELF, 0)
                    scores(b + 1, SELF, 1)
                output(sec, b, CROSS)

            late_steps("peeled", 0, True)
            with pe.Fori(1, B - 1) as i:
                late_steps("steady", i, True)
            late_steps("last", B - 1, False)

        @block.scalar
        def _(act):
            def turned(sec, b, a):
                for k in range(KT):
                    act.wait_ge(turn_filled[a].sem, turn_filled[a].at(b, k // 2 + 1))
                    bank = banks.bank(sec, ("turn", a, k // 2))
                    nc.scalar.activation(lnT[:, k, :], bank[:, (k % 2) * S:(k % 2 + 1) * S], ACT.Identity,
                                         bias=shifts[:, a, k:k + 1], scale=gains[:, a, k:k + 1]).then_inc(ln_done[a].sem, 1)

            def biased(sec, b, use, a, filled, done, bias, scale, tiles=range(KT)):
                for k in tiles:
                    act.wait_ge(filled[a].sem, filled[a].at(b, k // 2 + 1))
                    bank = banks.bank(sec, (use, a, k // 2))
                    nc.scalar.activation(full[:, k, :], bank[:, (k % 2) * S:(k % 2 + 1) * S], ACT.Identity,
                                         bias=bias[:, k:k + 1], scale=scale).then_inc(done[a].sem, 1)

            def front(sec, b, first):
                if not first:
                    act.wait_ge(q_filled[1].sem, q_filled[1].at(b - 1, 2))
                turned(sec, b, 0)
                if not first:
                    act.wait_ge(q_parts[1].sem, q_parts[1].at(b - 1, 1))
                biased(sec, b, "q", 0, q_filled, q_full, bqs[:, 0, :], SCALE)
                act.wait_ge(q_parts[0].sem, q_parts[0].at(b, 1))
                biased(sec, b, "k", 0, k_filled, k_full, bqkv[:, KT:2 * KT], 1.0)

            def values(sec, b, a, tiles=range(TT)):
                for t_ in tiles:
                    act.wait_ge(v_filled[a].sem, v_filled[a].at(b, t_ + 1))
                    nc.scalar.activation(val[a][:, t_, :], banks.bank(sec, ("v", a, t_)), ACT.Copy).then_inc(v_done[a].sem, 1)

            def encoder_step(sec, b, u):
                if 0 <= u < 2:
                    act.wait_ge(enc_filled.sem, enc_filled.at(b, u + 1))
                    nc.scalar.activation(encT[:, 2 * u:2 * u + 2, :], banks.bank(sec, ("enc", u)).rearrange("p (k n) -> p k n", k=2),
                                         ACT.Copy).then_inc(enc_done.sem, 1)
                elif u in (3, 5):
                    if u == 3:
                        act.wait_ge(k_parts[0].sem, k_parts[0].at(b, 1))
                    biased(sec, b, "k", 1, k_filled, k_full, bkv[:, 0:KT], 1.0, (u - 3, u - 2))

            def exponentials(b, a, u, first=False):
                act.wait_ge(max_done[a].sem, max_done[a].at(b, u + 1))
                if u >= 3:
                    act.wait_ge(pt_filled[a].sem, pt_filled[a].at(b, (u - 2) * TT))
                elif a == CROSS:
                    act.wait_ge(pt_filled[SELF].sem, pt_filled[SELF].at(b, NU * TT))
                elif not first:
                    act.wait_ge(pt_filled[CROSS].sem, pt_filled[CROSS].at(b - 1, NU * TT))
                for j in range(G):
                    last = nc.scalar.activation(pr[:, u % 3, j, :], t[:, u % 2, j, :], ACT.Exp, scale=-1.0,
                                                bias=nmax[:, u, j:j + 1], accum_out=esum[:, u, j:j + 1])
                last.then_inc(exp_done[a].sem, 1)

            def attend(sec, b, a, fill=None):
                def keep(u):
                    for k in range(TT):
                        act.wait_ge(pt_filled[a].sem, pt_filled[a].at(b, u * TT + k + 1))
                        if k == 0:
                            if u >= 2:
                                act.wait_ge(pv_done[a].sem, pv_done[a].at(b, u - 1))
                        nc.scalar.activation(pt[:, u % 2, k, :], banks.bank(sec, ("pt", a, u, k)), ACT.Copy).then_inc(pt_done[a].sem, 1)

                exponentials(b, a, 1)
                for u in range(NU):
                    keep(u)
                    if u + 2 < NU:
                        exponentials(b, a, u + 2)
                    if fill:
                        fill(sec, b + 1, u - FILL_FROM)

            def output(sec, b, a):
                bias = bqkv[:, 2 * KT:3 * KT] if a == SELF else bkv[:, KT:2 * KT]
                for k in range(KT):
                    act.wait_ge(cx_done[a].sem, cx_done[a].at(b, k // 2 * (NU // 2) + NU // 2 - 1 + k % 2))
                    nc.scalar.activation(cxT[:, k, :], cxT[:, k, :], ACT.Identity, bias=bias[:, k:k + 1]).then_inc(cxT_done[a].sem, 1)

            def second(sec, b):
                turned(sec, b, 1)
                act.wait_ge(k_parts[1].sem, k_parts[1].at(b, 1))
                biased(sec, b, "q", 1, q_filled, q_full, bqs[:, 1, :], SCALE)

            act.wait_ge(consts_in.sem, 16 * CONSTS)
            act.wait_ge(set_up.sem, 2)
            front("first", 0, True)
            values("first", 0, 0)
            for u in range(FILL_STEPS):
                encoder_step("first", 0, u)
            exponentials(0, SELF, 0, first=True)

            def late_steps(sec, b, more):
                attend(sec, b, SELF)
                output(sec, b, SELF)
                values(sec, b, 1)
                second(sec, b)
                if more:
                    front(sec, b + 1, False)
                exponentials(b, CROSS, 0)
                if more:
                    values(sec, b + 1, 0)
                attend(sec, b, CROSS, encoder_step if more else None)
                output(sec, b, CROSS)
                if more:
                    exponentials(b + 1, SELF, 0)

            late_steps("peeled", 0, True)
            with act.Fori(1, B - 1) as i:
                late_steps("steady", i, True)
            late_steps("last", B - 1, False)

        @block.vector
        def _(dve):
            def normalise(b, a, x):
                for t_ in range(TT):
                    nc.vector.bn_stats(stats[:, a, t_, :], x[:, t_, :])
                nc.vector.drain()
                for t_ in range(TT):
                    nc.vector.bn_aggr(mv[:, a, t_, :], stats[:, a, t_, :])
                nc.vector.drain()
                nc.vector.tensor_scalar(vare[:, a, :], mv[:, a, :, 1], EPS, None, ALU.add).then_inc(var_done[a].sem, 1)

            def apply(b, a, x):
                dve.wait_ge(rstd_done[a].sem, rstd_done[a].at(b, 1))
                for t_ in range(TT):
                    last = nc.vector.tensor_scalar(xn[:, t_, :], x[:, t_, :], mv[:, a, t_, 0:1], rstd[:, a, t_:t_ + 1],
                                                   ALU.subtract, ALU.mult)
                last.then_inc(xn_done[a].sem, 1)

            def split(b, full_done, ready, out=None, out_b=None):
                dve.wait_ge(full_done.sem, full_done.at(b, KT))
                if out is not None:
                    for half_out in out:
                        dve.wait_ge(half_out.sem, half_out.at(out_b, 2))
                nc.vector.tensor_copy(parts[:, 0], full[:])
                nc.vector.drain()
                nc.vector.tensor_tensor(parts[:, 1], full[:], parts[:, 0].bitcast(F32), ALU.subtract).then_inc(ready.sem, 1)

            def front_norm(b):
                dve.wait_ge(x_in.sem, x_in.at(b, 1))
                normalise(b, 0, xt)

            def front_apply(b, first):
                if not first:
                    dve.wait_ge(turn_filled[1].sem, turn_filled[1].at(b - 1, 2))
                apply(b, 0, xt)

            def front_split(b, first):
                if first:
                    split(b, q_full[0], q_parts[0])
                else:
                    split(b, q_full[0], q_parts[0], q_out[1], b - 1)
                split(b, k_full[0], k_parts[0], q_out[0], b)

            def negative(b):
                nc.vector.tensor_scalar(minus[1][:], mask[1][:], 1.0, MASKED, ALU.subtract, ALU.mult)

            def soften(b, a, u, first=False):
                h, q, four = unit(u)
                dve.wait_ge(score_filled[a].sem, score_filled[a].at(b, u + 1))
                if u >= 2:
                    dve.wait_ge(exp_done[a].sem, exp_done[a].at(b, u - 1))
                elif a == CROSS:
                    dve.wait_ge(exp_done[SELF].sem, exp_done[SELF].at(b, NU - 1 + u))
                elif not first:
                    dve.wait_ge(exp_done[CROSS].sem, exp_done[CROSS].at(b - 1, NU - 1 + u))
                nc.vector.tensor_tensor(t[:, u % 2], score[:, u % 2].rearrange("p x (y n) -> p (x y) n", y=2),
                                        mask[a][:, q, :].unsqueeze(1).broadcast_to([P, G, S]), ALU.mult).then_inc(masked[a].sem, 1)
                nc.vector.drain()
                for j in range(G):
                    last = nc.vector.tensor_tensor_reduce(t[:, u % 2, j, :], t[:, u % 2, j, :], minus[a][:, q, :], -1.0, HUGE,
                                                          ALU.add, ALU.min, accum_out=nmax[:, u, j:j + 1])
                last.then_inc(max_done[a].sem, 1)

            def attend(sec, b, a, more=False):
                def invert(u):
                    dve.wait_ge(exp_done[a].sem, exp_done[a].at(b, u + 1))
                    nc.vector.reciprocal(inverse[:, u, :], esum[:, u, :]).then_inc(inverse_done[a].sem, 1)

                def divide(u):
                    h, q, four = unit(u)
                    dve.wait_ge(pv_done[a].sem, pv_done[a].at(b, u + 1))
                    if u == 0 and a == CROSS:
                        dve.wait_ge(o_filled[SELF].sem, o_filled[SELF].at(b, TT))
                    bank = banks.bank(sec, ("w", a, u))
                    nc.vector.tensor_copy(spread[:, u % 2, :], bank[:, P:2 * P])
                    nc.vector.drain()
                    nc.vector.tensor_tensor(cxT[:, 2 * h + four, q * P:(q + 1) * P], bank[:, 0:P], spread[:, u % 2, :],
                                            ALU.mult).then_inc(cx_done[a].sem, 1)

                invert(0)
                for u in range(2, NU):
                    soften(b, a, u)
                    if u > 2:
                        divide(u - 3)
                    invert(u - 1)
                divide(NU - 3)
                if a == CROSS and more:
                    split(b + 1, k_full[1], k_parts[1], k_out[0], b + 1)
                divide(NU - 2)
                invert(NU - 1)
                divide(NU - 1)

            def output(sec, b, a):
                dve.wait_ge(x_biased[a].sem, x_biased[a].at(b, 1))
                if a == SELF:
                    dve.wait_ge(x_out.sem, x_out.at(b, 0))
                x = xt if a == SELF else x1
                for t_ in range(TT):
                    dve.wait_ge(o_filled[a].sem, o_filled[a].at(b, t_ + 1))
                    nc.vector.tensor_tensor(x1[:, t_, :], banks.bank(sec, ("o", a, t_)), x[:, t_, :], ALU.add).then_inc(x_done[a].sem, 1)

            def second_norm(b):
                dve.wait_ge(x_done[0].sem, x_done[0].at(b, TT))
                normalise(b, 1, x1)
                apply(b, 1, x1)

            dve.wait_ge(consts_in.sem, 16 * CONSTS)
            nc.vector.tensor_scalar(bqs[:, 0, :], bqkv[:, 0:KT], SCALE, None, ALU.mult).then_inc(set_up.sem, 1)
            nc.vector.tensor_scalar(bqs[:, 1, :], bq2[:], SCALE, None, ALU.mult).then_inc(set_up.sem, 1)
            dve.wait_ge(set_up.sem, 2)
            front_norm(0)
            front_apply(0, True)
            front_split(0, True)
            split(0, k_full[1], k_parts[1], k_out[0], 0)
            dve.wait_ge(mask0_in.sem, 16)
            nc.vector.tensor_scalar(minus[0][:], mask[0][:], 1.0, MASKED, ALU.subtract, ALU.mult)
            soften(0, SELF, 0, first=True)
            soften(0, SELF, 1, first=True)

            def late_steps(sec, b, more):
                attend(sec, b, SELF)
                output(sec, b, SELF)
                second_norm(b)
                dve.wait_ge(mask_in.sem, mask_in.at(b, 1))
                negative(b)
                if more:
                    front_norm(b + 1)
                if more:
                    front_apply(b + 1, False)
                split(b, q_full[1], q_parts[1], k_out[1], b)
                if more:
                    front_split(b + 1, False)
                soften(b, CROSS, 0)
                soften(b, CROSS, 1)
                attend(sec, b, CROSS, more)
                if more:
                    soften(b + 1, SELF, 0)
                    soften(b + 1, SELF, 1)
                output(sec, b, CROSS)

            late_steps("peeled", 0, True)
            with dve.Fori(1, B - 1) as i:
                late_steps("steady", i, True)
            late_steps("last", B - 1, False)


def network_layer(nc, sems, mid_in, ident_in, W, out):
    B, S, D = mid_in.shape
    KT = D // P
    TT = S // P
    F = W["w1"].shape[1]
    FT = F // P
    NP = FT // 2
    RING = 3
    CHUNK = 2 * P * KT
    SLOTS = 3
    LAG = 2
    with ExitStack() as ctx:
        def sb(name, shape, dt=F32):
            return ctx.enter_context(nc.sbuf_tensor("c_" + name, shape, dt))

        def sig(name, per, unit=1):
            return Signal(sems, nc, "c_" + name, per, unit)

        w1 = [sb(f"w1_{n}", [P, KT, F], F32R) for n in ("high", "low")]
        w2 = [sb(f"w2_{n}", [P, FT, D], F32R) for n in ("high", "low")]
        gain = sb("gain", [P, KT])
        shift = sb("shift", [P, KT])
        b1 = sb("b1", [P, FT])
        b2 = sb("b2", [P, D])
        ident = sb("ident", [P, P])
        half = sb("half", [P, 1])
        xt = sb("xt", [P, TT, D])
        xn = sb("xn", [P, TT, D])
        stage = sb("stage", [P, SLOTS, CHUNK])
        stats = sb("stats", [P, TT, 6])
        mv = sb("mv", [P, TT, 2])
        vare = sb("vare", [P, TT])
        rstd = sb("rstd", [P, TT])
        lnT = sb("lnT", [P, KT, S])
        lnp = [sb(f"ln_{n}", [P, KT, S], F32R) for n in ("high", "low")]
        gT = sb("gT", [P, 2, 2 * S])
        gp = [sb(f"g_{n}", [P, RING, 2 * S], F32R) for n in ("high", "low")]
        res = sb("res", [P, TT, D])

        consts_in = sig("consts_in", 1, 16)
        chunk_in = [sig(f"chunk_in{n}", 1, 16) for n in range(SLOTS)]
        chunk_high = sig("chunk_high", 1)
        chunk_split = sig("chunk_split", 1)
        x_in = sig("x_in", 1, 16)
        var_done = sig("var_done", 1)
        rstd_done = sig("rstd_done", 1)
        xn_done = sig("xn_done", 1)
        xb_done = sig("xb_done", 1)
        turn_filled = sig("turn_filled", 2)
        ln_full = sig("ln_full", 2)
        ln_split = sig("ln_split", 2)
        f1_filled = sig("f1_filled", NP)
        g_full = sig("g_full", NP)
        g_split = sig("g_split", NP)
        g_used = sig("g_used", NP - 1)
        f2_filled = sig("f2_filled", TT)
        res_done = sig("res_done", TT)
        x_out = sig("x_out", 1, 16)

        turns = [("turn", u) for u in range(2)]
        ups = [("f1", u) for u in range(NP)]
        read = {("turn", u): (ln_full, u + 1, False) for u in range(2)}
        read |= {("f1", u): (g_full, u + 1, True) for u in range(NP)}
        banks = Banks(ctx, nc, "c_d", 6, read, first=turns, steady=ups + turns, last=ups)
        sums = ctx.enter_context(nc.psum_tensor("c_sums", [P, TT, BANK], F32))

        block = ctx.enter_context(nc.Block())

        def tokens(v):
            return v.rearrange("(t p) n -> p t n", p=P)

        behind = [[(0, 0), (0, 1), (0, 2)], []]
        behind += [[(1, u - LAG)] + [(0, u + 1)] * (u + 1 < NP) for u in range(2, NP)]
        behind += [[(1, u) for u in range(NP - LAG, NP)]]
        chunks = [c for some in behind for c in some]

        def chunk(c, w1s, w2s):
            which, u = c
            return w2s[:, 2 * u:2 * u + 2, :] if which else w1s[:, :, 2 * u * P:2 * (u + 1) * P]

        def staged(c):
            return stage[:, chunks.index(c) % SLOTS, :].rearrange("p (k n) -> p k n", k=2 if c[0] else KT)

        @block.sync
        def _(sp):
            def load(dst, src, columns=False):
                sp.dma_start(dst, src, allow_slow_non_contiguous=columns).then_inc(consts_in.sem, 16)

            sp.dma_start(xt[:], tokens(mid_in[0])).then_inc(x_in.sem, 16)
            load(ident[:], ident_in)
            load(gain[:], rowwise(W["ln3_s"], KT), True)
            load(shift[:], rowwise(W["ln3_b"], KT), True)
            load(b1[:], rowwise(W["b1"], FT), True)
            load(b2[:], W["b2"].rearrange("(a n) -> a n", a=1).broadcast_to([P, D]))
            def fetch(b):
                sp.wait_ge(xb_done.sem, xb_done.at(b - 1, 1))
                sp.dma_start(xt[:], tokens(mid_in[b])).then_inc(x_in.sem, 16)

            for n, c in enumerate(chunks):
                if n == SLOTS:
                    fetch(1)
                if n >= SLOTS:
                    sp.wait_ge(chunk_split.sem, n - SLOTS + 1)
                src = chunk(c, W["w1"].rearrange("(k p) n -> p k n", p=P), W["w2"].rearrange("(k p) n -> p k n", p=P))
                sp.dma_start(staged(c), src).then_inc(chunk_in[n % SLOTS].sem, 16)

            def store(b):
                sp.wait_ge(res_done.sem, res_done.at(b, TT))
                sp.dma_start(tokens(out[b]), res[:]).then_inc(x_out.sem, 16)

            store(0)
            with sp.Fori(1, B - 1) as i:
                fetch(i + 1)
                store(i)
            store(B - 1)
            sp.wait_ge(x_out.sem, x_out.at(B, 0))

        @block.gpsimd
        def _(pool):
            nc.gpsimd.memset(half[:], -0.5)
            nc.gpsimd.drain()
            pool.wait_ge(consts_in.sem, 16 * 5)

            def steps(b, first=False):
                pool.wait_ge(var_done.sem, var_done.at(b, 1))
                nc.gpsimd.tensor_tensor(rstd[:], vare[:], half[:].broadcast_to([P, TT]), ALU.pow).then_inc(rstd_done.sem, 1)
                pool.wait_ge(xn_done.sem, xn_done.at(b, 1))
                if not first:
                    pool.wait_ge(x_out.sem, x_out.at(b - 1, 1))
                nc.gpsimd.tensor_tensor(res[:], xt[:], b2[:].unsqueeze(1).broadcast_to([P, TT, D]), ALU.add).then_inc(xb_done.sem, 1)

            steps(0, first=True)
            with pool.Fori(0, B - 1) as i:
                steps(i + 1)

        @block.tensor
        def _(pe):
            def turn(sec, b):
                pe.wait_ge(xn_done.sem, xn_done.at(b, 1))
                for u in range(2):
                    bank = banks.claim(pe, sec, ("turn", u), b)
                    for j in range(2):
                        for t_ in range(TT):
                            k = 2 * u + j
                            last = nc.tensor.transpose(bank[:, (j * TT + t_) * P:(j * TT + t_ + 1) * P],
                                                       xn[:, t_, k * P:(k + 1) * P], ident[:])
                    last.then_inc(turn_filled.sem, 1)

            def up(sec, b, u):
                if u == 0:
                    pe.wait_ge(ln_split.sem, ln_split.at(b, 2))
                bank = banks.claim(pe, sec, ("f1", u), b, late=True)
                for j in range(2):
                    m = (2 * u + j) * P
                    for k in range(KT):
                        for n, (w, v) in enumerate(((0, 0), (0, 1), (1, 0))):
                            mm = nc.tensor.matmul(bank[:, j * S:(j + 1) * S], w1[w][:, k, m:m + P], lnp[v][:, k, :],
                                                  start=(k == 0 and n == 0), stop=(k == KT - 1 and n == 2))
                mm.then_inc(f1_filled.sem, 1)

            def down(b, u, first=False):
                pe.wait_ge(g_split.sem, g_split.at(b, u + 1))
                if u == 0 and not first:
                    pe.wait_ge(res_done.sem, res_done.at(b - 1, TT))
                for t_ in range(TT):
                    for j in range(2):
                        k = 2 * u + j
                        for n, (v, w) in enumerate(((0, 0), (0, 1), (1, 0))):
                            at = j * S + t_ * P
                            mm = nc.tensor.matmul(sums[:, t_, :], gp[v][:, u % RING, at:at + P], w2[w][:, k, :],
                                                  start=(k == 0 and n == 0), stop=(k == FT - 1 and n == 2))
                    if u == NP - 1:
                        mm.then_inc(f2_filled.sem, 1)
                if u < NP - 1:
                    mm.then_inc(g_used.sem, 1)

            def network(sec, b, more, first=False):
                for u in range(NP):
                    up(sec, b, u)
                    if u >= LAG:
                        down(b, u - LAG, first)
                if more:
                    turn(sec, b + 1)
                for u in range(NP - LAG, NP):
                    down(b, u, first)

            pe.wait_ge(consts_in.sem, 16 * 5)
            turn("first", 0)
            for u in range(NP):
                pe.wait_ge(chunk_split.sem, chunks.index((0, u)) + 1)
                up("peeled", 0, u)
                if u >= LAG:
                    pe.wait_ge(chunk_split.sem, chunks.index((1, u - LAG)) + 1)
                    down(0, u - LAG, True)
            turn("peeled", 1)
            pe.wait_ge(chunk_split.sem, len(chunks))
            for u in range(NP - LAG, NP):
                down(0, u, True)
            with pe.Fori(1, B - 1) as i:
                network("steady", i, True)
            network("last", B - 1, False)

        @block.scalar
        def _(act):
            def high(c):
                n = chunks.index(c)
                act.wait_ge(chunk_in[n % SLOTS].sem, 16 * (n // SLOTS + 1))
                nc.scalar.activation(chunk(c, w1[0], w2[0]), staged(c), ACT.Copy).then_inc(chunk_high.sem, 1)

            def turned(sec, b):
                for u in range(2):
                    act.wait_ge(turn_filled.sem, turn_filled.at(b, u + 1))
                    for j in range(2):
                        k = 2 * u + j
                        last = nc.scalar.activation(lnT[:, k, :], banks.bank(sec, ("turn", u))[:, j * S:(j + 1) * S],
                                                    ACT.Identity, bias=shift[:, k:k + 1], scale=gain[:, k:k + 1])
                    last.then_inc(ln_full.sem, 1)

            def gelu(sec, b, weights=False):
                for u in range(NP):
                    if weights:
                        for c in behind[u]:
                            high(c)
                    act.wait_ge(f1_filled.sem, f1_filled.at(b, u + 1))
                    if u >= 2:
                        act.wait_ge(g_split.sem, g_split.at(b, u - 1))
                    for j in range(2):
                        m = 2 * u + j
                        last = nc.scalar.activation(gT[:, u % 2, j * S:(j + 1) * S], banks.bank(sec, ("f1", u))[:, j * S:(j + 1) * S],
                                                    ACT.Gelu_apprx_tanh, bias=b1[:, m:m + 1])
                    last.then_inc(g_full.sem, 1)

            act.wait_ge(consts_in.sem, 16 * 5)
            turned("first", 0)
            gelu("peeled", 0, weights=True)
            for c in behind[NP]:
                high(c)
            turned("peeled", 1)
            with act.Fori(1, B - 1) as i:
                gelu("steady", i)
                turned("steady", i + 1)
            gelu("last", B - 1)

        @block.vector
        def _(dve):
            def normalise(b):
                dve.wait_ge(x_in.sem, x_in.at(b, 1))
                for t_ in range(TT):
                    nc.vector.bn_stats(stats[:, t_, :], xt[:, t_, :])
                nc.vector.drain()
                for t_ in range(TT):
                    nc.vector.bn_aggr(mv[:, t_, :], stats[:, t_, :])
                nc.vector.drain()
                nc.vector.tensor_scalar(vare[:], mv[:, :, 1], EPS, None, ALU.add).then_inc(var_done.sem, 1)

            def apply(b):
                dve.wait_ge(rstd_done.sem, rstd_done.at(b, 1))
                for t_ in range(TT):
                    last = nc.vector.tensor_scalar(xn[:, t_, :], xt[:, t_, :], mv[:, t_, 0:1], rstd[:, t_:t_ + 1],
                                                   ALU.subtract, ALU.mult)
                last.then_inc(xn_done.sem, 1)

            def split(high, low, full, done):
                nc.vector.tensor_copy(high, full)
                nc.vector.drain()
                nc.vector.tensor_tensor(low, full, high.bitcast(F32), ALU.subtract).then_inc(done.sem, 1)

            def ln_parts(b, first=False):
                if not first:
                    dve.wait_ge(f1_filled.sem, f1_filled.at(b - 1, NP))
                for u in range(2):
                    dve.wait_ge(ln_full.sem, ln_full.at(b, u + 1))
                    k = slice(2 * u, 2 * u + 2)
                    split(lnp[0][:, k, :], lnp[1][:, k, :], lnT[:, k, :], ln_split)

            def low(c):
                dve.wait_ge(chunk_high.sem, chunks.index(c) + 1)
                nc.vector.tensor_tensor(chunk(c, w1[1], w2[1]), staged(c), chunk(c, w1[0], w2[0]).bitcast(F32),
                                        ALU.subtract).then_inc(chunk_split.sem, 1)

            def network(b, more, weights=False):
                for u in range(NP):
                    if weights:
                        for c in behind[u]:
                            low(c)
                    dve.wait_ge(g_full.sem, g_full.at(b, u + 1))
                    if u >= RING:
                        dve.wait_ge(g_used.sem, g_used.at(b, u - RING + 1))
                    split(gp[0][:, u % RING, :], gp[1][:, u % RING, :], gT[:, u % 2, :], g_split)
                    if more and u == 1:
                        normalise(b + 1)
                    if more and u == 3:
                        apply(b + 1)

            def add(b):
                dve.wait_ge(xb_done.sem, xb_done.at(b, 1))
                for t_ in range(TT):
                    dve.wait_ge(f2_filled.sem, f2_filled.at(b, t_ + 1))
                    nc.vector.tensor_tensor(res[:, t_, :], sums[:, t_, :], res[:, t_, :], ALU.add).then_inc(res_done.sem, 1)

            dve.wait_ge(consts_in.sem, 16 * 5)
            normalise(0)
            apply(0)
            ln_parts(0, first=True)
            network(0, True, weights=True)
            for c in behind[NP]:
                low(c)
            ln_parts(1)
            add(0)
            with dve.Fori(1, B - 1) as i:
                network(i, True)
                ln_parts(i + 1)
                add(i)
            network(B - 1, False)
            add(B - 1)


_L0 = ["Wq", "Wk", "Wv", "Wo", "ln_q_g", "ln_q_b", "ln_kv_g", "ln_kv_b", "ffn_ln_g", "ffn_ln_b", "W1", "b1", "W2", "b2"]
_L1 = ["ln1_s", "ln1_b", "w_qkv", "b_qkv", "w_ao", "b_ao", "ln2_s", "ln2_b", "w_q", "b_q", "w_kv", "b_kv", "w_co",
       "b_co", "ln3_s", "ln3_b", "w1", "b1", "w2", "b2"]
_IN = ["x", "ctx_2048", "mask_1x1xSxS2_fc1", "mask_Bx1xSxS2_ff1"]


def build(nc, a, out):
    x = a["x"]
    B, C, T = x.shape

    def scratch(name, shape, dt):
        return nc.dram_tensor(name, shape, dt, kind="Internal").ap()

    hid = scratch("hidden", [B, C, T], F32)
    mid = scratch("middle", [B, C, T], F32)
    with ExitStack() as sems:
        first_layer(nc, sems, x, a["ctx_2048"], a["positions"], a["identity"], {n: a["L0_xattn_" + n] for n in _L0}, hid,
                    scratch("a_q", [B, 3, C, T], BF16), scratch("a_k", [B, 3, C, T], BF16),
                    scratch("a_m", [B, 3, HEADS, T], BF16))
        W = {n: a["L1_xattn_" + n] for n in _L1}
        attention_layer(nc, sems, hid, a["ctx_2048"], (a["mask_1x1xSxS2_fc1"], a["mask_Bx1xSxS2_ff1"]), a["identity"],
                        W, mid, [[scratch(f"b_{n}{k}", [B, 2, T, C], F32) for n in "qk"] for k in range(2)])
        network_layer(nc, sems, mid, a["identity"], W, out)


def positions(c, t):
    import math
    import numpy as np
    pos = np.arange(t, dtype=np.float32)[:, None]
    div = np.exp(np.arange(0, c, 2, dtype=np.float32) * np.float32(-math.log(10000.0) / c))
    ang = pos * div
    pe = np.zeros((t, c), np.float32)
    pe[:, 0::2] = np.sin(ang)
    pe[:, 1::2] = np.cos(ang)
    return np.ascontiguousarray(pe.T)


def kernel(**inputs):
    import numpy as _np
    import concourse.bacc as _bacc
    from concourse import mybir as _mybir
    from concourse.bass_utils import run_bass_kernel_spmd as _run

    nc = _bacc.Bacc("TRN2", target_bir_lowering=False, num_devices=1)
    names = _IN + ["L0_xattn_" + n for n in _L0] + ["L1_xattn_" + n for n in _L1]
    given = {n: _np.ascontiguousarray(inputs[n]) for n in names}
    b, c, t = given["x"].shape
    given["positions"] = positions(c, t)
    given["identity"] = _np.eye(P, dtype=_np.float32)
    arrays, args = {}, {}
    for name, v in given.items():
        arrays[f"in_{name}"] = v
        args[name] = nc.dram_tensor(f"in_{name}", v.shape, _mybir.dt.from_np(v.dtype), kind="ExternalInput").ap()
    out = nc.dram_tensor("out_0", (b, c, t), F32, kind="ExternalOutput").ap()
    build(nc, args, out)
    r = _run(nc, [arrays], core_ids=[0])
    return r.results[0]["out_0"]
```
